# Optimizing a Trainium2 kernel written in Bass

```python
import numpy as np
import jax
import jax.numpy as jnp

def _softmax(x, axis=-1):
    return jax.nn.softmax(x, axis=axis)

def _gelu(x):
    return jax.nn.gelu(x, approximate=True)

def _silu(x):
    return jax.nn.silu(x)

def _sigmoid(x):
    return jax.nn.sigmoid(x)

def _layernorm(x, axis=-1, eps=1e-05):
    m = jnp.mean(x, axis=axis, keepdims=True)
    v = jnp.var(x, axis=axis, keepdims=True)
    return (x - m) / jnp.sqrt(v + eps)

def _scatter_add(tgt, idx, src, axis=0):
    return tgt.at[idx].add(src)

def _segment_sum(src, seg, n):
    return jax.ops.segment_sum(src, seg, n)
kernel_name = 'mk_sandwich_d1_jaxref_r4_a4320f'

def setup_inputs(seed: int=0):
    np.random.seed(seed)
    _w = jnp.asarray

    def _L0_attn_setup():
        import jax, jax.numpy as jnp
        import numpy as np
        N_HEAD = 16
        LATENT = 32

        def _rotate_half(x):
            xe = x[..., ::2]
            xo = x[..., 1::2]
            return jnp.stack((-xo, xe), axis=-1).reshape(x.shape)

        def _rope_tables(T, latent_dim, dtype):
            inv_freq = 1.0 / 10000.0 ** (jnp.arange(0, latent_dim, 2, dtype=jnp.float32) / latent_dim)
            t = jnp.arange(T, dtype=jnp.float32)
            freqs = jnp.outer(t, inv_freq)
            cos = jnp.repeat(jnp.cos(freqs), 2, axis=-1)[:, :latent_dim]
            sin = jnp.repeat(jnp.sin(freqs), 2, axis=-1)[:, :latent_dim]
            return (cos.astype(dtype), sin.astype(dtype))
        key = jax.random.key(seed)
        ks = jax.random.split(key, 14)
        C = 256
        hd = C // N_HEAD
        L = LATENT
        s = 0.02
        return {'x': jax.random.normal(ks[0], (4, 512, C), jnp.float32), 'c_attn_w': jax.random.normal(ks[1], (3 * C, C), jnp.float32) * s, 'c_attn_b': jnp.zeros((3 * C,), jnp.float32), 'q2l_w': jax.random.normal(ks[2], (L, hd), jnp.float32) * s, 'q2l_b': jnp.zeros((L,), jnp.float32), 'kv2l_w': jax.random.normal(ks[3], (L, hd), jnp.float32) * s, 'kv2l_b': jnp.zeros((L,), jnp.float32), 'l2o_w': jax.random.normal(ks[4], (hd, L), jnp.float32) * s, 'l2o_b': jnp.zeros((hd,), jnp.float32), 'wqk_w': jax.random.normal(ks[5], (L, L), jnp.float32) * s, 'wqk_b': jnp.zeros((L,), jnp.float32), 'cproj_w': jax.random.normal(ks[6], (C, C), jnp.float32) * s, 'cproj_b': jnp.zeros((C,), jnp.float32)}
    _L0_attn_in = _L0_attn_setup()

    def _L0_ffn_setup():
        import jax, jax.numpy as jnp
        import numpy as np
        B, S, D, H, E, K, F = (1, 256, 256, 16, 8, 2, 1024)

        def layernorm(x, g, b, eps=1e-05):
            m = x.mean(-1, keepdims=True)
            v = ((x - m) ** 2).mean(-1, keepdims=True)
            return (x - m) * jax.lax.rsqrt(v + eps) * g + b
        key = jax.random.key(seed)
        ks = jax.random.split(key, 8)
        n = lambda k, shape, sc: jax.random.normal(k, shape, dtype=jnp.float32) * sc
        return {'x': n(ks[0], (B, S, D), 1.0), 'w_qkv': n(ks[1], (D, 3 * D), D ** (-0.5)), 'w_o': n(ks[2], (D, D), D ** (-0.5)), 'g1': jnp.ones((D,), jnp.float32), 'b1': jnp.zeros((D,), jnp.float32), 'wg': n(ks[3], (D, E), D ** (-0.5)), 'w1': n(ks[4], (E, D, F), D ** (-0.5)), 'bb1': jnp.zeros((E, F), jnp.float32), 'w2': n(ks[5], (E, F, D), F ** (-0.5)), 'bb2': jnp.zeros((E, D), jnp.float32), 'g2': jnp.ones((D,), jnp.float32), 'b2': jnp.zeros((D,), jnp.float32)}
    _L0_ffn_in = _L0_ffn_setup()
    _d = {'L0_attn_x': _L0_attn_in['x'], 'L0_attn_c_attn_w': _L0_attn_in['c_attn_w'], 'L0_attn_c_attn_b': _L0_attn_in['c_attn_b'], 'L0_attn_q2l_w': _L0_attn_in['q2l_w'], 'L0_attn_q2l_b': _L0_attn_in['q2l_b'], 'L0_attn_kv2l_w': _L0_attn_in['kv2l_w'], 'L0_attn_kv2l_b': _L0_attn_in['kv2l_b'], 'L0_attn_l2o_w': _L0_attn_in['l2o_w'], 'L0_attn_l2o_b': _L0_attn_in['l2o_b'], 'L0_attn_wqk_w': _L0_attn_in['wqk_w'], 'L0_attn_wqk_b': _L0_attn_in['wqk_b'], 'L0_attn_cproj_w': _L0_attn_in['cproj_w'], 'L0_attn_cproj_b': _L0_attn_in['cproj_b'], 'L0_ffn_w_qkv': _L0_ffn_in['w_qkv'], 'L0_ffn_w_o': _L0_ffn_in['w_o'], 'L0_ffn_g1': _L0_ffn_in['g1'], 'L0_ffn_b1': _L0_ffn_in['b1'], 'L0_ffn_wg': _L0_ffn_in['wg'], 'L0_ffn_w1': _L0_ffn_in['w1'], 'L0_ffn_bb1': _L0_ffn_in['bb1'], 'L0_ffn_w2': _L0_ffn_in['w2'], 'L0_ffn_bb2': _L0_ffn_in['bb2'], 'L0_ffn_g2': _L0_ffn_in['g2'], 'L0_ffn_b2': _L0_ffn_in['b2']}
    _x0 = _d['L0_attn_x']
    _d['L0_attn_x'] = jax.random.normal(jax.random.fold_in(jax.random.key(seed), 1), (4, 1024, 256), dtype=_x0.dtype)
    del _x0
    return _d

def reference(L0_attn_x, L0_attn_c_attn_w, L0_attn_c_attn_b, L0_attn_q2l_w, L0_attn_q2l_b, L0_attn_kv2l_w, L0_attn_kv2l_b, L0_attn_l2o_w, L0_attn_l2o_b, L0_attn_wqk_w, L0_attn_wqk_b, L0_attn_cproj_w, L0_attn_cproj_b, L0_ffn_w_qkv, L0_ffn_w_o, L0_ffn_g1, L0_ffn_b1, L0_ffn_wg, L0_ffn_w1, L0_ffn_bb1, L0_ffn_w2, L0_ffn_bb2, L0_ffn_g2, L0_ffn_b2):

    def _L0_attn_ref(x, c_attn_w, c_attn_b, q2l_w, q2l_b, kv2l_w, kv2l_b, l2o_w, l2o_b, wqk_w, wqk_b, cproj_w, cproj_b):
        import jax, jax.numpy as jnp
        import numpy as np
        N_HEAD = 16
        LATENT = 32

        def _rotate_half(x):
            xe = x[..., ::2]
            xo = x[..., 1::2]
            return jnp.stack((-xo, xe), axis=-1).reshape(x.shape)

        def _rope_tables(T, latent_dim, dtype):
            inv_freq = 1.0 / 10000.0 ** (jnp.arange(0, latent_dim, 2, dtype=jnp.float32) / latent_dim)
            t = jnp.arange(T, dtype=jnp.float32)
            freqs = jnp.outer(t, inv_freq)
            cos = jnp.repeat(jnp.cos(freqs), 2, axis=-1)[:, :latent_dim]
            sin = jnp.repeat(jnp.sin(freqs), 2, axis=-1)[:, :latent_dim]
            return (cos.astype(dtype), sin.astype(dtype))
        B, T, C = x.shape
        H = N_HEAD
        hd = C // H
        L = q2l_w.shape[0]
        qkv = x @ c_attn_w.T + c_attn_b
        q, k, v = jnp.split(qkv, 3, axis=2)

        def heads(t):
            return t.reshape(B, T, H, hd).transpose(0, 2, 1, 3)
        q, k, v = (heads(q), heads(k), heads(v))
        q_lat = q @ q2l_w.T + q2l_b
        k_lat = k @ kv2l_w.T + kv2l_b
        v_lat = v @ kv2l_w.T + kv2l_b
        cos, sin = _rope_tables(T, L, x.dtype)
        cos = cos[None, None]
        sin = sin[None, None]
        q_lat = q_lat * cos + _rotate_half(q_lat) * sin
        k_lat = k_lat * cos + _rotate_half(k_lat) * sin
        q_for_k = q_lat @ wqk_w.T + wqk_b
        att = jnp.einsum('bhql,bhkl->bhqk', q_for_k, k_lat) * L ** (-0.5)
        causal = jnp.tril(jnp.ones((T, T), dtype=bool))
        att = jnp.where(causal[None, None], att, -jnp.inf)
        att = jax.nn.softmax(att, axis=-1)
        y_lat = jnp.einsum('bhqk,bhkl->bhql', att, v_lat)
        y = y_lat @ l2o_w.T + l2o_b
        y = y.transpose(0, 2, 1, 3).reshape(B, T, C)
        return y @ cproj_w.T + cproj_b

    def _L0_ffn_ref(x, w_qkv, w_o, g1, b1, wg, w1, bb1, w2, bb2, g2, b2):
        import jax, jax.numpy as jnp
        import numpy as np
        B, S, D, H, E, K, F = (1, 256, 256, 16, 8, 2, 1024)

        def layernorm(x, g, b, eps=1e-05):
            m = x.mean(-1, keepdims=True)
            v = ((x - m) ** 2).mean(-1, keepdims=True)
            return (x - m) * jax.lax.rsqrt(v + eps) * g + b
        b, s, d = x.shape
        hd = d // H
        qkv = x @ w_qkv
        q, k, v = jnp.split(qkv, 3, axis=-1)
        to_heads = lambda t: t.reshape(b, s, H, hd).transpose(0, 2, 1, 3)
        q, k, v = (to_heads(q), to_heads(k), to_heads(v))
        scores = jnp.einsum('bhqd,bhkd->bhqk', q, k) / jnp.sqrt(jnp.float32(hd))
        causal = jnp.tril(jnp.ones((s, s), bool))
        scores = jnp.where(causal, scores, jnp.finfo(scores.dtype).min)
        attn = jax.nn.softmax(scores, axis=-1)
        o = jnp.einsum('bhqk,bhkd->bhqd', attn, v)
        o = o.transpose(0, 2, 1, 3).reshape(b, s, d) @ w_o
        h = layernorm(x + o, g1, b1)
        probs = jax.nn.softmax(h @ wg, axis=-1)
        topv, topi = jax.lax.top_k(probs, K)
        topv = topv / topv.sum(-1, keepdims=True)
        w = (topv[..., None] * jax.nn.one_hot(topi, E, dtype=h.dtype)).sum(-2)
        h1 = jax.nn.gelu(jnp.einsum('bsd,edf->ebsf', h, w1) + bb1[:, None, None, :])
        y = jnp.einsum('ebsf,efd->ebsd', h1, w2) + bb2[:, None, None, :]
        moe = jnp.einsum('ebsd,bse->bsd', y, w)
        return layernorm(h + moe, g2, b2)
    x = L0_attn_x
    x = x + _layernorm(_L0_attn_ref(_layernorm(x, axis=-1), L0_attn_c_attn_w, L0_attn_c_attn_b, L0_attn_q2l_w, L0_attn_q2l_b, L0_attn_kv2l_w, L0_attn_kv2l_b, L0_attn_l2o_w, L0_attn_l2o_b, L0_attn_wqk_w, L0_attn_wqk_b, L0_attn_cproj_w, L0_attn_cproj_b), axis=-1)
    x = x + _layernorm(_L0_ffn_ref(_layernorm(x, axis=-1), L0_ffn_w_qkv, L0_ffn_w_o, L0_ffn_g1, L0_ffn_b1, L0_ffn_wg, L0_ffn_w1, L0_ffn_bb1, L0_ffn_w2, L0_ffn_bb2, L0_ffn_g2, L0_ffn_b2), axis=-1)
    return x

_drawn_inputs = setup_inputs


def setup_inputs(seed=0):
    import zlib

    import numpy as np

    out = dict(_drawn_inputs(seed))
    spreads = {'L0_attn_c_attn_b': (0.0, 0.8),
     'L0_attn_q2l_b': (0.0, 0.8),
     'L0_attn_kv2l_b': (0.0, 0.1),
     'L0_attn_l2o_b': (0.0, 0.1),
     'L0_attn_wqk_b': (0.0, 0.8),
     'L0_attn_cproj_b': (0.0, 0.1),
     'L0_ffn_g1': (1.0, 0.2),
     'L0_ffn_b1': (0.0, 0.1),
     'L0_ffn_bb1': (0.0, 0.397),
     'L0_ffn_bb2': (0.0, 0.281),
     'L0_ffn_g2': (1.0, 0.2),
     'L0_ffn_b2': (0.0, 0.1)}
    factors = {'L0_attn_c_attn_w': 8.0,
     'L0_attn_q2l_w': 8.0,
     'L0_attn_kv2l_w': 7.123,
     'L0_attn_wqk_w': 8.0}
    for name, (base, spread) in spreads.items():
        noise = np.random.default_rng([zlib.crc32(name.encode()), seed]).standard_normal(out[name].shape)
        drawn = base * np.exp(spread * noise) if base else spread * noise
        out[name] = jnp.asarray(drawn.astype(out[name].dtype))
    for name, factor in factors.items():
        out[name] = (out[name] * factor).astype(out[name].dtype)
    return out
```

```python
from contextlib import ExitStack

import concourse.bass as bass
from concourse import mybir
import numpy as np

F32 = mybir.dt.float32
F32R = mybir.dt.float32r
BF16 = mybir.dt.bfloat16
FP16 = mybir.dt.float16
U32 = mybir.dt.uint32
ALU = mybir.AluOpType
ACT = mybir.ActivationFunctionType
AX = mybir.AxisListType

P = 128
B, T, C = 4, 1024, 256
H, HD, L = 16, 16, 32
NH = B * H
E, F = 8, 1024
CC = C // P
CH = 512
NT = CH // P
KB = T // P
TT = B * T // P
TILES = 2 * TT + E
EPS = 1e-5
MASKED = -1e30

PACKS = {
    "latent": dict(
        wq_rows=2 * C,
        wk_rows=2 * C,
        bq=2, bk=2,
        q2l_blocks=2 * P,
        kv2l_blocks=2 * P,
        q2l_bias=2, kv2l_bias=2,
        wqk_blocks=4 * P,
        wqk_bias=2,
        wv=CC * C,
        bv=C,
        l2o_blocks=4 * P,
        kvl_blocks=4 * P,
        cproj=2 * C,
        l2o_bias=P,
        kvl_bias=P,
        cproj_bias=C,
    ),
    "block": dict(
        ident=P,
        eps=1,
        wqkv2=CC * 3 * C,
        wo2=CC * C,
        g1=C, b1=C, g2=C, b2=C,
        wg=CC * E,
        before=P,
        ones=P,
        expert=E,
        tile=TILES,
    ),
}
PLACE = {name: (pack, sum(list(widths.values())[:k]), width)
         for pack, widths in PACKS.items() for k, (name, width) in enumerate(widths.items())}
WIDTH = {pack: sum(widths.values()) for pack, widths in PACKS.items()}


def pack(which, named):
    out = np.zeros((P, WIDTH[which]), np.float32)
    for name, a in named.items():
        _, at, width = PLACE[name]
        out[: a.shape[0], at:at + width] = a.reshape(a.shape[0], -1)
    return out


def const(cst, name):
    which, at, width = PLACE[name]
    return cst[which][:, at:at + width]


def attention_constants(i):
    w, bias = i["L0_attn_c_attn_w"], i["L0_attn_c_attn_b"]
    q2l, kv2l, wqk, l2o = (i["L0_attn_" + n] for n in ("q2l_w", "kv2l_w", "wqk_w", "l2o_w"))
    rows = lambda a: a.reshape(2, P, C).transpose(1, 0, 2)
    halves = lambda a: a.reshape(2, P).T

    def blocks(m):
        r, c = m.shape
        out = np.zeros((8, r, 8, c), np.float32)
        for h in range(8):
            out[h, :, h, :] = m
        return out.reshape(8 * r, 8 * c)

    wqk_blocks = np.stack([blocks(wqk[po::2, pi::2].T) for po in range(2) for pi in range(2)], 1)
    l2o_blocks = np.zeros((8, HD, 4, 4, L), np.float32)
    kvl_blocks = np.zeros((4, L, 4, 8, HD), np.float32)
    for hg in range(4):
        for h in range(4):
            l2o_blocks[(hg % 2) * 4 + h, :, hg, h, :] = l2o
            kvl_blocks[h, :, hg, (hg % 2) * 4 + h, :] = kv2l
    tiled = lambda v: np.tile(v, 8)[:, None]
    return {
        "wq_rows": rows(w[:C]), "wk_rows": rows(w[C:2 * C]),
        "bq": halves(bias[:C]), "bk": halves(bias[C:2 * C]),
        "q2l_blocks": np.stack([blocks(q2l[p::2].T) for p in range(2)], 1),
        "kv2l_blocks": np.stack([blocks(kv2l[p::2].T) for p in range(2)], 1),
        "q2l_bias": np.concatenate([tiled(i["L0_attn_q2l_b"][p::2]) for p in range(2)], 1),
        "kv2l_bias": np.concatenate([tiled(i["L0_attn_kv2l_b"][p::2]) for p in range(2)], 1),
        "wqk_blocks": wqk_blocks,
        "wqk_bias": np.concatenate([tiled(i["L0_attn_wqk_b"][p::2]) for p in range(2)], 1),
        "wv": w[2 * C:].T.reshape(CC, P, C).transpose(1, 0, 2),
        "bv": np.tile(bias[2 * C:], (P, 1)),
        "l2o_blocks": l2o_blocks.reshape(P, 4 * P), "kvl_blocks": kvl_blocks.reshape(P, 4 * P),
        "cproj": i["L0_attn_cproj_w"].T.reshape(2, P, C).transpose(1, 0, 2),
        "l2o_bias": np.tile(np.tile(i["L0_attn_l2o_b"], 8)[:, None], (1, P)),
        "kvl_bias": np.tile(np.tile(i["L0_attn_kv2l_b"], 4)[:, None], (1, P)),
        "cproj_bias": np.tile(i["L0_attn_cproj_b"], (P, 1)),
    }


def block_constants(i):
    chunks = lambda a: a.reshape(CC, P, -1).transpose(1, 0, 2)
    f = lambda n: i["L0_ffn_" + n]
    out = {
        "wqkv2": chunks(f("w_qkv")), "wo2": chunks(f("w_o")), "wg": chunks(f("wg")),
        "ident": np.eye(P, dtype=np.float32), "eps": np.full((P, 1), EPS, np.float32),
        "before": np.triu(np.ones((P, P), np.float32), 1), "ones": np.ones((P, P), np.float32),
        "expert": np.tile(np.arange(E, dtype=np.float32), (P, 1)), "tile": np.tile(np.arange(TILES, dtype=np.float32), (P, 1)),
    }
    return out | {n: np.tile(f(n), (P, 1)) for n in ("g1", "b1", "g2", "b2")}


def rope_tables():
    inv = (1.0 / 10000.0 ** (np.arange(0, L, 2, dtype=np.float32) / np.float32(L))).astype(np.float32)
    angle = np.tile(inv, 8)[:, None] * np.arange(T, dtype=np.float32)[None, :]
    return np.stack([np.cos(angle), np.sin(angle)], 1).astype(np.float32)


def over_chunks(eng, chunk):
    for half in range(2):
        chunk(0, half, half == 0)
    with eng.Fori(1, B) as b:
        for half in range(2):
            chunk(b, half, False)


class Tools:

    def __init__(self, nc, ctx, sems):
        self.nc, self.ctx, self.sems = nc, ctx, sems

    def sbuf(self, name, shape, dt=F32):
        return self.ctx.enter_context(self.nc.sbuf_tensor(name, shape, dt))

    def psum(self, name, shape, dt=F32):
        return self.ctx.enter_context(self.nc.psum_tensor(name, shape, dt))

    def sem(self, name):
        self.sems.append(self.nc.alloc_semaphore(name))
        return self.sems[-1]


def renew_semaphores(nc, sems):
    nc.clear_and_free_semaphores(sems)
    sems.clear()
    nc.all_engine_barrier()


def compose_weights(nc, t, packed, cst, rope_dram, rope, wlat, blat, wout, cout):
    ps = [t.psum(f"cw_ps{n}", [P, 512]) for n in range(2)]
    t1 = t.sbuf("cw_t1", [P, 4, C])
    loaded, made, moved = t.sem("cw_loaded"), t.sem("cw_made"), t.sem("cw_moved")

    c = lambda name: const(cst, name)
    rows = [c("wq_rows").rearrange("p (g c) -> p g c", g=2), c("wk_rows").rearrange("p (g c) -> p g c", g=2)]
    to_latent = [c("q2l_blocks").rearrange("p (e m) -> p e m", e=2), c("kv2l_blocks").rearrange("p (e m) -> p e m", e=2)]
    l2o = c("l2o_blocks").rearrange("p (g m) -> p g m", g=4)
    kvl = c("kvl_blocks").rearrange("p (g m) -> p g m", g=4)
    cproj = c("cproj").rearrange("p (g n) -> p g n", g=2)
    with nc.Block() as block:
        @block.sync
        def _(sp):
            for which in PACKS:
                sp.dma_start(cst[which][:, :], packed[which]).then_inc(loaded, 16)
            sp.dma_start(rope[:, :, :], rope_dram).then_inc(loaded, 16)

        @block.tensor
        def _(pe):
            pe.wait_ge(loaded, 48)
            step = 0
            for w in range(2):
                for g in range(2):
                    if step >= 2:
                        pe.wait_ge(moved, step - 1)
                    for cc in range(CC):
                        last = nc.tensor.matmul(ps[step % 2][:, cc * C:(cc + 1) * C], rows[w][:, g, cc * P:(cc + 1) * P],
                                                to_latent[w].rearrange("p e m -> p (e m)"), start=True, stop=True)
                    last.then_inc(made, 1)
                    step += 1
            pe.wait_ge(moved, step - 1)
            for w, b in enumerate(("bq", "bk")):
                for e in range(2):
                    last = nc.tensor.matmul(ps[0][:, (w * 2 + e) * 2:(w * 2 + e) * 2 + 2], to_latent[w][:, e, :], c(b),
                                            start=True, stop=True)
            last.then_inc(made, 1)
            step += 1
            for hg in range(4):
                pe.wait_ge(moved, step - 1)
                nc.tensor.matmul(ps[step % 2][:, 0:C], l2o[:, hg, :], cproj[:, hg // 2, :], start=True, stop=True).then_inc(made, 1)
                step += 1
            pe.wait_ge(moved, step)
            for g in range(2):
                for k in range(2):
                    last = nc.tensor.matmul(ps[g][:, 0:C], kvl[:, 2 * g + k, :], t1[:, 2 * g + k, :], start=(k == 0), stop=(k == 1))
                last.then_inc(made, 1)
                step += 1
            pe.wait_ge(moved, step - 1)
            for g in range(2):
                nc.tensor.matmul(ps[0][:, 0:C], c("l2o_bias"), cproj[:, g, :], start=(g == 0), stop=False)
            for hg in range(4):
                last = nc.tensor.matmul(ps[0][:, 0:C], c("kvl_bias"), t1[:, hg, :], start=False, stop=(hg == 3))
            last.then_inc(made, 1)

        @block.vector
        def _(dve):
            step = 0
            for w in range(2):
                for g in range(2):
                    dve.wait_ge(made, step + 1)
                    nc.vector.tensor_copy(wlat[:, :, w, :, g, :],
                                          ps[step % 2][:, :].rearrange("p (c e m) -> p c e m", c=CC, e=2)).then_inc(moved, 1)
                    step += 1
            dve.wait_ge(made, step + 1)
            for w, b in enumerate(("q2l_bias", "kv2l_bias")):
                for e in range(2):
                    last = nc.vector.tensor_scalar(blat[:, w, e, :], ps[0][:, (w * 2 + e) * 2:(w * 2 + e) * 2 + 2],
                                                   c(b)[:, e:e + 1], None, ALU.add)
            last.then_inc(moved, 1)
            step += 1
            for hg in range(4):
                dve.wait_ge(made, step + 1)
                nc.vector.tensor_copy(t1[:, hg, :], ps[step % 2][:, 0:C]).then_inc(moved, 1)
                step += 1
            for g in range(2):
                dve.wait_ge(made, step + 1)
                nc.vector.tensor_copy(wout[:, g, :], ps[g][:, 0:C]).then_inc(moved, 1)
                step += 1
            dve.wait_ge(made, step + 1)
            nc.vector.tensor_tensor(cout[:, :], ps[0][:, 0:C], c("cproj_bias"), ALU.add).then_inc(moved, 1)


def latent_projections(nc, t, x, cst, rope, wlat, blat, qk, vs):
    ps_t = [t.psum(f"lp_t{n}", [P, CH]) for n in range(2)]
    ps_pair = [[t.psum(f"lp_pair{n}{e}", [P, CH]) for e in range(2)] for n in range(2)]
    ps_q = [t.psum(f"lp_q{e}", [P, CH]) for e in range(2)]
    xc = t.sbuf("lp_x", [P, 2, NT, C])
    xn = t.sbuf("lp_xn", [P, NT, C])
    xT = t.sbuf("lp_xT", [P, CC, CH])
    stats = t.sbuf("lp_stats", [P, NT, 6])
    mv = t.sbuf("lp_mv", [P, NT, 2])
    std = t.sbuf("lp_std", [P, NT])
    rstd = t.sbuf("lp_rstd", [P, NT])
    prod = t.sbuf("lp_prod", [P, 4, CH])
    rot = t.sbuf("lp_rot", [P, 2, 2, CH])
    out = t.sbuf("lp_out", [P, 4, 2, 2, CH], F32R)
    vt = t.sbuf("lp_v", [P, NT, H, 2 * HD])
    x_in = [t.sem(f"lp_x_in{n}") for n in range(2)]
    stats_done, var_ready, std_ready, rstd_ready = (t.sem("lp_" + n) for n in ("stats_done", "var_ready", "std_ready", "rstd_ready"))
    xn_ready, turned, xT_ready = (t.sem("lp_" + n) for n in ("xn_ready", "turned", "xT_ready"))
    pair_ready, products, rot_ready, q_ready = (t.sem("lp_" + n) for n in ("pair_ready", "products", "rot_ready", "q_ready"))
    hi_ready, lo_ready, v_ready, v_used, zeroed = (t.sem("lp_" + n) for n in ("hi_ready", "lo_ready", "v_ready", "v_used", "zeroed"))
    out_left = [t.sem(f"lp_out_left{r}") for r in range(4)]
    v_left = t.sem("lp_v_left")
    wqk = const(cst, "wqk_blocks").rearrange("p (o i m) -> p o i m", o=2, i=2)
    ident, wqk_bias, eps = const(cst, "ident"), const(cst, "wqk_bias"), const(cst, "eps")
    wv = const(cst, "wv").rearrange("p (c n) -> p c n", c=CC)
    bv = const(cst, "bv").rearrange("p (h d) -> p h d", h=H)
    xt = x.rearrange("b (s j p) c -> (b s) p j c", s=2, p=P)
    chunks = 2 * B

    with nc.Block() as block:
        @block.sync
        def _(sp):
            for half in range(2):
                sp.dma_start(xc[:, half], xt[half]).then_inc(x_in[half], 16)

            def chunk(b, half, more):
                ck = 2 * b + half
                if more:
                    sp.wait_ge(xn_ready, NT * (ck + 1))
                    sp.dma_start(xc[:, half], xt[bass.ds(ck + 2, 1)].rearrange("a p j c -> p (a j) c")).then_inc(x_in[half], 16)
                for r in range(4):
                    w, g = r // 2, r % 2
                    sp.wait_ge(lo_ready, 2 * (4 * ck + r + 1))
                    for hl in range(2):
                        for e in range(2):
                            dst = qk[w][hl][bass.ds(b * H + g * 8, 8), e * HD:(e + 1) * HD, half * CH:(half + 1) * CH]
                            sp.dma_start(dst, out[:, r, hl, e, :].bitcast(F32)).then_inc(out_left[r], 16)
                sp.wait_ge(v_used, NT * (ck + 1))
                for j in range(NT):
                    kb = half * NT + j
                    dst = vs[bass.ds(b * H, H), :, kb * 2 * HD:(kb + 1) * 2 * HD].rearrange("h p e -> p h e")
                    sp.dma_start(dst, vt[:, j]).then_inc(v_left, 16)

            with sp.Fori(0, B - 1) as b:
                for half in range(2):
                    chunk(b, half, True)
            for half in range(2):
                chunk(B - 1, half, False)
            for r in range(4):
                sp.wait_ge(out_left[r], 16 * 4 * chunks)
            sp.wait_ge(v_left, 16 * NT * chunks)

        @block.vector
        def _(dve):
            nc.vector.memset(vt[:, :, :, HD + 1:], 0.0).then_inc(zeroed, 1)
            nc.vector.memset(vt[:, :, :, HD:HD + 1], 1.0).then_inc(zeroed, 1)

            def chunk(b, half, first):
                ck = 2 * b + half
                dve.wait_ge(x_in[half], 16 * b + 16)
                for j in range(NT):
                    nc.vector.bn_stats(stats[:, j], xc[:, half, j, :]).then_inc(stats_done, 1)
                dve.wait_ge(stats_done, NT * (ck + 1))
                nc.vector.memset(std[:, :], 0.0)
                for j in range(NT):
                    nc.vector.bn_aggr(mv[:, j], stats[:, j]).then_inc(var_ready, 1)
                dve.wait_ge(std_ready, ck + 1)
                nc.vector.reciprocal(rstd[:, :], std[:, :]).then_inc(rstd_ready, 1)
                dve.wait_ge(rstd_ready, ck + 1)
                if not first:
                    dve.wait_ge(turned, CC * ck)
                for j in range(NT):
                    nc.vector.tensor_scalar(xn[:, j], xc[:, half, j, :], mv[:, j, 0:1], rstd[:, j:j + 1],
                                            ALU.subtract, ALU.mult).then_inc(xn_ready, 1)
                for r in range(4):
                    w, g, n = r // 2, r % 2, 4 * ck + r
                    dve.wait_ge(pair_ready, n + 1)
                    cos, sin = (rope[:, k, half * CH:(half + 1) * CH] for k in range(2))
                    for k, (e, table) in enumerate(((0, cos), (1, sin), (1, cos), (0, sin))):
                        nc.vector.scalar_tensor_tensor(out=prod[:, k], in0=ps_pair[r % 2][e][:, :], scalar=blat[:, w, e, g:g + 1],
                                                       in1=table, op0=ALU.add, op1=ALU.mult).then_inc(products, 1)
                    dve.wait_ge(products, 4 * (n + 1))
                    nc.vector.tensor_tensor(rot[:, r % 2, 0], prod[:, 0], prod[:, 1], ALU.subtract).then_inc(rot_ready, 1)
                    nc.vector.tensor_tensor(rot[:, r % 2, 1], prod[:, 2], prod[:, 3], ALU.add).then_inc(rot_ready, 1)
                    dve.wait_ge(hi_ready, 2 * (n + 1))
                    dve.wait_ge(rot_ready, 2 * (n + 1))
                    for e in range(2):
                        hi, lo = out[:, r, 0, e, :].bitcast(F32), out[:, r, 1, e, :]
                        if w == 0:
                            nc.vector.scalar_tensor_tensor(out=lo, in0=ps_q[e][:, :], scalar=wqk_bias[:, e:e + 1], in1=hi,
                                                           op0=ALU.add, op1=ALU.subtract).then_inc(lo_ready, 1)
                        else:
                            nc.vector.tensor_tensor(lo, rot[:, r % 2, e], hi, ALU.subtract).then_inc(lo_ready, 1)
                if first:
                    dve.wait_ge(zeroed, 2)
                else:
                    dve.wait_ge(v_left, 16 * NT * ck)
                for j in range(NT):
                    dve.wait_ge(v_ready, 2 * ck + j // 2 + 1)
                    nc.vector.tensor_tensor(vt[:, j, :, 0:HD], ps_t[j // 2][:, (j % 2) * C:(j % 2 + 1) * C].rearrange("p (h d) -> p h d", h=H),
                                            bv, ALU.add).then_inc(v_used, 1)

            over_chunks(dve, chunk)

        @block.scalar
        def _(act):
            def chunk(b, half, first):
                ck = 2 * b + half
                act.wait_ge(var_ready, NT * (ck + 1))
                nc.scalar.activation(std[:, :], mv[:, :, 1], ACT.Sqrt, bias=eps).then_inc(std_ready, 1)
                if not first:
                    act.wait_ge(v_ready, 2 * ck)
                for cc in range(CC):
                    act.wait_ge(turned, CC * ck + cc + 1)
                    nc.scalar.copy(xT[:, cc, :], ps_t[cc][:, :]).then_inc(xT_ready, 1)
                for r in range(4):
                    w, n = r // 2, 4 * ck + r
                    if w == 0:
                        act.wait_ge(q_ready, 2 * ck + r + 1)
                    else:
                        act.wait_ge(rot_ready, 2 * (n + 1))
                    if not first:
                        act.wait_ge(out_left[r], 64 * ck)
                    for e in range(2):
                        if w == 0:
                            ins = nc.scalar.activation(out[:, r, 0, e, :], ps_q[e][:, :], ACT.Identity, bias=wqk_bias[:, e:e + 1])
                        else:
                            ins = nc.scalar.copy(out[:, r, 0, e, :], rot[:, r % 2, e])
                        ins.then_inc(hi_ready, 1)

            over_chunks(act, chunk)

        @block.tensor
        def _(pe):
            def chunk(b, half, first):
                ck = 2 * b + half
                pe.wait_ge(xn_ready, NT * (ck + 1))
                if not first:
                    pe.wait_ge(v_used, NT * ck)
                for cc in range(CC):
                    for j in range(NT):
                        last = nc.tensor.transpose(ps_t[cc][:, j * P:(j + 1) * P], xn[:, j, cc * P:(cc + 1) * P], ident)
                    last.then_inc(turned, 1)
                pe.wait_ge(xT_ready, CC * (ck + 1))

                def pair(r):
                    w, g, n = r // 2, r % 2, 4 * ck + r
                    if not (first and r < 2):
                        pe.wait_ge(products, 4 * (n - 1))
                    for e in range(2):
                        for cc in range(CC):
                            last = nc.tensor.matmul(ps_pair[r % 2][e][:, :], wlat[:, cc, w, e, g, :], xT[:, cc, :],
                                                    start=(cc == 0), stop=(cc == CC - 1))
                    last.then_inc(pair_ready, 1)

                def apply_wqk(r):
                    n = 4 * ck + r
                    pe.wait_ge(rot_ready, 2 * (n + 1))
                    if r == 1:
                        pe.wait_ge(lo_ready, 2 * n)
                    elif not first:
                        pe.wait_ge(lo_ready, 2 * (n - 2))
                    for o in range(2):
                        for e in range(2):
                            last = nc.tensor.matmul(ps_q[o][:, :], wqk[:, o, e, :], rot[:, r % 2, e], start=(e == 0), stop=(e == 1))
                    last.then_inc(q_ready, 1)

                pair(0)
                pair(1)
                apply_wqk(0)
                pair(2)
                apply_wqk(1)
                pair(3)
                for j in range(NT):
                    for cc in range(CC):
                        last = nc.tensor.matmul(ps_t[j // 2][:, (j % 2) * C:(j % 2 + 1) * C], xT[:, cc, j * P:(j + 1) * P], wv[:, cc, :],
                                                start=(cc == 0), stop=(cc == CC - 1))
                    if j % 2:
                        last.then_inc(v_ready, 1)

            over_chunks(pe, chunk)


def between_attentions(nc, t, x, os, cst, wout, cout, x1, n1, qk, vs):
    ps_t = [t.psum(f"mi_t{n}", [P, CH]) for n in range(2)]
    ps_y = [t.psum(f"mi_y{n}", [P, CH]) for n in range(2)]
    ps_p = [t.psum(f"mi_p{n}", [P, CH]) for n in range(4)]
    oc = t.sbuf("mi_o", [P, 2, NT, C])
    xc = t.sbuf("mi_x", [P, 2, NT, C])
    oT = t.sbuf("mi_oT", [P, CC, CH])
    nT = t.sbuf("mi_nT", [P, CC, CH])
    y = t.sbuf("mi_y", [P, NT, C])
    yn = t.sbuf("mi_yn", [P, NT, C])
    x1c = t.sbuf("mi_x1", [P, NT, C])
    n1c = t.sbuf("mi_n1", [P, NT, C])
    stats = t.sbuf("mi_stats", [P, 2, NT, 6])
    mv = t.sbuf("mi_mv", [P, 2, NT, 2])
    std = t.sbuf("mi_std", [P, 2, NT])
    rstd = t.sbuf("mi_rstd", [P, 2, NT])
    out = t.sbuf("mi_out", [P, 4, 2, CH], F32R)
    vt = t.sbuf("mi_v", [P, NT, H, 2 * HD])
    names = ("turned", "oT_ready", "y_ready", "y_used", "nT_ready", "n_turned", "p_ready", "hi_ready", "lo_ready", "v_ready", "v_used",
             "yn_ready", "x1_ready", "n1_ready", "zeroed")
    turned, oT_ready, y_ready, y_used, nT_ready, n_turned, p_ready, hi_ready, lo_ready, v_ready, v_used, yn_ready, x1_ready, \
        n1_ready, zeroed = (t.sem("mi_" + n) for n in names)
    stats_done, var_ready, std_ready, rstd_ready = ([t.sem(f"mi_{n}{k}") for k in range(2)] for n in ("stats", "var", "std", "rstd"))
    o_in, x_in = ([t.sem(f"mi_{n}_in{k}") for k in range(2)] for n in "ox")
    out_left = [t.sem(f"mi_out_left{r}") for r in range(4)]
    v_left, x1_left, n1_left = (t.sem(f"mi_{n}_left") for n in ("v", "x1", "n1"))
    ident, eps = const(cst, "ident"), const(cst, "eps")
    wqkv = const(cst, "wqkv2").rearrange("p (c n) -> p c n", c=CC)
    tiles = lambda a: a.rearrange("b (s j p) c -> (b s) p j c", s=2, p=P)
    xt = tiles(x)
    x1t = tiles(x1)
    n1t = tiles(n1)
    chunks = 2 * B
    HG = H // 4

    with nc.Block() as block:
        @block.sync
        def _(sp):
            def load(b, half):
                for hg in range(HG):
                    sp.dma_start(oc[:, half, :, hg * 4 * HD:(hg + 1) * 4 * HD],
                                 os[bass.ds(2 * (b * HG + hg) + half, 1)].rearrange("a p q d -> p (a q) d")).then_inc(o_in[half], 16)
                sp.dma_start(xc[:, half], xt[bass.ds(2 * b + half, 1)].rearrange("a p j c -> p (a j) c")).then_inc(x_in[half], 16)

            for half in range(2):
                load(0, half)

            def chunk(b, half, more):
                ck = 2 * b + half
                sp.wait_ge(x1_ready, ck + 1)
                if more:
                    load(b + 1, half)
                sp.dma_start(x1t[bass.ds(ck, 1)].rearrange("a p j c -> p (a j) c"), x1c[:, :, :]).then_inc(x1_left, 16)
                sp.wait_ge(n1_ready, NT * (ck + 1))
                sp.dma_start(n1t[bass.ds(ck, 1)].rearrange("a p j c -> p (a j) c"), n1c[:, :, :]).then_inc(n1_left, 16)
                for r in range(4):
                    w, g = r // 2, r % 2
                    sp.wait_ge(lo_ready, 4 * ck + r + 1)
                    for hl in range(2):
                        dst = qk[w][hl][bass.ds(b * H + g * 8, 8), 0:HD, half * CH:(half + 1) * CH]
                        sp.dma_start(dst, out[:, r, hl, :].bitcast(F32)).then_inc(out_left[r], 16)
                sp.wait_ge(v_used, 2 * (ck + 1))
                for j in range(NT):
                    kb = half * NT + j
                    dst = vs[bass.ds(b * H, H), :, kb * 2 * HD:(kb + 1) * 2 * HD].rearrange("h p e -> p h e")
                    sp.dma_start(dst, vt[:, j]).then_inc(v_left, 16)

            with sp.Fori(0, B - 1) as b:
                for half in range(2):
                    chunk(b, half, True)
            for half in range(2):
                chunk(B - 1, half, False)
            for r in range(4):
                sp.wait_ge(out_left[r], 16 * 2 * chunks)
            sp.wait_ge(v_left, 16 * NT * chunks)
            sp.wait_ge(x1_left, 16 * chunks)
            sp.wait_ge(n1_left, 16 * chunks)

        @block.vector
        def _(dve):
            nc.vector.memset(vt[:, :, :, HD + 1:], 0.0).then_inc(zeroed, 1)
            nc.vector.memset(vt[:, :, :, HD:HD + 1], 1.0).then_inc(zeroed, 1)

            def norm(ck, k, src, dst, ready):
                for j in range(NT):
                    nc.vector.bn_stats(stats[:, k, j], src[:, j, :]).then_inc(stats_done[k], 1)
                dve.wait_ge(stats_done[k], NT * (ck + 1))
                nc.vector.memset(std[:, k, :], 0.0)
                for j in range(NT):
                    nc.vector.bn_aggr(mv[:, k, j], stats[:, k, j]).then_inc(var_ready[k], 1)
                dve.wait_ge(std_ready[k], ck + 1)
                nc.vector.reciprocal(rstd[:, k, :], std[:, k, :]).then_inc(rstd_ready[k], 1)
                dve.wait_ge(rstd_ready[k], ck + 1)
                for j in range(NT):
                    nc.vector.tensor_scalar(dst[:, j], src[:, j], mv[:, k, j, 0:1], rstd[:, k, j:j + 1], ALU.subtract, ALU.mult).then_inc(ready, 1)

            def chunk(b, half, first):
                ck = 2 * b + half
                for k in range(2):
                    dve.wait_ge(y_ready, 2 * ck + k + 1)
                    nc.vector.tensor_tensor(y[:, 2 * k:2 * k + 2], ps_y[k][:, :].rearrange("p (j n) -> p j n", j=2),
                                            cout[:, :].unsqueeze(1).to_broadcast([P, 2, C]), ALU.add).then_inc(y_used, 1)
                dve.wait_ge(y_used, 2 * (ck + 1))
                norm(ck, 0, y, yn, yn_ready)
                dve.wait_ge(yn_ready, NT * (ck + 1))
                dve.wait_ge(x_in[half], 16 * (b + 1))
                if not first:
                    dve.wait_ge(x1_left, 16 * ck)
                nc.vector.tensor_tensor(x1c[:, :, :], xc[:, half], yn[:, :, :], ALU.add).then_inc(x1_ready, 1)
                dve.wait_ge(x1_ready, ck + 1)
                if not first:
                    dve.wait_ge(n1_left, 16 * ck)
                norm(ck, 1, x1c, n1c, n1_ready)
                for r in range(4):
                    n = 4 * ck + r
                    dve.wait_ge(hi_ready, n + 1)
                    nc.vector.tensor_tensor(out[:, r, 1, :], ps_p[r][:, :], out[:, r, 0, :].bitcast(F32), ALU.subtract).then_inc(lo_ready, 1)
                if first:
                    dve.wait_ge(zeroed, 2)
                else:
                    dve.wait_ge(v_left, 16 * NT * ck)
                for k in range(2):
                    dve.wait_ge(v_ready, 2 * ck + k + 1)
                    nc.vector.tensor_copy(vt[:, 2 * k:2 * k + 2, :, 0:HD],
                                          ps_y[k][:, :].rearrange("p (j h d) -> p j h d", j=2, h=H)).then_inc(v_used, 1)

            over_chunks(dve, chunk)

        @block.scalar
        def _(act):
            def deviation(ck, k):
                act.wait_ge(var_ready[k], NT * (ck + 1))
                nc.scalar.activation(std[:, k, :], mv[:, k, :, 1], ACT.Sqrt, bias=eps).then_inc(std_ready[k], 1)

            def chunk(b, half, first):
                ck = 2 * b + half
                for cc in range(CC):
                    act.wait_ge(turned, CC * ck + cc + 1)
                    nc.scalar.copy(oT[:, cc, :], ps_t[cc][:, :]).then_inc(oT_ready, 1)
                deviation(ck, 0)
                deviation(ck, 1)
                for cc in range(CC):
                    act.wait_ge(n_turned, CC * ck + cc + 1)
                    nc.scalar.copy(nT[:, cc, :], ps_t[cc][:, :]).then_inc(nT_ready, 1)
                for r in range(4):
                    n = 4 * ck + r
                    act.wait_ge(p_ready, n + 1)
                    if not first:
                        act.wait_ge(out_left[r], 32 * ck)
                    nc.scalar.copy(out[:, r, 0, :], ps_p[r][:, :]).then_inc(hi_ready, 1)

            over_chunks(act, chunk)

        @block.tensor
        def _(pe):
            def turn(src, done):
                for cc in range(CC):
                    for j in range(NT):
                        last = nc.tensor.transpose(ps_t[cc][:, j * P:(j + 1) * P], src[:, j, cc * P:(cc + 1) * P], ident)
                    last.then_inc(done, 1)

            def chunk(b, half, first):
                ck = 2 * b + half
                pe.wait_ge(o_in[half], 16 * HG * (b + 1))
                if not first:
                    pe.wait_ge(nT_ready, CC * ck)
                turn(oc[:, half], turned)
                pe.wait_ge(oT_ready, CC * (ck + 1))
                if not first:
                    pe.wait_ge(v_used, 2 * ck)
                for j in range(NT):
                    for cc in range(CC):
                        last = nc.tensor.matmul(ps_y[j // 2][:, (j % 2) * C:(j % 2 + 1) * C], oT[:, cc, j * P:(j + 1) * P], wout[:, cc, :],
                                                start=(cc == 0), stop=(cc == CC - 1))
                    if j % 2:
                        last.then_inc(y_ready, 1)
                pe.wait_ge(n1_ready, NT * (ck + 1))
                turn(n1c, n_turned)
                pe.wait_ge(nT_ready, CC * (ck + 1))
                for r in range(4):
                    if not first:
                        pe.wait_ge(lo_ready, 4 * (ck - 1) + r + 1)
                    for cc in range(CC):
                        last = nc.tensor.matmul(ps_p[r][:, :], wqkv[:, cc, r * P:(r + 1) * P], nT[:, cc, :], start=(cc == 0), stop=(cc == CC - 1))
                    last.then_inc(p_ready, 1)
                pe.wait_ge(y_used, 2 * (ck + 1))
                for j in range(NT):
                    for cc in range(CC):
                        last = nc.tensor.matmul(ps_y[j // 2][:, (j % 2) * C:(j % 2 + 1) * C], nT[:, cc, j * P:(j + 1) * P], wqkv[:, cc, 2 * C:],
                                                start=(cc == 0), stop=(cc == CC - 1))
                    if j % 2:
                        last.then_inc(v_ready, 1)

            over_chunks(pe, chunk)


def after_attentions(nc, t, n1, os, cst, h, logits):
    ps_t = [t.psum(f"af_t{n}", [P, CH]) for n in range(2)]
    ps_y = [t.psum(f"af_y{n}", [P, CH]) for n in range(2)]
    ps_l = t.psum("af_l", [P, NT, E])
    oc = t.sbuf("af_o", [P, 2, NT, C])
    nc1 = t.sbuf("af_n", [P, 2, NT, C])
    oT = t.sbuf("af_oT", [P, CC, CH])
    hT = t.sbuf("af_hT", [P, CC, CH])
    y = t.sbuf("af_y", [P, NT, C])
    yn = t.sbuf("af_yn", [P, NT, C])
    yg = t.sbuf("af_yg", [P, NT, C])
    hc = t.sbuf("af_h", [P, 2, NT, C])
    stats = t.sbuf("af_stats", [P, NT, 6])
    mv = t.sbuf("af_mv", [P, NT, 2])
    std = t.sbuf("af_std", [P, NT])
    rstd = t.sbuf("af_rstd", [P, NT])
    names = ("turned", "oT_ready", "y_ready", "y_used", "stats_done", "var_ready", "std_ready", "rstd_ready", "yn_ready", "yg_ready",
             "h_ready", "h_turned", "hT_ready", "l_ready", "l_used")
    turned, oT_ready, y_ready, y_used, stats_done, var_ready, std_ready, rstd_ready, yn_ready, yg_ready, h_ready, h_turned, hT_ready, \
        l_ready, l_used = (t.sem("af_" + n) for n in names)
    o_in, n_in, h_left = ([t.sem(f"af_{n}{k}") for k in range(2)] for n in ("o_in", "n_in", "h_left"))
    ident, eps = const(cst, "ident"), const(cst, "eps")
    wo = const(cst, "wo2").rearrange("p (c n) -> p c n", c=CC)
    wg = const(cst, "wg").rearrange("p (c n) -> p c n", c=CC)
    n1t = n1.rearrange("b (s j p) c -> (b s) p j c", s=2, p=P)
    ht = h.rearrange("b (s j p) c -> (b s) p j c", s=2, p=P)
    HG = H // 4
    over_tiles = lambda a: a.unsqueeze(1).to_broadcast([P, NT, C])

    with nc.Block() as block:
        @block.sync
        def _(sp):
            def load(b, half):
                for hg in range(HG):
                    sp.dma_start(oc[:, half, :, hg * 4 * HD:(hg + 1) * 4 * HD],
                                 os[bass.ds(2 * (b * HG + hg) + half, 1)].rearrange("a p q d -> p (a q) d")).then_inc(o_in[half], 16)
                sp.dma_start(nc1[:, half], n1t[bass.ds(2 * b + half, 1)].rearrange("a p j c -> p (a j) c")).then_inc(n_in[half], 16)

            for half in range(2):
                load(0, half)

            def chunk(b, half, more):
                ck = 2 * b + half
                sp.wait_ge(h_ready, ck + 1)
                if more:
                    load(b + 1, half)
                sp.dma_start(ht[bass.ds(ck, 1)].rearrange("a p j c -> p (a j) c"), hc[:, half]).then_inc(h_left[half], 16)

            with sp.Fori(0, B - 1) as b:
                for half in range(2):
                    chunk(b, half, True)
            for half in range(2):
                chunk(B - 1, half, False)
                sp.wait_ge(h_left[half], 16 * B)

        @block.vector
        def _(dve):
            def chunk(b, half, first):
                ck = 2 * b + half
                dve.wait_ge(n_in[half], 16 * (b + 1))
                for k in range(2):
                    dve.wait_ge(y_ready, 2 * ck + k + 1)
                    nc.vector.tensor_tensor(y[:, 2 * k:2 * k + 2], ps_y[k][:, :].rearrange("p (j n) -> p j n", j=2),
                                            nc1[:, half, 2 * k:2 * k + 2], ALU.add).then_inc(y_used, 1)
                dve.wait_ge(y_used, 2 * (ck + 1))
                for j in range(NT):
                    nc.vector.bn_stats(stats[:, j], y[:, j, :]).then_inc(stats_done, 1)
                dve.wait_ge(stats_done, NT * (ck + 1))
                nc.vector.memset(std[:, :], 0.0)
                for j in range(NT):
                    nc.vector.bn_aggr(mv[:, j], stats[:, j]).then_inc(var_ready, 1)
                dve.wait_ge(std_ready, ck + 1)
                nc.vector.reciprocal(rstd[:, :], std[:, :]).then_inc(rstd_ready, 1)
                dve.wait_ge(rstd_ready, ck + 1)
                for j in range(NT):
                    nc.vector.tensor_scalar(yn[:, j], y[:, j], mv[:, j, 0:1], rstd[:, j:j + 1], ALU.subtract, ALU.mult).then_inc(yn_ready, 1)
                dve.wait_ge(yn_ready, NT * (ck + 1))
                nc.vector.tensor_tensor(yg[:, :, :], yn[:, :, :], over_tiles(const(cst, "g1")), ALU.mult).then_inc(yg_ready, 1)
                dve.wait_ge(yg_ready, ck + 1)
                if not isinstance(b, int):
                    dve.wait_ge(h_left[half], 16 * b)
                nc.vector.tensor_tensor(hc[:, half], yg[:, :, :], over_tiles(const(cst, "b1")), ALU.add).then_inc(h_ready, 1)
                dve.wait_ge(l_ready, ck + 1)
                nc.vector.tensor_copy(logits[:, bass.ds(ck * NT, NT), :], ps_l[:, :, :]).then_inc(l_used, 1)

            over_chunks(dve, chunk)

        @block.scalar
        def _(act):
            def chunk(b, half, first):
                ck = 2 * b + half
                for cc in range(CC):
                    act.wait_ge(turned, CC * ck + cc + 1)
                    nc.scalar.copy(oT[:, cc, :], ps_t[cc][:, :]).then_inc(oT_ready, 1)
                act.wait_ge(var_ready, NT * (ck + 1))
                nc.scalar.activation(std[:, :], mv[:, :, 1], ACT.Sqrt, bias=eps).then_inc(std_ready, 1)
                for cc in range(CC):
                    act.wait_ge(h_turned, CC * ck + cc + 1)
                    nc.scalar.copy(hT[:, cc, :], ps_t[cc][:, :]).then_inc(hT_ready, 1)

            over_chunks(act, chunk)

        @block.tensor
        def _(pe):
            def chunk(b, half, first):
                ck = 2 * b + half
                pe.wait_ge(o_in[half], 16 * HG * (b + 1))
                if not first:
                    pe.wait_ge(hT_ready, CC * ck)
                for cc in range(CC):
                    for j in range(NT):
                        last = nc.tensor.transpose(ps_t[cc][:, j * P:(j + 1) * P], oc[:, half, j, cc * P:(cc + 1) * P], ident)
                    last.then_inc(turned, 1)
                pe.wait_ge(oT_ready, CC * (ck + 1))
                if not first:
                    pe.wait_ge(y_used, 2 * ck)
                for j in range(NT):
                    for cc in range(CC):
                        last = nc.tensor.matmul(ps_y[j // 2][:, (j % 2) * C:(j % 2 + 1) * C], oT[:, cc, j * P:(j + 1) * P], wo[:, cc, :],
                                                start=(cc == 0), stop=(cc == CC - 1))
                    if j % 2:
                        last.then_inc(y_ready, 1)
                pe.wait_ge(h_ready, ck + 1)
                for cc in range(CC):
                    for j in range(NT):
                        last = nc.tensor.transpose(ps_t[cc][:, j * P:(j + 1) * P], hc[:, half, j, cc * P:(cc + 1) * P], ident)
                    last.then_inc(h_turned, 1)
                pe.wait_ge(hT_ready, CC * (ck + 1))
                if not first:
                    pe.wait_ge(l_used, ck)
                for j in range(NT):
                    for cc in range(CC):
                        last = nc.tensor.matmul(ps_l[:, j, :], hT[:, cc, j * P:(j + 1) * P], wg[:, cc, :], start=(cc == 0), stop=(cc == CC - 1))
                last.then_inc(l_ready, 1)

            over_chunks(pe, chunk)


def route(nc, t, cst, logits, weight, place, tile_expert, xs):
    ps = t.psum("ro_ps", [P, 2, TT, E])
    top = t.sbuf("ro_top", [P, TT, 8])
    index = t.sbuf("ro_index", [P, TT, 8], U32)
    chosen = t.sbuf("ro_chosen", [P, TT, 2])
    onehot = t.sbuf("ro_onehot", [P, TT, 2, E])
    count = t.sbuf("ro_count", [P, TT, E])
    scan = [t.sbuf(f"ro_scan{n}", [P, TT, E]) for n in range(2)]
    loc = t.sbuf("ro_loc", [P, TT, E])
    rows = t.sbuf("ro_rows", [P, TT, 2, E])
    placef = t.sbuf("ro_placef", [P, TT, 2])
    gap = t.sbuf("ro_gap", [P, TT])
    egap = t.sbuf("ro_egap", [P, TT])
    denom = t.sbuf("ro_denom", [P, TT])
    total = t.sbuf("ro_total", [P, E])
    tiles_i = t.sbuf("ro_tiles_i", [P, E], mybir.dt.int32)
    shifted = t.sbuf("ro_shifted", [P, E], mybir.dt.int32)
    tiles = t.sbuf("ro_tiles", [P, E])
    ends = t.sbuf("ro_ends", [P, E + 1])
    passed = t.sbuf("ro_passed", [P, TILES, E])
    expf = t.sbuf("ro_expf", [P, TILES])
    zeros = t.sbuf("ro_zeros", [P, TILES * C // 8])
    step, gap_ready, egap_ready, counted, ranked, zeroed, filled = (
        t.sem("ro_" + n) for n in ("step", "gap_ready", "egap_ready", "counted", "ranked", "zeroed", "filled"))

    with nc.Block() as block:
        @block.gpsimd
        def _(pool):
            nc.gpsimd.memset(zeros[:, :], 0.0).then_inc(zeroed, 1)

        @block.sync
        def _(sp):
            sp.wait_ge(zeroed, 1)
            for n in range(8):
                sp.dma_start(xs.rearrange("(n p r) c -> n p (r c)", n=8, p=P)[n], zeros[:, :]).then_inc(filled, 16)
            sp.wait_ge(filled, 16 * 8)

        @block.scalar
        def _(act):
            act.wait_ge(gap_ready, 1)
            nc.scalar.activation(egap[:, :], gap[:, :], ACT.Exp).then_inc(egap_ready, 1)

        @block.tensor
        def _(pe):
            pe.wait_ge(counted, 1)
            flat = count[:, :, :].rearrange("p t e -> p (t e)")
            nc.tensor.matmul(ps[:, 0].rearrange("p t e -> p (t e)"), const(cst, "before"), flat, start=True, stop=True)
            nc.tensor.matmul(ps[:, 1].rearrange("p t e -> p (t e)"), const(cst, "ones"), flat, start=True, stop=True).then_inc(ranked, 1)

        @block.vector
        def _(dve):
            done = 0

            def link(ins):
                nonlocal done
                done += 1
                ins.then_inc(step, 1)
                dve.wait_ge(step, done)

            for k in range(TT):
                last = nc.vector.max(top[:, k], logits[:, k])
            link(last)
            for k in range(TT):
                last = nc.vector.max_index(index[:, k], top[:, k], logits[:, k])
            link(last)
            nc.vector.tensor_tensor(gap[:, :], top[:, :, 1], top[:, :, 0], ALU.subtract).then_inc(gap_ready, 1)
            link(nc.vector.tensor_copy(chosen[:, :, :], index[:, :, 0:2]))
            wide = lambda a: a.unsqueeze(3).to_broadcast([P, TT, 2, E])
            experts = const(cst, "expert").unsqueeze(1).to_broadcast([P, TT, E])
            for s in range(2):
                last = nc.vector.tensor_tensor(onehot[:, :, s], chosen[:, :, s].unsqueeze(2).to_broadcast([P, TT, E]), experts, ALU.is_equal)
            link(last)
            nc.vector.tensor_tensor(count[:, :, :], onehot[:, :, 0], onehot[:, :, 1], ALU.add).then_inc(counted, 1)
            dve.wait_ge(egap_ready, 1)
            link(nc.vector.tensor_scalar(denom[:, :], egap[:, :], 1.0, None, ALU.add))
            link(nc.vector.reciprocal(weight[:, :, 0], denom[:, :]))
            link(nc.vector.tensor_tensor(weight[:, :, 1], weight[:, :, 0], egap[:, :], ALU.mult))
            dve.wait_ge(ranked, 1)
            link(nc.vector.tensor_copy(scan[0][:, :, :], ps[:, 1]))
            at, k = 0, 1
            while k < TT:
                nc.vector.tensor_copy(scan[1 - at][:, 0:k], scan[at][:, 0:k])
                link(nc.vector.tensor_tensor(scan[1 - at][:, k:], scan[at][:, k:], scan[at][:, 0:TT - k], ALU.add))
                at, k = 1 - at, 2 * k
            upto = scan[at]
            link(nc.vector.tensor_scalar(total[:, :], upto[:, TT - 1], float(P - 1), None, ALU.add))
            link(nc.vector.tensor_copy(tiles_i[:, :], total[:, :]))
            link(nc.vector.tensor_single_scalar(shifted[:, :], tiles_i[:, :], 7, ALU.logical_shift_right))
            link(nc.vector.tensor_copy(tiles[:, :], shifted[:, :]))
            link(nc.vector.memset(ends[:, 0:1], 0.0))
            for e in range(E):
                link(nc.vector.tensor_tensor(ends[:, e + 1:e + 2], ends[:, e:e + 1], tiles[:, e:e + 1], ALU.add))
            link(nc.vector.tensor_tensor(loc[:, :, :], upto[:, :, :], ps[:, 1], ALU.subtract))
            link(nc.vector.tensor_tensor(loc[:, :, :], loc[:, :, :], ps[:, 0], ALU.add))
            link(nc.vector.scalar_tensor_tensor(out=loc[:, :, :], in0=ends[:, 0:E].unsqueeze(1).to_broadcast([P, TT, E]), scalar=float(P),
                                                in1=loc[:, :, :], op0=ALU.mult, op1=ALU.add))
            for s in range(2):
                last = nc.vector.tensor_tensor(rows[:, :, s], onehot[:, :, s], loc[:, :, :], ALU.mult)
            link(last)
            link(nc.vector.tensor_reduce(placef[:, :, :], rows[:, :, :, :], AX.X, ALU.add))
            link(nc.vector.tensor_copy(place[:, :, :], placef[:, :, :].rearrange("p t s -> p s t")))
            link(nc.vector.tensor_tensor(passed[:, :, :], ends[:, 1:E + 1].unsqueeze(1).to_broadcast([P, TILES, E]),
                                         const(cst, "tile").unsqueeze(2).to_broadcast([P, TILES, E]), ALU.is_le))
            link(nc.vector.tensor_reduce(expf[:, :], passed[:, :, :], AX.X, ALU.add))
            link(nc.vector.tensor_scalar(expf[:, :], expf[:, :], float(E - 1), None, ALU.min))
            link(nc.vector.tensor_copy(tile_expert[:, :], expf[:, :]))


def scatter_rows(nc, t, h, place, xs):
    RINGS = 4
    ht = h.rearrange("b (k p) c -> (b k) p c", p=P)
    rows = [t.sbuf(f"sc_rows{n}", [P, C]) for n in range(RINGS)]
    h_in, scattered = ([t.sem(f"sc_{n}{k}") for k in range(RINGS)] for n in ("h_in", "scattered"))
    with nc.Block() as block:
        @block.sync
        def _(sp):
            for n in range(RINGS):
                sp.dma_start(rows[n][:, :], ht[n]).then_inc(h_in[n], 16)
            with sp.Fori(1, TT // RINGS) as k:
                for n in range(RINGS):
                    sp.wait_ge(scattered[n], 32 * k)
                    sp.dma_start(rows[n][:, :], ht[bass.ds(RINGS * k + n, 1)].rearrange("a p c -> p (a c)")).then_inc(h_in[n], 16)

        @block.gpsimd
        def _(pool):
            for k in range(TT):
                pool.wait_ge(h_in[k % RINGS], 16 * (k // RINGS + 1))
                for s in range(2):
                    nc.gpsimd.indirect_dma_start(xs, bass.IndirectOffsetOnAxis(place[:, s, k:k + 1], 0), rows[k % RINGS][:, :], None).then_inc(
                        scattered[k % RINGS], 16)
            for n in range(RINGS):
                pool.wait_ge(scattered[n], 32 * TT // RINGS)


def split_expert_weights(nc, t, w1, w2, w1s, w2s, bb_dram, bb):
    FC = F // P
    stage = [[t.sbuf(f"sw_{w}{n}", [P, CC * F]) for n in range(2)] for w in range(2)]
    w_in = [[t.sem(f"sw_in{w}{n}") for n in range(2)] for w in range(2)]
    hi, lo, bb_in = t.sem("sw_hi"), t.sem("sw_lo"), t.sem("sw_bb_in")
    src = [w1.rearrange("e (c p) f -> e p c f", p=P), w2.rearrange("e (c p) n -> e p c n", p=P)]
    views = [lambda a: a.rearrange("p (c f) -> p c f", c=CC), lambda a: a.rearrange("p (c n) -> p c n", c=FC)]
    with nc.Block() as block:
        @block.sync
        def _(sp):
            for dst, src_bb in zip(bb, bb_dram):
                sp.dma_start(dst[:, :, :], src_bb).then_inc(bb_in, 16)
            for e in range(E):
                for w in range(2):
                    if e >= 2:
                        sp.wait_ge(lo, 2 * (e - 2) + w + 1)
                    sp.dma_start(views[w](stage[w][e % 2][:, :]), src[w][e]).then_inc(w_in[w][e % 2], 16)
            sp.wait_ge(bb_in, 32)

        @block.scalar
        def _(act):
            for e in range(E):
                for w, pair in enumerate((w1s, w2s)):
                    act.wait_ge(w_in[w][e % 2], 16 * (e // 2 + 1))
                    nc.scalar.copy(pair[0][:, e].rearrange("p a b -> p (a b)"), stage[w][e % 2][:, :]).then_inc(hi, 1)

        @block.vector
        def _(dve):
            for e in range(E):
                for w, pair in enumerate((w1s, w2s)):
                    dve.wait_ge(hi, 2 * e + w + 1)
                    nc.vector.tensor_tensor(pair[1][:, e].rearrange("p a b -> p (a b)"), stage[w][e % 2][:, :],
                                            pair[0][:, e].rearrange("p a b -> p (a b)"), ALU.subtract).then_inc(lo, 1)


def experts(nc, t, cst, xs, ys, tile_expert, bb, w1s, w2s):
    FC = F // P
    HALF = FC // 2
    ps_x = t.psum("ex_x", [P, CC, P])
    ps_h = [[t.psum(f"ex_h{n}{k}", [P, HALF, P]) for k in range(2)] for n in range(2)]
    ps_y = [t.psum(f"ex_y{n}", [P, C]) for n in range(2)]
    xc = t.sbuf("ex_xc", [P, 2, C])
    xh = t.sbuf("ex_xh", [P, 2, CC, P], FP16)
    xl = t.sbuf("ex_xl", [P, 2, CC, P], BF16)
    act_f = t.sbuf("ex_gelu", [P, 2, FC, P])
    ah = t.sbuf("ex_ah", [P, 2, FC, P], FP16)
    al = t.sbuf("ex_al", [P, 2, FC, P], BF16)
    yc = t.sbuf("ex_yc", [P, 2, C])
    bb1, bb2 = bb
    ident = const(cst, "ident")
    x_in, y_left = ([t.sem(f"ex_{n}{k}") for k in range(2)] for n in ("x_in", "y_left"))
    turned, xh_ready, xl_ready, h_ready, gelu_ready, ah_ready, al_ready, y_ready, y_used = (
        t.sem("ex_" + n) for n in ("turned", "xh_ready", "xl_ready", "h_ready", "gelu_ready", "ah_ready", "al_ready", "y_ready", "y_used"))
    xst = xs.rearrange("(i p) c -> i p c", p=P)
    yst = ys.rearrange("(i p) c -> i p c", p=P)
    row = lambda a: a.rearrange("a p c -> p (a c)")
    PAIRS = TILES // 2

    def over_pairs(eng, step):
        for par in range(2):
            step(0, par, par == 0)
        with eng.Fori(1, PAIRS) as k:
            for par in range(2):
                step(k, par, False)

    def expert_of(eng, tile):
        return eng.value_load(tile_expert[0:1, bass.ds(tile, 1)] if not isinstance(tile, int) else tile_expert[0:1, tile:tile + 1],
                              min_val=0, max_val=E - 1)

    with nc.Block() as block:
        @block.sync
        def _(sp):
            for par in range(2):
                sp.dma_start(xc[:, par], xst[par]).then_inc(x_in[par], 16)

            def load(k, par):
                sp.wait_ge(turned, 2 * k + par + 1)
                sp.dma_start(xc[:, par], row(xst[bass.ds(2 * (k + 1) + par, 1)])).then_inc(x_in[par], 16)

            def store(k, par):
                sp.wait_ge(y_used, 2 * k + par + 1)
                sp.dma_start(row(yst[bass.ds(2 * k + par, 1)]), yc[:, par]).then_inc(y_left[par], 16)

            for par in range(2):
                load(0, par)
            with sp.Fori(1, PAIRS - 1) as k:
                for par in range(2):
                    load(k, par)
                    store(k - 1, par)
            for k in range(PAIRS - 2, PAIRS):
                for par in range(2):
                    store(k, par)
            for par in range(2):
                sp.wait_ge(y_left[par], 16 * PAIRS)

        @block.tensor
        def _(pe):
            def turn(k, par, first):
                i = 2 * k + par
                pe.wait_ge(x_in[par], 16 * (k + 1))
                if not first:
                    pe.wait_ge(xl_ready, i)
                for cc in range(CC):
                    last = nc.tensor.transpose(ps_x[:, cc, :], xc[:, par, cc * P:(cc + 1) * P], ident)
                last.then_inc(turned, 1)

            def first_product(k, par, first):
                i = 2 * k + par
                e = expert_of(pe, i)
                pe.wait_ge(xl_ready, i + 1)
                for half in range(2):
                    if not first:
                        pe.wait_ge(gelu_ready, FC * (i - 2) + HALF * (half + 1))
                    for f in range(HALF):
                        fc = half * HALF + f
                        terms = [(w, a, cc) for cc in range(CC) for w, a in ((0, xh), (0, xl), (1, xh))]
                        for n, (w, a, cc) in enumerate(terms):
                            last = nc.tensor.matmul(ps_h[par][half][:, f, :],
                                                    w1s[w][:, bass.ds(e, 1), cc, fc * P:(fc + 1) * P].rearrange("p a f -> p (a f)"),
                                                    a[:, par, cc, :], start=(n == 0), stop=(n == len(terms) - 1))
                    last.then_inc(h_ready, 1)

            def second_product(k, par, first):
                i = 2 * k + par
                e = expert_of(pe, i)
                if not first:
                    pe.wait_ge(y_used, i - 1)
                for half in range(2):
                    pe.wait_ge(al_ready, 2 * i + half + 1)
                    for f in range(HALF):
                        fc = half * HALF + f
                        for n, (w, a) in enumerate(((0, ah), (0, al), (1, ah))):
                            last = nc.tensor.matmul(ps_y[par][:, :], a[:, par, fc, :],
                                                    w2s[w][:, bass.ds(e, 1), fc, :].rearrange("p a n -> p (a n)"),
                                                    start=(fc == 0 and n == 0), stop=(fc == FC - 1 and n == 2))
                last.then_inc(y_ready, 1)

            turn(0, 0, True)
            turn(0, 1, False)
            first_product(0, 0, True)
            turn(1, 0, False)
            first_product(0, 1, True)
            second_product(0, 0, True)
            turn(1, 1, False)
            first_product(1, 0, False)
            second_product(0, 1, True)
            with pe.Fori(1, PAIRS - 1) as k:
                turn(k + 1, 0, False)
                first_product(k, 1, False)
                second_product(k, 0, False)
                turn(k + 1, 1, False)
                first_product(k + 1, 0, False)
                second_product(k, 1, False)
            first_product(PAIRS - 1, 1, False)
            second_product(PAIRS - 1, 0, False)
            second_product(PAIRS - 1, 1, False)

        @block.scalar
        def _(act):
            def step(k, par, first):
                i = 2 * k + par
                act.wait_ge(turned, i + 1)
                if not (isinstance(k, int) and k == 0):
                    act.wait_ge(h_ready, 2 * (i - 1))
                nc.scalar.copy(xh[:, par], ps_x[:, :, :]).then_inc(xh_ready, 1)

            def gelu(k, par, first):
                i = 2 * k + par
                e = expert_of(act, i)
                for half in range(2):
                    act.wait_ge(h_ready, 2 * i + half + 1)
                    if not first:
                        act.wait_ge(al_ready, 2 * (i - 2) + half + 1)
                    for f in range(HALF):
                        fc = half * HALF + f
                        nc.scalar.activation(act_f[:, par, fc, :], ps_h[par][half][:, f, :], ACT.Gelu_apprx_tanh,
                                             bias=bb1[:, bass.ds(e, 1), fc:fc + 1].rearrange("p a f -> p (a f)")).then_inc(gelu_ready, 1)

            step(0, 0, True)
            step(0, 1, True)
            gelu(0, 0, True)
            step(1, 0, False)
            gelu(0, 1, True)
            step(1, 1, False)
            with act.Fori(1, PAIRS - 1) as k:
                gelu(k, 0, False)
                step(k + 1, 0, False)
                gelu(k, 1, False)
                step(k + 1, 1, False)
            gelu(PAIRS - 1, 0, False)
            gelu(PAIRS - 1, 1, False)

        @block.vector
        def _(dve):
            def low_x(k, par):
                i = 2 * k + par
                dve.wait_ge(xh_ready, i + 1)
                nc.vector.tensor_tensor(xl[:, par], ps_x[:, :, :], xh[:, par], ALU.subtract).then_inc(xl_ready, 1)

            def split(k, par, first):
                i = 2 * k + par
                for half in range(2):
                    part = slice(half * HALF, (half + 1) * HALF)
                    dve.wait_ge(gelu_ready, FC * i + HALF * (half + 1))
                    if not first and half == 0:
                        dve.wait_ge(y_ready, i - 1)
                    nc.vector.tensor_copy(ah[:, par, part], act_f[:, par, part]).then_inc(ah_ready, 1)
                    dve.wait_ge(ah_ready, 2 * i + half + 1)
                    nc.vector.tensor_tensor(al[:, par, part], act_f[:, par, part], ah[:, par, part], ALU.subtract).then_inc(al_ready, 1)

            def add_bias(k, par, first):
                i = 2 * k + par
                e = expert_of(dve, i)
                dve.wait_ge(y_ready, i + 1)
                if not first:
                    dve.wait_ge(y_left[par], 16 * k)
                nc.vector.tensor_tensor(yc[:, par], ps_y[par][:, :], bb2[:, bass.ds(e, 1), :].rearrange("p a n -> p (a n)"),
                                        ALU.add).then_inc(y_used, 1)

            low_x(0, 0)
            low_x(0, 1)
            split(0, 0, True)
            low_x(1, 0)
            split(0, 1, True)
            add_bias(0, 0, True)
            low_x(1, 1)
            split(1, 0, False)
            add_bias(0, 1, True)
            with dve.Fori(1, PAIRS - 1) as k:
                low_x(k + 1, 0)
                split(k, 1, False)
                add_bias(k, 0, False)
                low_x(k + 1, 1)
                split(k + 1, 0, False)
                add_bias(k, 1, False)
            split(PAIRS - 1, 1, False)
            add_bias(PAIRS - 1, 0, False)
            add_bias(PAIRS - 1, 1, False)


def combine(nc, t, cst, weight, place, ys, h, x1, out):
    y = t.sbuf("co_y", [P, 2, NT, 2, C])
    hc = t.sbuf("co_h", [P, 2, NT, C])
    xc = t.sbuf("co_x", [P, 2, NT, C])
    part = t.sbuf("co_part", [P, NT, C])
    s = t.sbuf("co_sum", [P, NT, C])
    norm1 = t.sbuf("co_norm", [P, NT, C])
    gained = t.sbuf("co_gained", [P, NT, C])
    v = t.sbuf("co_v", [P, NT, C])
    vn = t.sbuf("co_vn", [P, NT, C])
    result = t.sbuf("co_result", [P, 2, NT, C])
    stats = t.sbuf("co_stats", [P, 2, NT, 6])
    mv = t.sbuf("co_mv", [P, 2, NT, 2])
    std = t.sbuf("co_std", [P, 2, NT])
    rstd = t.sbuf("co_rstd", [P, 2, NT])
    y_in, h_in, x_in, left = ([t.sem(f"co_{n}{k}") for k in range(2)] for n in ("y_in", "h_in", "x_in", "left"))
    part_ready, sum_ready, n_ready, gained_ready, v_ready, vn_ready, ready = (
        t.sem("co_" + n) for n in ("part_ready", "sum_ready", "n_ready", "gained_ready", "v_ready", "vn_ready", "ready"))
    stats_done, var_ready, std_ready, rstd_ready = ([t.sem(f"co_{n}{k}") for k in range(2)] for n in ("stats", "var", "std", "rstd"))
    eps = const(cst, "eps")
    tiles = lambda a: a.rearrange("b (s j p) c -> (b s) p j c", s=2, p=P)
    one = lambda a: a.rearrange("a p j c -> p (a j) c")
    over_tiles = lambda a: a.unsqueeze(1).to_broadcast([P, NT, C])
    chunks = 2 * B

    with nc.Block() as block:
        @block.gpsimd
        def _(pool):
            for ck in range(chunks):
                if ck >= 2:
                    pool.wait_ge(sum_ready, NT * (ck - 1))
                for j in range(NT):
                    for e in range(2):
                        nc.gpsimd.indirect_dma_start(y[:, ck % 2, j, e, :], None, ys,
                                                     bass.IndirectOffsetOnAxis(place[:, e, ck * NT + j:ck * NT + j + 1], 0)).then_inc(y_in[ck % 2], 16)

        @block.sync
        def _(sp):
            def load(b, half):
                sp.dma_start(hc[:, half], one(tiles(h)[bass.ds(2 * b + half, 1)])).then_inc(h_in[half], 16)
                sp.dma_start(xc[:, half], one(tiles(x1)[bass.ds(2 * b + half, 1)])).then_inc(x_in[half], 16)

            def chunk(b, half, more):
                ck = 2 * b + half
                sp.wait_ge(ready, ck + 1)
                sp.dma_start(one(tiles(out)[bass.ds(ck, 1)]), result[:, half]).then_inc(left[half], 16)
                if more:
                    load(b + 1, half)

            for half in range(2):
                load(0, half)
            with sp.Fori(0, B - 1) as b:
                for half in range(2):
                    chunk(b, half, True)
            for half in range(2):
                chunk(B - 1, half, False)
            for half in range(2):
                sp.wait_ge(left[half], 16 * B)

        @block.scalar
        def _(act):
            def chunk(b, half, first):
                for k in range(2):
                    act.wait_ge(var_ready[k], NT * (2 * b + half + 1))
                    nc.scalar.activation(std[:, k, :], mv[:, k, :, 1], ACT.Sqrt, bias=eps).then_inc(std_ready[k], 1)

            over_chunks(act, chunk)

        @block.vector
        def _(dve):
            def norm(ck, k, src, dst, ready):
                for j in range(NT):
                    nc.vector.bn_stats(stats[:, k, j], src[:, j, :]).then_inc(stats_done[k], 1)
                dve.wait_ge(stats_done[k], NT * (ck + 1))
                nc.vector.memset(std[:, k, :], 0.0)
                for j in range(NT):
                    nc.vector.bn_aggr(mv[:, k, j], stats[:, k, j]).then_inc(var_ready[k], 1)
                dve.wait_ge(std_ready[k], ck + 1)
                nc.vector.reciprocal(rstd[:, k, :], std[:, k, :]).then_inc(rstd_ready[k], 1)
                dve.wait_ge(rstd_ready[k], ck + 1)
                for j in range(NT):
                    nc.vector.tensor_scalar(dst[:, j], src[:, j], mv[:, k, j, 0:1], rstd[:, k, j:j + 1], ALU.subtract, ALU.mult).then_inc(ready, 1)

            def chunk(b, half, first):
                ck = 2 * b + half
                dve.wait_ge(h_in[half], 16 * (b + 1))
                dve.wait_ge(y_in[half], 16 * 2 * NT * (b + 1))
                share = lambda j, e: weight[:, bass.ds(ck * NT + j, 1), e]
                for j in range(NT):
                    nc.vector.scalar_tensor_tensor(out=part[:, j], in0=y[:, half, j, 0], scalar=share(j, 0), in1=hc[:, half, j],
                                                   op0=ALU.mult, op1=ALU.add).then_inc(part_ready, 1)
                dve.wait_ge(part_ready, NT * (ck + 1))
                for j in range(NT):
                    nc.vector.scalar_tensor_tensor(out=s[:, j], in0=y[:, half, j, 1], scalar=share(j, 1), in1=part[:, j],
                                                   op0=ALU.mult, op1=ALU.add).then_inc(sum_ready, 1)
                dve.wait_ge(sum_ready, NT * (ck + 1))
                norm(ck, 0, s, norm1, n_ready)
                dve.wait_ge(n_ready, NT * (ck + 1))
                nc.vector.tensor_tensor(gained[:, :, :], norm1[:, :, :], over_tiles(const(cst, "g2")), ALU.mult).then_inc(gained_ready, 1)
                dve.wait_ge(gained_ready, ck + 1)
                nc.vector.tensor_tensor(v[:, :, :], gained[:, :, :], over_tiles(const(cst, "b2")), ALU.add).then_inc(v_ready, 1)
                dve.wait_ge(v_ready, ck + 1)
                norm(ck, 1, v, vn, vn_ready)
                dve.wait_ge(vn_ready, NT * (ck + 1))
                dve.wait_ge(x_in[half], 16 * (b + 1))
                if not isinstance(b, int):
                    dve.wait_ge(left[half], 16 * b)
                nc.vector.tensor_tensor(result[:, half], xc[:, half], vn[:, :, :], ALU.add).then_inc(ready, 1)

            over_chunks(dve, chunk)


UNITS = 12
LAG = 2
RING = 4

ROWS = [(qt, 0, P * (qt + 1)) for qt in range(4)] + \
       [x for qt in range(4, KB) for x in ((qt, 0, 512), (qt, 4, P * (qt - 3)))]
COLUMNS = [(qc, j, max(512 * qc, P * j)) for qc in range(2) for j in range(4 * qc + 4)]


def attention(nc, t, name, cst, masks, qk, vs, part_rows, scale, os):
    ps_s = [t.psum(f"{name}_s{n}", [P, 512]) for n in range(2)]
    ps_st = [t.psum(f"{name}_st{n}", [P, 512]) for n in range(3)]
    ps_o = [t.psum(f"{name}_o{n}", [P, 512]) for n in range(2)]
    ps_m = t.psum(f"{name}_m", [P, 512])
    stack = [[t.sbuf(f"{name}_{w}{n}", [98, T], F32R) for n in range(RING)] for w in "qk"]
    vh = t.sbuf(f"{name}_v", [P, RING, KB, 2 * HD])
    prob = t.sbuf(f"{name}_p", [P, 3, 512])
    maxima = t.sbuf(f"{name}_mx", [P, 2, UNITS])
    split = t.sbuf(f"{name}_split", [P, 2, 2, KB], F32R)
    mrow = t.sbuf(f"{name}_mrow", [2 * KB, RING, P], F32R)
    oT = t.sbuf(f"{name}_oT", [P, 2, 512])
    recip = t.sbuf(f"{name}_recip", [P, 2, 4, 4])
    ob = t.sbuf(f"{name}_ob", [P, 2, 4, 4, HD])
    ident = const(cst, "ident")
    ident_b, mask_rows, mask_cols = masks[:, 0], masks[:, 1], masks[:, 2]

    loaded = [t.sem(f"{name}_loaded{n}") for n in range(RING)]
    mrow_in = [t.sem(f"{name}_mrow_in{n}") for n in range(RING)]
    stored = [t.sem(f"{name}_stored{n}") for n in range(2)]
    zeroed, s_ready, s_reduced, st_ready, p_ready, pv_done = (
        t.sem(f"{name}_" + n) for n in ("zeroed", "s_ready", "s_reduced", "st_ready", "p_ready", "pv_done"))
    joined, high, split_ready, mT_ready, mrow_ready = (
        t.sem(f"{name}_" + n) for n in ("joined", "high", "split_ready", "mT_ready", "mrow_ready"))
    oT_ready, o_turned, recip_ready, o_ready = (t.sem(f"{name}_" + n) for n in ("oT_ready", "o_turned", "recip_ready", "o_ready"))
    LOADS = 16 * 7
    groups = NH // 4

    def over_groups(eng, body):
        body(0, True, False)
        with eng.Fori(1, groups - 1) as g:
            body(g, False, False)
        body(groups - 1, False, True)

    with nc.Block() as block:
        @block.sync
        def _(sp):
            def load(head, slot):
                for part, (hq, hk) in enumerate(((0, 0), (0, 1), (1, 0))):
                    for w, hl in ((0, hq), (1, hk)):
                        src = qk[w][hl][bass.ds(head, 1), 0:part_rows, :].rearrange("a r t -> (a r) t")
                        sp.dma_start(stack[w][slot][32 * part:32 * part + part_rows, :].bitcast(F32), src).then_inc(loaded[slot], 16)
                sp.dma_start(vh[:, slot], vs[bass.ds(head, 1), :, :].rearrange("a p (k e) -> p (a k) e", e=2 * HD)).then_inc(loaded[slot], 16)

            def store(g, qc):
                sp.wait_ge(o_ready, 2 * g + qc + 1)
                sp.dma_start(os[bass.ds(g * 2 + qc, 1)].rearrange("a p q d -> p (a q) d"),
                             ob[:, qc].rearrange("p q h d -> p q (h d)")).then_inc(stored[qc], 16)

            sp.wait_ge(zeroed, 3)
            for n in range(3):
                load(n, n)

            def body(g, first, last):
                for h in range(4):
                    n = 4 * g + h
                    if not (last and h > 0):
                        if not (first and h == 0):
                            sp.wait_ge(pv_done, UNITS * n)
                        load(n + 3, (h + 3) % 4)
                    if first and h == 0:
                        for m in range(2):
                            rows(m, m)
                    elif not (last and h == 3):
                        rows(n + 1, (h + 1) % 4)
                    if h == 0 and not first:
                        store(g - 1, 1)
                store(g, 0)

            def rows(m, slot):
                sp.wait_ge(mrow_ready, m + 1)
                for k in range(2):
                    sp.dma_start(stack[0][slot][96 + k:97 + k, :].bitcast(F32), mrow[k * KB:(k + 1) * KB, slot, :].bitcast(F32)).then_inc(mrow_in[slot], 16)

            over_groups(sp, body)
            store(groups - 1, 1)
            for qc in range(2):
                sp.wait_ge(stored[qc], 16 * groups)

        @block.gpsimd
        def _(pool):
            for n in range(RING):
                for w in range(2):
                    last = nc.gpsimd.memset(stack[w][n][0:96, :].bitcast(F32), 0.0)
            last.then_inc(zeroed, 1)
            for n in range(RING):
                last = nc.gpsimd.memset(stack[1][n][96:98, :].bitcast(F32), -1.0)
            last.then_inc(zeroed, 2)

        @block.vector
        def _(dve):
            def reduce(m, u, parity):
                qt, k0, width = ROWS[u]
                dve.wait_ge(s_ready, UNITS * m + u + 1)
                nc.vector.tensor_reduce(maxima[:, parity, u:u + 1], ps_s[u % 2][:, 0:width], AX.X, ALU.max).then_inc(s_reduced, 1)

            def join(m, parity):
                dve.wait_ge(s_reduced, UNITS * (m + 1))
                two = maxima[:, parity, 4:UNITS].rearrange("p (q k) -> p q k", k=2)
                nc.vector.tensor_tensor(maxima[:, parity, 4:8], two[:, :, 0], two[:, :, 1], ALU.max).then_inc(joined, 1)
                dve.wait_ge(joined, m + 1)
                nc.vector.tensor_copy(split[:, parity, 0], maxima[:, parity, 0:KB]).then_inc(high, 1)
                dve.wait_ge(high, m + 1)
                nc.vector.tensor_tensor(split[:, parity, 1], maxima[:, parity, 0:KB], split[:, parity, 0].bitcast(F32),
                                        ALU.subtract).then_inc(split_ready, 1)

            def take_rows(m, slot):
                dve.wait_ge(mT_ready, m + 1)
                nc.vector.tensor_copy(mrow[:, slot, :], ps_m[0:2 * KB, 0:P]).then_inc(mrow_ready, 1)

            def normalise(g, qc, first):
                dve.wait_ge(o_turned, 2 * g + qc + 1)
                o = ps_m[:, :].rearrange("p (q h e) -> p q h e", q=4, h=4)
                nc.vector.reciprocal(recip[:, qc], o[:, :, :, HD]).then_inc(recip_ready, 1)
                dve.wait_ge(recip_ready, 2 * g + qc + 1)
                if not first:
                    dve.wait_ge(stored[qc], 16 * g)
                nc.vector.tensor_tensor(ob[:, qc], o[:, :, :, 0:HD], recip[:, qc].unsqueeze(3).to_broadcast([P, 4, 4, HD]),
                                        ALU.mult).then_inc(o_ready, 1)

            for m in range(2):
                for u in range(UNITS):
                    reduce(m, u, m)
                join(m, m)
            take_rows(0, 0)

            def body(g, first, last):
                for h in range(4):
                    n = 4 * g + h
                    for u in range(UNITS):
                        if not (last and h >= 2):
                            reduce(n + 2, u, h % 2)
                        if u == 5 and not (last and h == 3):
                            take_rows(n + 1, (h + 1) % 4)
                        if u == 9 and h == 0 and not first:
                            normalise(g - 1, 1, first_second)
                    if not (last and h >= 2):
                        join(n + 2, h % 2)
                normalise(g, 0, first)

            first_second = True
            body(0, True, False)
            body(1, False, False)
            first_second = False
            with dve.Fori(2, groups - 1) as g:
                body(g, False, False)
            body(groups - 1, False, True)
            normalise(groups - 1, 1, False)

        @block.scalar
        def _(act):
            def take_output(g, qc, first):
                act.wait_ge(pv_done, UNITS * 4 * g + (UNITS * 3 + 4 if qc == 0 else UNITS * 4))
                if not first:
                    act.wait_ge(o_turned, 2 * g + qc - 1)
                nc.scalar.copy(oT[:, qc, :], ps_o[qc][:, :]).then_inc(oT_ready, 1)

            def body(g, first, last):
                for h in range(4):
                    n = 4 * g + h
                    for u in range(UNITS):
                        qc, j, q0 = COLUMNS[u]
                        width = 512 * (qc + 1) - q0
                        act.wait_ge(st_ready, UNITS * n + u + 1)
                        if not (first and h == 0 and u < 3):
                            act.wait_ge(pv_done, UNITS * n + u - 2)
                        nc.scalar.activation(prob[:, u % 3, 0:width], ps_st[u % 3][:, 0:width], ACT.Exp, scale=scale).then_inc(p_ready, 1)
                        if u == 2 and h == 0 and not first:
                            take_output(g - 1, 1, first_two)
                        if u == 7 and h == 3:
                            take_output(g, 0, first)

            first_two = True
            body(0, True, False)
            body(1, False, False)
            first_two = False
            with act.Fori(2, groups) as g:
                body(g, False, False)
            take_output(groups - 1, 1, False)

        @block.tensor
        def _(pe):
            def row_scores(m, u, slot, first):
                qt, k0, width = ROWS[u]
                if not first:
                    pe.wait_ge(s_reduced, UNITS * m + u - 1)
                on_diagonal = k0 * P + width == (qt + 1) * P
                ins = nc.tensor.matmul(ps_s[u % 2][:, 0:width], stack[0][slot][0:96, qt * P:(qt + 1) * P],
                                       stack[1][slot][0:96, k0 * P:k0 * P + width], start=True, stop=not on_diagonal)
                if on_diagonal:
                    ins = nc.tensor.matmul(ps_s[u % 2][:, width - P:width], ident_b, mask_rows, start=False, stop=True)
                ins.then_inc(s_ready, 1)

            def column_scores(n, u, slot, first):
                qc, j, q0 = COLUMNS[u]
                width = 512 * (qc + 1) - q0
                if not first:
                    pe.wait_ge(p_ready, UNITS * n + u - 2)
                ins = nc.tensor.matmul(ps_st[u % 3][:, 0:width], stack[1][slot][:, j * P:(j + 1) * P], stack[0][slot][:, q0:q0 + width],
                                       start=True, stop=j < 4 * qc)
                if j >= 4 * qc:
                    ins = nc.tensor.matmul(ps_st[u % 3][:, 0:P], ident_b, mask_cols, start=False, stop=True)
                ins.then_inc(st_ready, 1)

            def value_product(n, u, h):
                qc, j, q0 = COLUMNS[u]
                width = 512 * (qc + 1) - q0
                pe.wait_ge(p_ready, UNITS * n + u + 1)
                nc.tensor.matmul(ps_o[qc][32 * h:32 * h + 32, 512 - width:512], vh[:, h, j, :], prob[:, u % 3, 0:width],
                                 start=(j == 0), stop=(j == 4 * qc + 3)).then_inc(pv_done, 1)

            def turn_maxima(m, parity):
                pe.wait_ge(split_ready, m + 1)
                nc.tensor.transpose(ps_m[0:2 * KB, 0:P], split[:, parity].rearrange("p s q -> p (s q)").bitcast(F32), ident).then_inc(mT_ready, 1)

            def turn_output(g, qc):
                pe.wait_ge(oT_ready, 2 * g + qc + 1)
                for q in range(4):
                    last = nc.tensor.transpose(ps_m[:, q * P:(q + 1) * P], oT[:, qc, q * P:(q + 1) * P], ident)
                last.then_inc(o_turned, 1)

            for m in range(2):
                pe.wait_ge(loaded[m], LOADS)
                for u in range(UNITS):
                    row_scores(m, u, m, m == 0 and u < 2)
            turn_maxima(0, 0)

            def body(g, first, last):
                for h in range(4):
                    n = 4 * g + h
                    for u in range(UNITS):
                        if not (last and h >= 2):
                            if u == 0:
                                pe.wait_ge(loaded[(h + 2) % 4], LOADS * (g + 1 + h // 2))
                            row_scores(n + 2, u, (h + 2) % 4, False)
                        if u == 0:
                            pe.wait_ge(mrow_in[h], 32 * (g + 1))
                        column_scores(n, u, h, first and h == 0 and u < 3)
                        if u >= LAG:
                            if h == 0 and not first and u == LAG:
                                pe.wait_ge(oT_ready, 2 * g - 1)
                            if h == 0 and not first and u == LAG + 4:
                                pe.wait_ge(oT_ready, 2 * g)
                            value_product(n, u - LAG, h)
                        elif h > 0:
                            value_product(n - 1, UNITS + u - LAG, h - 1)
                        elif not first:
                            value_product(n - 1, UNITS + u - LAG, 3)
                        if u == 3 and not (last and h == 3):
                            if h == 0 and not first:
                                pe.wait_ge(o_ready, 2 * g - 1)
                            elif h == 1 and not first:
                                pe.wait_ge(o_ready, 2 * g)
                            else:
                                pe.wait_ge(mrow_ready, n + 1)
                            turn_maxima(n + 1, (h + 1) % 2)
                        if u == 8 and h == 0 and not first:
                            pe.wait_ge(mrow_ready, n + 2)
                            turn_output(g - 1, 1)
                    if h == 3:
                        pe.wait_ge(mrow_ready, n + (1 if last else 2))
                        turn_output(g, 0)

            over_groups(pe, body)
            for u in range(UNITS - LAG, UNITS):
                value_product(NH - 1, u, 3)
            pe.wait_ge(o_ready, 2 * groups - 1)
            turn_output(groups - 1, 1)


def build(nc, a, outs):
    internal = lambda name, shape, dt=F32: nc.dram_tensor(name, shape, dt, kind="Internal").ap()
    qk = [[internal(f"{w}_{hl}", [NH, 2 * HD, T]) for hl in ("high", "low")] for w in "qk"]
    vs = internal("v_rows", [NH, P, KB * 2 * HD])
    os = internal("attended", [NH // 4 * 2, P, 4, 4 * HD])
    x1, n1, h = (internal(n, [B, T, C]) for n in ("x1", "n1", "h_rows"))
    xs, ys = (internal(n, [TILES * P, C]) for n in ("sorted_rows", "expert_rows"))
    sems = []
    with ExitStack() as whole:
        t = outer = Tools(nc, whole, sems)
        cst = {"block": t.sbuf("constants", [P, WIDTH["block"]])}
        masks = t.sbuf("masks", [P, 3, P], BF16)
        wout = t.sbuf("w_out1", [P, 2, C])
        cout = t.sbuf("bias_out1", [P, C])
        masked = t.sem("masked")
        with nc.Block() as block:
            @block.gpsimd
            def _(pool):
                nc.gpsimd.memset(masks[:, 0], 0.0).then_inc(masked, 1)
                nc.gpsimd.memset(masks[:, 1:3], 0.0).then_inc(masked, 1)
                pool.wait_ge(masked, 2)
                nc.gpsimd.affine_select(out=masks[:, 0], in_=masks[:, 0], compare_op=ALU.not_equal, fill=1.0, base=0,
                                        pattern=[[-1, P]], channel_multiplier=1)
                nc.gpsimd.affine_select(out=masks[:, 1], in_=masks[:, 1], compare_op=ALU.is_ge, fill=MASKED, base=0,
                                        pattern=[[-1, P]], channel_multiplier=1)
                nc.gpsimd.affine_select(out=masks[:, 2], in_=masks[:, 2], compare_op=ALU.is_ge, fill=MASKED, base=0,
                                        pattern=[[1, P]], channel_multiplier=-1)
        with ExitStack() as ctx:
            t = Tools(nc, ctx, sems)
            cst["latent"] = t.sbuf("latent_constants", [P, WIDTH["latent"]])
            rope = t.sbuf("rope", [P, 2, T])
            wlat = t.sbuf("w_latent", [P, CC, 2, 2, 2, P])
            blat = t.sbuf("b_latent", [P, 2, 2, 2])
            with ExitStack() as inner:
                compose_weights(nc, Tools(nc, inner, sems), {which: a[which] for which in PACKS}, cst, a["rope"], rope, wlat, blat, wout, cout)
            with ExitStack() as inner:
                latent_projections(nc, Tools(nc, inner, sems), a["x"], cst, rope, wlat, blat, qk, vs)
        with ExitStack() as ctx:
            attention(nc, Tools(nc, ctx, sems), "a1", cst, masks, qk, vs, 2 * HD, float(L) ** -0.5, os)
        renew_semaphores(nc, sems)
        with ExitStack() as ctx:
            between_attentions(nc, Tools(nc, ctx, sems), a["x"], os, cst, wout, cout, x1, n1, qk, vs)
        with ExitStack() as ctx:
            attention(nc, Tools(nc, ctx, sems), "a2", cst, masks, qk, vs, HD, float(HD) ** -0.5, os)
        renew_semaphores(nc, sems)
        logits = outer.sbuf("logits", [P, TT, E])
        weight = outer.sbuf("weight", [P, TT, 2])
        place = outer.sbuf("place", [P, 2, TT], U32)
        tile_expert = outer.sbuf("tile_expert", [P, TILES], mybir.dt.int32)
        with ExitStack() as ctx:
            after_attentions(nc, Tools(nc, ctx, sems), n1, os, cst, h, logits)
        with ExitStack() as ctx:
            route(nc, Tools(nc, ctx, sems), cst, logits, weight, place, tile_expert, xs)
        with ExitStack() as ctx:
            scatter_rows(nc, Tools(nc, ctx, sems), h, place, xs)
        with ExitStack() as ctx:
            e = Tools(nc, ctx, sems)
            w1s = [e.sbuf("w1_high", [P, E, CC, F], FP16), e.sbuf("w1_low", [P, E, CC, F], BF16)]
            w2s = [e.sbuf("w2_high", [P, E, F // P, C], FP16), e.sbuf("w2_low", [P, E, F // P, C], BF16)]
            bb = [e.sbuf("bb1", [P, E, F // P]), e.sbuf("bb2", [P, E, C])]
            with ExitStack() as inner:
                split_expert_weights(nc, Tools(nc, inner, sems), a["w1"], a["w2"], w1s, w2s, [a["bb1"], a["bb2"]], bb)
            with ExitStack() as inner:
                experts(nc, Tools(nc, inner, sems), cst, xs, ys, tile_expert, bb, w1s, w2s)
        with ExitStack() as ctx:
            combine(nc, Tools(nc, ctx, sems), cst, weight, place, ys, h, x1, outs["out"])


def kernel(**inputs):
    import concourse.bacc as _bacc
    from concourse.bass_utils import run_bass_kernel_spmd as _run

    i = {k: np.asarray(v) for k, v in inputs.items()}
    arrays = {
        "x": np.ascontiguousarray(i["L0_attn_x"]),
        "latent": pack("latent", attention_constants(i)),
        "block": pack("block", block_constants(i)),
        "w1": np.ascontiguousarray(i["L0_ffn_w1"]),
        "w2": np.ascontiguousarray(i["L0_ffn_w2"]),
        "bb1": np.ascontiguousarray(i["L0_ffn_bb1"].reshape(E, F // P, P).transpose(2, 0, 1)),
        "bb2": np.tile(i["L0_ffn_bb2"], (P, 1, 1)),
        "rope": rope_tables(),
    }
    nc = _bacc.Bacc("TRN2", target_bir_lowering=False, num_devices=1)
    a = {n: nc.dram_tensor(n + "_dram", v.shape, mybir.dt.from_np(v.dtype), kind="ExternalInput").ap() for n, v in arrays.items()}
    out = nc.dram_tensor("out_dram", (B, T, C), F32, kind="ExternalOutput").ap()
    build(nc, a, {"out": out})
    r = _run(nc, [{n + "_dram": v for n, v in arrays.items()}], core_ids=[0])
    return r.results[0]["out_dram"]
```

```python
from contextlib import ExitStack

import concourse.bass as bass
from concourse import mybir
import numpy as np

F32 = mybir.dt.float32
F32R = mybir.dt.float32r
BF16 = mybir.dt.bfloat16
FP16 = mybir.dt.float16
U32 = mybir.dt.uint32
ALU = mybir.AluOpType
ACT = mybir.ActivationFunctionType
AX = mybir.AxisListType

P = 128
B, T, C = 4, 1024, 256
H, HD, L = 16, 16, 32
NH = B * H
E, F = 8, 1024
CC = C // P
CH = 512
NT = CH // P
KB = T // P
TT = B * T // P
TILES = 2 * TT + E
EPS = 1e-5
MASKED = -1e30

PACKS = {
    "latent": dict(
        wq_rows=2 * C,
        wk_rows=2 * C,
        bq=2, bk=2,
        q2l_blocks=2 * P,
        kv2l_blocks=2 * P,
        q2l_bias=2, kv2l_bias=2,
        wqk_blocks=4 * P,
        wqk_bias=2,
        wv=CC * C,
        bv=C,
        l2o_blocks=4 * P,
        kvl_blocks=4 * P,
        cproj=2 * C,
        l2o_bias=P,
        kvl_bias=P,
        cproj_bias=C,
    ),
    "block": dict(
        ident=P,
        eps=1,
        wqkv2=CC * 3 * C,
        wo2=CC * C,
        g1=C, b1=C, g2=C, b2=C,
        wg=CC * E,
        before=P,
        ones=P,
        expert=E,
        tile=TILES,
    ),
}
PLACE = {name: (pack, sum(list(widths.values())[:k]), width)
         for pack, widths in PACKS.items() for k, (name, width) in enumerate(widths.items())}
WIDTH = {pack: sum(widths.values()) for pack, widths in PACKS.items()}


def pack(which, named):
    out = np.zeros((P, WIDTH[which]), np.float32)
    for name, a in named.items():
        _, at, width = PLACE[name]
        out[: a.shape[0], at:at + width] = a.reshape(a.shape[0], -1)
    return out


def const(cst, name):
    which, at, width = PLACE[name]
    return cst[which][:, at:at + width]


def attention_constants(i):
    w, bias = i["L0_attn_c_attn_w"], i["L0_attn_c_attn_b"]
    q2l, kv2l, wqk, l2o = (i["L0_attn_" + n] for n in ("q2l_w", "kv2l_w", "wqk_w", "l2o_w"))
    rows = lambda a: a.reshape(2, P, C).transpose(1, 0, 2)
    halves = lambda a: a.reshape(2, P).T

    def blocks(m):
        r, c = m.shape
        out = np.zeros((8, r, 8, c), np.float32)
        for h in range(8):
            out[h, :, h, :] = m
        return out.reshape(8 * r, 8 * c)

    wqk_blocks = np.stack([blocks(wqk[po::2, pi::2].T) for po in range(2) for pi in range(2)], 1)
    l2o_blocks = np.zeros((8, HD, 4, 4, L), np.float32)
    kvl_blocks = np.zeros((4, L, 4, 8, HD), np.float32)
    for hg in range(4):
        for h in range(4):
            l2o_blocks[(hg % 2) * 4 + h, :, hg, h, :] = l2o
            kvl_blocks[h, :, hg, (hg % 2) * 4 + h, :] = kv2l
    tiled = lambda v: np.tile(v, 8)[:, None]
    return {
        "wq_rows": rows(w[:C]), "wk_rows": rows(w[C:2 * C]),
        "bq": halves(bias[:C]), "bk": halves(bias[C:2 * C]),
        "q2l_blocks": np.stack([blocks(q2l[p::2].T) for p in range(2)], 1),
        "kv2l_blocks": np.stack([blocks(kv2l[p::2].T) for p in range(2)], 1),
        "q2l_bias": np.concatenate([tiled(i["L0_attn_q2l_b"][p::2]) for p in range(2)], 1),
        "kv2l_bias": np.concatenate([tiled(i["L0_attn_kv2l_b"][p::2]) for p in range(2)], 1),
        "wqk_blocks": wqk_blocks,
        "wqk_bias": np.concatenate([tiled(i["L0_attn_wqk_b"][p::2]) for p in range(2)], 1),
        "wv": w[2 * C:].T.reshape(CC, P, C).transpose(1, 0, 2),
        "bv": np.tile(bias[2 * C:], (P, 1)),
        "l2o_blocks": l2o_blocks.reshape(P, 4 * P), "kvl_blocks": kvl_blocks.reshape(P, 4 * P),
        "cproj": i["L0_attn_cproj_w"].T.reshape(2, P, C).transpose(1, 0, 2),
        "l2o_bias": np.tile(np.tile(i["L0_attn_l2o_b"], 8)[:, None], (1, P)),
        "kvl_bias": np.tile(np.tile(i["L0_attn_kv2l_b"], 4)[:, None], (1, P)),
        "cproj_bias": np.tile(i["L0_attn_cproj_b"], (P, 1)),
    }


def block_constants(i):
    chunks = lambda a: a.reshape(CC, P, -1).transpose(1, 0, 2)
    f = lambda n: i["L0_ffn_" + n]
    out = {
        "wqkv2": chunks(f("w_qkv")), "wo2": chunks(f("w_o")), "wg": chunks(f("wg")),
        "ident": np.eye(P, dtype=np.float32), "eps": np.full((P, 1), EPS, np.float32),
        "before": np.triu(np.ones((P, P), np.float32), 1), "ones": np.ones((P, P), np.float32),
        "expert": np.tile(np.arange(E, dtype=np.float32), (P, 1)), "tile": np.tile(np.arange(TILES, dtype=np.float32), (P, 1)),
    }
    return out | {n: np.tile(f(n), (P, 1)) for n in ("g1", "b1", "g2", "b2")}


def rope_tables():
    inv = (1.0 / 10000.0 ** (np.arange(0, L, 2, dtype=np.float32) / np.float32(L))).astype(np.float32)
    angle = np.tile(inv, 8)[:, None] * np.arange(T, dtype=np.float32)[None, :]
    return np.stack([np.cos(angle), np.sin(angle)], 1).astype(np.float32)


def over_chunks(eng, chunk):
    for half in range(2):
        chunk(0, half, half == 0)
    with eng.Fori(1, B) as b:
        for half in range(2):
            chunk(b, half, False)


def over_chunks_ahead(eng, begin, finish):
    def ahead(b, half):
        def call(*between):
            begin(b, half, False, *between)
            return True
        return call

    begin(0, 0, True)
    finish(0, 0, True, ahead(0, 1))
    finish(0, 1, False, ahead(1, 0))
    with eng.Fori(1, B - 1) as b:
        finish(b, 0, False, ahead(b, 1))
        finish(b, 1, False, ahead(b + 1, 0))
    finish(B - 1, 0, False, ahead(B - 1, 1))
    finish(B - 1, 1, False, lambda *between: False)


def beyond_first_batch(b):
    return not isinstance(b, int) or b > 0


class Tools:

    def __init__(self, nc, ctx, sems):
        self.nc, self.ctx, self.sems = nc, ctx, sems

    def sbuf(self, name, shape, dt=F32):
        return self.ctx.enter_context(self.nc.sbuf_tensor(name, shape, dt))

    def psum(self, name, shape, dt=F32):
        return self.ctx.enter_context(self.nc.psum_tensor(name, shape, dt))

    def sem(self, name):
        self.sems.append(self.nc.alloc_semaphore(name))
        return self.sems[-1]


def renew_semaphores(nc, sems):
    nc.clear_and_free_semaphores(sems)
    sems.clear()
    nc.all_engine_barrier()


def compose_weights(nc, t, packed, cst, rope_dram, rope, wlat, blat, wout, cout):
    ps = [t.psum(f"cw_ps{n}", [P, 512]) for n in range(2)]
    t1 = t.sbuf("cw_t1", [P, 4, C])
    loaded, made, moved = t.sem("cw_loaded"), t.sem("cw_made"), t.sem("cw_moved")

    c = lambda name: const(cst, name)
    rows = [c("wq_rows").rearrange("p (g c) -> p g c", g=2), c("wk_rows").rearrange("p (g c) -> p g c", g=2)]
    to_latent = [c("q2l_blocks").rearrange("p (e m) -> p e m", e=2), c("kv2l_blocks").rearrange("p (e m) -> p e m", e=2)]
    l2o = c("l2o_blocks").rearrange("p (g m) -> p g m", g=4)
    kvl = c("kvl_blocks").rearrange("p (g m) -> p g m", g=4)
    cproj = c("cproj").rearrange("p (g n) -> p g n", g=2)
    with nc.Block() as block:
        @block.sync
        def _(sp):
            for which in PACKS:
                sp.dma_start(cst[which][:, :], packed[which]).then_inc(loaded, 16)
            sp.dma_start(rope[:, :, :], rope_dram).then_inc(loaded, 16)

        @block.tensor
        def _(pe):
            pe.wait_ge(loaded, 48)
            step = 0
            for w in range(2):
                for g in range(2):
                    if step >= 2:
                        pe.wait_ge(moved, step - 1)
                    for cc in range(CC):
                        last = nc.tensor.matmul(ps[step % 2][:, cc * C:(cc + 1) * C], rows[w][:, g, cc * P:(cc + 1) * P],
                                                to_latent[w].rearrange("p e m -> p (e m)"), start=True, stop=True)
                    last.then_inc(made, 1)
                    step += 1
            pe.wait_ge(moved, step - 1)
            for w, b in enumerate(("bq", "bk")):
                for e in range(2):
                    last = nc.tensor.matmul(ps[0][:, (w * 2 + e) * 2:(w * 2 + e) * 2 + 2], to_latent[w][:, e, :], c(b),
                                            start=True, stop=True)
            last.then_inc(made, 1)
            step += 1
            for hg in range(4):
                pe.wait_ge(moved, step - 1)
                nc.tensor.matmul(ps[step % 2][:, 0:C], l2o[:, hg, :], cproj[:, hg // 2, :], start=True, stop=True).then_inc(made, 1)
                step += 1
            pe.wait_ge(moved, step)
            for g in range(2):
                for k in range(2):
                    last = nc.tensor.matmul(ps[g][:, 0:C], kvl[:, 2 * g + k, :], t1[:, 2 * g + k, :], start=(k == 0), stop=(k == 1))
                last.then_inc(made, 1)
                step += 1
            pe.wait_ge(moved, step - 1)
            for g in range(2):
                nc.tensor.matmul(ps[0][:, 0:C], c("l2o_bias"), cproj[:, g, :], start=(g == 0), stop=False)
            for hg in range(4):
                last = nc.tensor.matmul(ps[0][:, 0:C], c("kvl_bias"), t1[:, hg, :], start=False, stop=(hg == 3))
            last.then_inc(made, 1)

        @block.vector
        def _(dve):
            step = 0
            for w in range(2):
                for g in range(2):
                    dve.wait_ge(made, step + 1)
                    nc.vector.tensor_copy(wlat[:, :, w, :, g, :],
                                          ps[step % 2][:, :].rearrange("p (c e m) -> p c e m", c=CC, e=2)).then_inc(moved, 1)
                    step += 1
            dve.wait_ge(made, step + 1)
            for w, b in enumerate(("q2l_bias", "kv2l_bias")):
                for e in range(2):
                    last = nc.vector.tensor_scalar(blat[:, w, e, :], ps[0][:, (w * 2 + e) * 2:(w * 2 + e) * 2 + 2],
                                                   c(b)[:, e:e + 1], None, ALU.add)
            last.then_inc(moved, 1)
            step += 1
            for hg in range(4):
                dve.wait_ge(made, step + 1)
                nc.vector.tensor_copy(t1[:, hg, :], ps[step % 2][:, 0:C]).then_inc(moved, 1)
                step += 1
            for g in range(2):
                dve.wait_ge(made, step + 1)
                nc.vector.tensor_copy(wout[:, g, :], ps[g][:, 0:C]).then_inc(moved, 1)
                step += 1
            dve.wait_ge(made, step + 1)
            nc.vector.tensor_tensor(cout[:, :], ps[0][:, 0:C], c("cproj_bias"), ALU.add).then_inc(moved, 1)


def latent_projections(nc, t, x, cst, rope, wlat, blat, qk, vs):
    ps_t = [t.psum(f"lp_t{n}", [P, CH]) for n in range(2)]
    ps_pair = [[t.psum(f"lp_pair{n}{e}", [P, CH]) for e in range(2)] for n in range(2)]
    ps_q = [t.psum(f"lp_q{e}", [P, CH]) for e in range(2)]
    xc = t.sbuf("lp_x", [P, 2, NT, C])
    xn = t.sbuf("lp_xn", [P, NT, C])
    xT = t.sbuf("lp_xT", [P, 2, CC, CH])
    stats = t.sbuf("lp_stats", [P, NT, 6])
    mv = t.sbuf("lp_mv", [P, NT, 2])
    std = t.sbuf("lp_std", [P, NT])
    rstd = t.sbuf("lp_rstd", [P, NT])
    prod = t.sbuf("lp_prod", [P, 2, 4, CH])
    rot = t.sbuf("lp_rot", [P, 2, 2, CH])
    out = t.sbuf("lp_out", [P, 4, 2, 2, CH], F32R)
    vt = t.sbuf("lp_v", [P, NT, H, 2 * HD])
    x_in = [t.sem(f"lp_x_in{n}") for n in range(2)]
    stats_done, var_ready, std_ready, rstd_ready = (t.sem("lp_" + n) for n in ("stats_done", "var_ready", "std_ready", "rstd_ready"))
    xn_ready, turned, xT_ready = (t.sem("lp_" + n) for n in ("xn_ready", "turned", "xT_ready"))
    pair_ready, products, rot_ready, q_ready = (t.sem("lp_" + n) for n in ("pair_ready", "products", "rot_ready", "q_ready"))
    hi_ready, lo_ready, v_ready, v_used, zeroed = (t.sem("lp_" + n) for n in ("hi_ready", "lo_ready", "v_ready", "v_used", "zeroed"))
    out_left = [t.sem(f"lp_out_left{r}") for r in range(4)]
    v_left = t.sem("lp_v_left")
    wqk = const(cst, "wqk_blocks").rearrange("p (o i m) -> p o i m", o=2, i=2)
    ident, wqk_bias, eps = const(cst, "ident"), const(cst, "wqk_bias"), const(cst, "eps")
    wv = const(cst, "wv").rearrange("p (c n) -> p c n", c=CC)
    bv = const(cst, "bv").rearrange("p (h d) -> p h d", h=H)
    xt = x.rearrange("b (s j p) c -> (b s) p j c", s=2, p=P)
    chunks = 2 * B

    with nc.Block() as block:
        @block.sync
        def _(sp):
            for half in range(2):
                sp.dma_start(xc[:, half], xt[half]).then_inc(x_in[half], 16)

            def chunk(b, half, more):
                ck = 2 * b + half
                if more:
                    sp.wait_ge(xn_ready, NT * (ck + 1))
                    sp.dma_start(xc[:, half], xt[bass.ds(ck + 2, 1)].rearrange("a p j c -> p (a j) c")).then_inc(x_in[half], 16)
                for r in range(4):
                    w, g = r // 2, r % 2
                    sp.wait_ge(lo_ready, 2 * (4 * ck + r + 1))
                    for hl in range(2):
                        for e in range(2):
                            dst = qk[w][hl][bass.ds(b * H + g * 8, 8), e * HD:(e + 1) * HD, half * CH:(half + 1) * CH]
                            sp.dma_start(dst, out[:, r, hl, e, :].bitcast(F32)).then_inc(out_left[r], 16)
                sp.wait_ge(v_used, NT * (ck + 1))
                for j in range(NT):
                    kb = half * NT + j
                    dst = vs[bass.ds(b * H, H), :, kb * 2 * HD:(kb + 1) * 2 * HD].rearrange("h p e -> p h e")
                    sp.dma_start(dst, vt[:, j]).then_inc(v_left, 16)

            with sp.Fori(0, B - 1) as b:
                for half in range(2):
                    chunk(b, half, True)
            for half in range(2):
                chunk(B - 1, half, False)
            for r in range(4):
                sp.wait_ge(out_left[r], 16 * 4 * chunks)
            sp.wait_ge(v_left, 16 * NT * chunks)

        @block.vector
        def _(dve):
            nc.vector.memset(vt[:, :, :, HD + 1:], 0.0).then_inc(zeroed, 1)
            nc.vector.memset(vt[:, :, :, HD:HD + 1], 1.0).then_inc(zeroed, 1)

            def begin(b, half, first):
                ck = 2 * b + half
                dve.wait_ge(x_in[half], 16 * b + 16)
                for j in range(NT):
                    nc.vector.bn_stats(stats[:, j], xc[:, half, j, :]).then_inc(stats_done, 1)
                dve.wait_ge(stats_done, NT * (ck + 1))
                nc.vector.memset(std[:, :], 0.0)
                for j in range(NT):
                    nc.vector.bn_aggr(mv[:, j], stats[:, j]).then_inc(var_ready, 1)
                dve.wait_ge(std_ready, ck + 1)
                nc.vector.reciprocal(rstd[:, :], std[:, :]).then_inc(rstd_ready, 1)
                dve.wait_ge(rstd_ready, ck + 1)
                if not first:
                    dve.wait_ge(turned, CC * ck)
                for j in range(NT):
                    nc.vector.tensor_scalar(xn[:, j], xc[:, half, j, :], mv[:, j, 0:1], rstd[:, j:j + 1],
                                            ALU.subtract, ALU.mult).then_inc(xn_ready, 1)

            def rotate(ck, half, r):
                w, g, n = r // 2, r % 2, 4 * ck + r
                dve.wait_ge(pair_ready, n + 1)
                cos, sin = (rope[:, k, half * CH:(half + 1) * CH] for k in range(2))
                for k, (e, table) in enumerate(((0, cos), (1, sin), (1, cos), (0, sin))):
                    nc.vector.scalar_tensor_tensor(out=prod[:, r % 2, k], in0=ps_pair[r % 2][e][:, :], scalar=blat[:, w, e, g:g + 1],
                                                   in1=table, op0=ALU.add, op1=ALU.mult).then_inc(products, 1)
                dve.wait_ge(products, 4 * (n + 1))
                nc.vector.tensor_tensor(rot[:, r % 2, 0], prod[:, r % 2, 0], prod[:, r % 2, 1], ALU.subtract).then_inc(rot_ready, 1)
                nc.vector.tensor_tensor(rot[:, r % 2, 1], prod[:, r % 2, 2], prod[:, r % 2, 3], ALU.add).then_inc(rot_ready, 1)

            def low(ck, r):
                w, n = r // 2, 4 * ck + r
                dve.wait_ge(hi_ready, 2 * (n + 1))
                for e in range(2):
                    hi, lo = out[:, r, 0, e, :].bitcast(F32), out[:, r, 1, e, :]
                    if w == 0:
                        nc.vector.scalar_tensor_tensor(out=lo, in0=ps_q[e][:, :], scalar=wqk_bias[:, e:e + 1], in1=hi,
                                                       op0=ALU.add, op1=ALU.subtract).then_inc(lo_ready, 1)
                    else:
                        nc.vector.tensor_tensor(lo, rot[:, r % 2, e], hi, ALU.subtract).then_inc(lo_ready, 1)

            def finish(b, half, first, ahead):
                ck = 2 * b + half
                rotate(ck, half, 0)
                rotate(ck, half, 1)
                low(ck, 0)
                ahead()
                low(ck, 1)
                rotate(ck, half, 2)
                rotate(ck, half, 3)
                low(ck, 2)
                low(ck, 3)
                if first:
                    dve.wait_ge(zeroed, 2)
                else:
                    dve.wait_ge(v_left, 16 * NT * ck)
                for j in range(NT):
                    dve.wait_ge(v_ready, 2 * ck + j // 2 + 1)
                    nc.vector.tensor_tensor(vt[:, j, :, 0:HD], ps_t[j // 2][:, (j % 2) * C:(j % 2 + 1) * C].rearrange("p (h d) -> p h d", h=H),
                                            bv, ALU.add).then_inc(v_used, 1)

            over_chunks_ahead(dve, begin, finish)

        @block.scalar
        def _(act):
            def begin(b, half, first, between=lambda: None):
                ck = 2 * b + half
                act.wait_ge(var_ready, NT * (ck + 1))
                nc.scalar.activation(std[:, :], mv[:, :, 1], ACT.Sqrt, bias=eps).then_inc(std_ready, 1)
                between()
                if beyond_first_batch(b):
                    act.wait_ge(v_ready, 2 * (ck - 1))
                for cc in range(CC):
                    act.wait_ge(turned, CC * ck + cc + 1)
                    nc.scalar.copy(xT[:, half, cc, :], ps_t[cc][:, :]).then_inc(xT_ready, 1)

            def high(ck, r, first):
                w, n = r // 2, 4 * ck + r
                if w == 0:
                    act.wait_ge(q_ready, 2 * ck + r + 1)
                else:
                    act.wait_ge(rot_ready, 2 * (n + 1))
                if not first:
                    act.wait_ge(out_left[r], 64 * ck)
                for e in range(2):
                    if w == 0:
                        ins = nc.scalar.activation(out[:, r, 0, e, :], ps_q[e][:, :], ACT.Identity, bias=wqk_bias[:, e:e + 1])
                    else:
                        ins = nc.scalar.copy(out[:, r, 0, e, :], rot[:, r % 2, e])
                    ins.then_inc(hi_ready, 1)

            def finish(b, half, first, ahead):
                ck = 2 * b + half
                high(ck, 0, first)
                if not ahead(lambda: high(ck, 1, first)):
                    high(ck, 1, first)
                for r in range(2, 4):
                    high(ck, r, first)

            over_chunks_ahead(act, begin, finish)

        @block.tensor
        def _(pe):
            def begin(b, half, first):
                ck = 2 * b + half
                pe.wait_ge(xn_ready, NT * (ck + 1))
                if beyond_first_batch(b):
                    pe.wait_ge(v_used, NT * (ck - 1))
                for cc in range(CC):
                    for j in range(NT):
                        last = nc.tensor.transpose(ps_t[cc][:, j * P:(j + 1) * P], xn[:, j, cc * P:(cc + 1) * P], ident)
                    last.then_inc(turned, 1)

            def finish(b, half, first, ahead):
                ck = 2 * b + half
                pe.wait_ge(xT_ready, CC * (ck + 1))

                def pair(r):
                    w, g, n = r // 2, r % 2, 4 * ck + r
                    if not (first and r < 2):
                        pe.wait_ge(products, 4 * (n - 1))
                    for e in range(2):
                        for cc in range(CC):
                            last = nc.tensor.matmul(ps_pair[r % 2][e][:, :], wlat[:, cc, w, e, g, :], xT[:, half, cc, :],
                                                    start=(cc == 0), stop=(cc == CC - 1))
                    last.then_inc(pair_ready, 1)

                def apply_wqk(r):
                    n = 4 * ck + r
                    pe.wait_ge(rot_ready, 2 * (n + 1))
                    if r == 1:
                        pe.wait_ge(lo_ready, 2 * n)
                    elif not first:
                        pe.wait_ge(lo_ready, 2 * (n - 2))
                    for o in range(2):
                        for e in range(2):
                            last = nc.tensor.matmul(ps_q[o][:, :], wqk[:, o, e, :], rot[:, r % 2, e], start=(e == 0), stop=(e == 1))
                    last.then_inc(q_ready, 1)

                pair(0)
                pair(1)
                apply_wqk(0)
                pair(2)
                apply_wqk(1)
                if ahead():
                    pair(3)
                    pe.wait_ge(xT_ready, CC * (ck + 2))
                else:
                    pair(3)
                    pe.wait_ge(v_used, NT * ck)
                for j in range(NT):
                    for cc in range(CC):
                        last = nc.tensor.matmul(ps_t[j // 2][:, (j % 2) * C:(j % 2 + 1) * C], xT[:, half, cc, j * P:(j + 1) * P], wv[:, cc, :],
                                                start=(cc == 0), stop=(cc == CC - 1))
                    if j % 2:
                        last.then_inc(v_ready, 1)

            over_chunks_ahead(pe, begin, finish)


def between_attentions(nc, t, x, os, cst, wout, cout, x1, n1, qk, vs):
    ps_t = [t.psum(f"mi_t{n}", [P, CH]) for n in range(2)]
    ps_y = [t.psum(f"mi_y{n}", [P, CH]) for n in range(2)]
    ps_p = [t.psum(f"mi_p{n}", [P, CH]) for n in range(4)]
    oc = t.sbuf("mi_o", [P, 2, NT, C])
    xc = t.sbuf("mi_x", [P, 2, NT, C])
    oT = t.sbuf("mi_oT", [P, CC, CH])
    nT = t.sbuf("mi_nT", [P, CC, CH])
    y = t.sbuf("mi_y", [P, NT, C])
    yn = t.sbuf("mi_yn", [P, NT, C])
    x1c = t.sbuf("mi_x1", [P, NT, C])
    n1c = t.sbuf("mi_n1", [P, NT, C])
    stats = t.sbuf("mi_stats", [P, 2, NT, 6])
    mv = t.sbuf("mi_mv", [P, 2, NT, 2])
    std = t.sbuf("mi_std", [P, 2, NT])
    rstd = t.sbuf("mi_rstd", [P, 2, NT])
    out = t.sbuf("mi_out", [P, 4, 2, CH], F32R)
    vt = t.sbuf("mi_v", [P, NT, H, 2 * HD])
    names = ("turned", "oT_ready", "y_ready", "y_used", "nT_ready", "n_turned", "p_ready", "hi_ready", "lo_ready", "v_ready", "v_used",
             "yn_ready", "x1_ready", "n1_ready", "zeroed")
    turned, oT_ready, y_ready, y_used, nT_ready, n_turned, p_ready, hi_ready, lo_ready, v_ready, v_used, yn_ready, x1_ready, \
        n1_ready, zeroed = (t.sem("mi_" + n) for n in names)
    stats_done, var_ready, std_ready, rstd_ready = ([t.sem(f"mi_{n}{k}") for k in range(2)] for n in ("stats", "var", "std", "rstd"))
    o_in, x_in = ([t.sem(f"mi_{n}_in{k}") for k in range(2)] for n in "ox")
    out_left = [t.sem(f"mi_out_left{r}") for r in range(4)]
    v_left, x1_left, n1_left = (t.sem(f"mi_{n}_left") for n in ("v", "x1", "n1"))
    ident, eps = const(cst, "ident"), const(cst, "eps")
    wqkv = const(cst, "wqkv2").rearrange("p (c n) -> p c n", c=CC)
    tiles = lambda a: a.rearrange("b (s j p) c -> (b s) p j c", s=2, p=P)
    xt = tiles(x)
    x1t = tiles(x1)
    n1t = tiles(n1)
    chunks = 2 * B
    HG = H // 4

    with nc.Block() as block:
        @block.sync
        def _(sp):
            def load(b, half):
                for hg in range(HG):
                    sp.dma_start(oc[:, half, :, hg * 4 * HD:(hg + 1) * 4 * HD],
                                 os[bass.ds(2 * (b * HG + hg) + half, 1)].rearrange("a p q d -> p (a q) d")).then_inc(o_in[half], 16)
                sp.dma_start(xc[:, half], xt[bass.ds(2 * b + half, 1)].rearrange("a p j c -> p (a j) c")).then_inc(x_in[half], 16)

            for half in range(2):
                load(0, half)

            def chunk(b, half, more):
                ck = 2 * b + half
                sp.wait_ge(x1_ready, ck + 1)
                if more:
                    load(b + 1, half)
                sp.dma_start(x1t[bass.ds(ck, 1)].rearrange("a p j c -> p (a j) c"), x1c[:, :, :]).then_inc(x1_left, 16)
                sp.wait_ge(n1_ready, NT * (ck + 1))
                sp.dma_start(n1t[bass.ds(ck, 1)].rearrange("a p j c -> p (a j) c"), n1c[:, :, :]).then_inc(n1_left, 16)
                for r in range(4):
                    w, g = r // 2, r % 2
                    sp.wait_ge(lo_ready, 4 * ck + r + 1)
                    for hl in range(2):
                        dst = qk[w][hl][bass.ds(b * H + g * 8, 8), 0:HD, half * CH:(half + 1) * CH]
                        sp.dma_start(dst, out[:, r, hl, :].bitcast(F32)).then_inc(out_left[r], 16)
                sp.wait_ge(v_used, 2 * (ck + 1))
                for j in range(NT):
                    kb = half * NT + j
                    dst = vs[bass.ds(b * H, H), :, kb * 2 * HD:(kb + 1) * 2 * HD].rearrange("h p e -> p h e")
                    sp.dma_start(dst, vt[:, j]).then_inc(v_left, 16)

            with sp.Fori(0, B - 1) as b:
                for half in range(2):
                    chunk(b, half, True)
            for half in range(2):
                chunk(B - 1, half, False)
            for r in range(4):
                sp.wait_ge(out_left[r], 16 * 2 * chunks)
            sp.wait_ge(v_left, 16 * NT * chunks)
            sp.wait_ge(x1_left, 16 * chunks)
            sp.wait_ge(n1_left, 16 * chunks)

        @block.vector
        def _(dve):
            nc.vector.memset(vt[:, :, :, HD + 1:], 0.0).then_inc(zeroed, 1)
            nc.vector.memset(vt[:, :, :, HD:HD + 1], 1.0).then_inc(zeroed, 1)

            def norm(ck, k, src, dst, ready):
                for j in range(NT):
                    nc.vector.bn_stats(stats[:, k, j], src[:, j, :]).then_inc(stats_done[k], 1)
                dve.wait_ge(stats_done[k], NT * (ck + 1))
                nc.vector.memset(std[:, k, :], 0.0)
                for j in range(NT):
                    nc.vector.bn_aggr(mv[:, k, j], stats[:, k, j]).then_inc(var_ready[k], 1)
                dve.wait_ge(std_ready[k], ck + 1)
                nc.vector.reciprocal(rstd[:, k, :], std[:, k, :]).then_inc(rstd_ready[k], 1)
                dve.wait_ge(rstd_ready[k], ck + 1)
                for j in range(NT):
                    nc.vector.tensor_scalar(dst[:, j], src[:, j], mv[:, k, j, 0:1], rstd[:, k, j:j + 1], ALU.subtract, ALU.mult).then_inc(ready, 1)

            def begin(b, half, first):
                ck = 2 * b + half
                for k in range(2):
                    dve.wait_ge(y_ready, 2 * ck + k + 1)
                    nc.vector.tensor_tensor(y[:, 2 * k:2 * k + 2], ps_y[k][:, :].rearrange("p (j n) -> p j n", j=2),
                                            cout[:, :].unsqueeze(1).to_broadcast([P, 2, C]), ALU.add).then_inc(y_used, 1)
                dve.wait_ge(y_used, 2 * (ck + 1))
                norm(ck, 0, y, yn, yn_ready)
                dve.wait_ge(yn_ready, NT * (ck + 1))
                dve.wait_ge(x_in[half], 16 * (b + 1))
                if not first:
                    dve.wait_ge(x1_left, 16 * ck)
                nc.vector.tensor_tensor(x1c[:, :, :], xc[:, half], yn[:, :, :], ALU.add).then_inc(x1_ready, 1)
                dve.wait_ge(x1_ready, ck + 1)
                if not first:
                    dve.wait_ge(n1_left, 16 * ck)
                norm(ck, 1, x1c, n1c, n1_ready)

            def finish(b, half, first, ahead):
                ck = 2 * b + half
                ahead()
                for r in range(4):
                    n = 4 * ck + r
                    dve.wait_ge(hi_ready, n + 1)
                    nc.vector.tensor_tensor(out[:, r, 1, :], ps_p[r][:, :], out[:, r, 0, :].bitcast(F32), ALU.subtract).then_inc(lo_ready, 1)
                if first:
                    dve.wait_ge(zeroed, 2)
                else:
                    dve.wait_ge(v_left, 16 * NT * ck)
                for k in range(2):
                    dve.wait_ge(v_ready, 2 * ck + k + 1)
                    nc.vector.tensor_copy(vt[:, 2 * k:2 * k + 2, :, 0:HD],
                                          ps_y[k][:, :].rearrange("p (j h d) -> p j h d", j=2, h=H)).then_inc(v_used, 1)

            over_chunks_ahead(dve, begin, finish)

        @block.scalar
        def _(act):
            def deviation(ck, k):
                act.wait_ge(var_ready[k], NT * (ck + 1))
                nc.scalar.activation(std[:, k, :], mv[:, k, :, 1], ACT.Sqrt, bias=eps).then_inc(std_ready[k], 1)

            def take_transposed(ck, src_turned, dst, done):
                for cc in range(CC):
                    act.wait_ge(src_turned, CC * ck + cc + 1)
                    nc.scalar.copy(dst[:, cc, :], ps_t[cc][:, :]).then_inc(done, 1)

            def high(ck, r, first):
                act.wait_ge(p_ready, 4 * ck + r + 1)
                if not first:
                    act.wait_ge(out_left[r], 32 * ck)
                nc.scalar.copy(out[:, r, 0, :], ps_p[r][:, :]).then_inc(hi_ready, 1)

            def begin(ck, before):
                take_transposed(ck, turned, oT, oT_ready)
                deviation(ck, 0)
                for r in range(2):
                    before(r)
                deviation(ck, 1)
                for r in range(2, 4):
                    before(r)
                take_transposed(ck, n_turned, nT, nT_ready)

            begin(0, lambda r: None)
            begin(1, lambda r: high(0, r, True))
            begin(2, lambda r: high(1, r, False))
            with act.Fori(1, B - 1) as b:
                for half in range(2):
                    begin(2 * b + half + 1, lambda r: high(2 * b + half, r, False))
            begin(2 * B - 1, lambda r: high(2 * B - 2, r, False))
            for r in range(4):
                high(2 * B - 1, r, False)

        @block.tensor
        def _(pe):
            def turn(src, done):
                for cc in range(CC):
                    for j in range(NT):
                        last = nc.tensor.transpose(ps_t[cc][:, j * P:(j + 1) * P], src[:, j, cc * P:(cc + 1) * P], ident)
                    last.then_inc(done, 1)

            def begin(b, half, first):
                ck = 2 * b + half
                pe.wait_ge(o_in[half], 16 * HG * (b + 1))
                if not first:
                    pe.wait_ge(nT_ready, CC * ck)
                turn(oc[:, half], turned)
                pe.wait_ge(oT_ready, CC * (ck + 1))
                if beyond_first_batch(b):
                    pe.wait_ge(v_used, 2 * (ck - 1))
                for j in range(NT):
                    for cc in range(CC):
                        last = nc.tensor.matmul(ps_y[j // 2][:, (j % 2) * C:(j % 2 + 1) * C], oT[:, cc, j * P:(j + 1) * P], wout[:, cc, :],
                                                start=(cc == 0), stop=(cc == CC - 1))
                    if j % 2:
                        last.then_inc(y_ready, 1)

            def turn_n1(ck):
                pe.wait_ge(n1_ready, NT * (ck + 1))
                turn(n1c, n_turned)

            def finish(b, half, first, ahead):
                ck = 2 * b + half
                if first:
                    turn_n1(0)
                pe.wait_ge(nT_ready, CC * (ck + 1))
                more = ahead()
                for r in range(4):
                    if not first:
                        pe.wait_ge(lo_ready, 4 * (ck - 1) + r + 1)
                    for cc in range(CC):
                        last = nc.tensor.matmul(ps_p[r][:, :], wqkv[:, cc, r * P:(r + 1) * P], nT[:, cc, :], start=(cc == 0), stop=(cc == CC - 1))
                    last.then_inc(p_ready, 1)
                if more:
                    pe.wait_ge(y_used, 2 * (ck + 2))
                else:
                    pe.wait_ge(v_used, 2 * ck)
                for j in range(NT):
                    for cc in range(CC):
                        last = nc.tensor.matmul(ps_y[j // 2][:, (j % 2) * C:(j % 2 + 1) * C], nT[:, cc, j * P:(j + 1) * P], wqkv[:, cc, 2 * C:],
                                                start=(cc == 0), stop=(cc == CC - 1))
                    if j % 2:
                        last.then_inc(v_ready, 1)
                if more:
                    turn_n1(ck + 1)

            over_chunks_ahead(pe, begin, finish)


def after_attentions(nc, t, n1, os, cst, h, logits, xs):
    ps_t = [t.psum(f"af_t{n}", [P, CH]) for n in range(2)]
    ps_y = [t.psum(f"af_y{n}", [P, CH]) for n in range(2)]
    ps_l = t.psum("af_l", [P, NT, E])
    oc = t.sbuf("af_o", [P, 2, NT, C])
    nc1 = t.sbuf("af_n", [P, 2, NT, C])
    oT = t.sbuf("af_oT", [P, CC, CH])
    hT = t.sbuf("af_hT", [P, CC, CH])
    y = t.sbuf("af_y", [P, NT, C])
    yn = t.sbuf("af_yn", [P, NT, C])
    yg = t.sbuf("af_yg", [P, NT, C])
    hc = t.sbuf("af_h", [P, 2, NT, C])
    stats = t.sbuf("af_stats", [P, NT, 6])
    mv = t.sbuf("af_mv", [P, NT, 2])
    std = t.sbuf("af_std", [P, NT])
    rstd = t.sbuf("af_rstd", [P, NT])
    names = ("turned", "oT_ready", "y_ready", "y_used", "stats_done", "var_ready", "std_ready", "rstd_ready", "yn_ready", "yg_ready",
             "h_ready", "h_turned", "hT_ready", "l_ready", "l_used")
    turned, oT_ready, y_ready, y_used, stats_done, var_ready, std_ready, rstd_ready, yn_ready, yg_ready, h_ready, h_turned, hT_ready, \
        l_ready, l_used = (t.sem("af_" + n) for n in names)
    o_in, n_in, h_left = ([t.sem(f"af_{n}{k}") for k in range(2)] for n in ("o_in", "n_in", "h_left"))
    ident, eps = const(cst, "ident"), const(cst, "eps")
    wo = const(cst, "wo2").rearrange("p (c n) -> p c n", c=CC)
    wg = const(cst, "wg").rearrange("p (c n) -> p c n", c=CC)
    n1t = n1.rearrange("b (s j p) c -> (b s) p j c", s=2, p=P)
    ht = h.rearrange("b (s j p) c -> (b s) p j c", s=2, p=P)
    HG = H // 4
    FILLS = 8
    zeros = t.sbuf("af_zeros", [P, TILES * C // FILLS])
    zeroed, filled = t.sem("af_zeroed"), t.sem("af_filled")
    over_tiles = lambda a: a.unsqueeze(1).to_broadcast([P, NT, C])

    with nc.Block() as block:
        @block.gpsimd
        def _(pool):
            nc.gpsimd.memset(zeros[:, :], 0.0).then_inc(zeroed, 1)
            pool.wait_ge(zeroed, 1)
            for n in range(FILLS):
                pool.dma_start(xs.rearrange("(n p r) c -> n p (r c)", n=FILLS, p=P)[n], zeros[:, :]).then_inc(filled, 16)
            pool.wait_ge(filled, 16 * FILLS)

        @block.sync
        def _(sp):
            def load(b, half):
                for hg in range(HG):
                    sp.dma_start(oc[:, half, :, hg * 4 * HD:(hg + 1) * 4 * HD],
                                 os[bass.ds(2 * (b * HG + hg) + half, 1)].rearrange("a p q d -> p (a q) d")).then_inc(o_in[half], 16)
                sp.dma_start(nc1[:, half], n1t[bass.ds(2 * b + half, 1)].rearrange("a p j c -> p (a j) c")).then_inc(n_in[half], 16)

            for half in range(2):
                load(0, half)

            def chunk(b, half, more):
                ck = 2 * b + half
                sp.wait_ge(h_ready, ck + 1)
                if more:
                    load(b + 1, half)
                sp.dma_start(ht[bass.ds(ck, 1)].rearrange("a p j c -> p (a j) c"), hc[:, half]).then_inc(h_left[half], 16)

            with sp.Fori(0, B - 1) as b:
                for half in range(2):
                    chunk(b, half, True)
            for half in range(2):
                chunk(B - 1, half, False)
                sp.wait_ge(h_left[half], 16 * B)

        @block.vector
        def _(dve):
            def begin(b, half, first):
                ck = 2 * b + half
                dve.wait_ge(n_in[half], 16 * (b + 1))
                for k in range(2):
                    dve.wait_ge(y_ready, 2 * ck + k + 1)
                    nc.vector.tensor_tensor(y[:, 2 * k:2 * k + 2], ps_y[k][:, :].rearrange("p (j n) -> p j n", j=2),
                                            nc1[:, half, 2 * k:2 * k + 2], ALU.add).then_inc(y_used, 1)
                dve.wait_ge(y_used, 2 * (ck + 1))
                for j in range(NT):
                    nc.vector.bn_stats(stats[:, j], y[:, j, :]).then_inc(stats_done, 1)
                dve.wait_ge(stats_done, NT * (ck + 1))
                nc.vector.memset(std[:, :], 0.0)
                for j in range(NT):
                    nc.vector.bn_aggr(mv[:, j], stats[:, j]).then_inc(var_ready, 1)
                dve.wait_ge(std_ready, ck + 1)
                nc.vector.reciprocal(rstd[:, :], std[:, :]).then_inc(rstd_ready, 1)
                dve.wait_ge(rstd_ready, ck + 1)
                for j in range(NT):
                    nc.vector.tensor_scalar(yn[:, j], y[:, j], mv[:, j, 0:1], rstd[:, j:j + 1], ALU.subtract, ALU.mult).then_inc(yn_ready, 1)
                dve.wait_ge(yn_ready, NT * (ck + 1))
                nc.vector.tensor_tensor(yg[:, :, :], yn[:, :, :], over_tiles(const(cst, "g1")), ALU.mult).then_inc(yg_ready, 1)
                dve.wait_ge(yg_ready, ck + 1)
                if beyond_first_batch(b):
                    dve.wait_ge(h_left[half], 16 * b)
                nc.vector.tensor_tensor(hc[:, half], yg[:, :, :], over_tiles(const(cst, "b1")), ALU.add).then_inc(h_ready, 1)

            def finish(b, half, first, ahead):
                ck = 2 * b + half
                ahead()
                dve.wait_ge(l_ready, ck + 1)
                nc.vector.tensor_copy(logits[:, bass.ds(ck * NT, NT), :], ps_l[:, :, :]).then_inc(l_used, 1)

            over_chunks_ahead(dve, begin, finish)

        @block.scalar
        def _(act):
            def take_transposed(ck, src_turned, dst, done):
                for cc in range(CC):
                    act.wait_ge(src_turned, CC * ck + cc + 1)
                    nc.scalar.copy(dst[:, cc, :], ps_t[cc][:, :]).then_inc(done, 1)

            def deviation(ck):
                act.wait_ge(var_ready, NT * (ck + 1))
                nc.scalar.activation(std[:, :], mv[:, :, 1], ACT.Sqrt, bias=eps).then_inc(std_ready, 1)

            def step(ck):
                take_transposed(ck + 1, turned, oT, oT_ready)
                take_transposed(ck, h_turned, hT, hT_ready)
                deviation(ck + 1)

            take_transposed(0, turned, oT, oT_ready)
            deviation(0)
            step(0)
            with act.Fori(1, 2 * B - 1) as ck:
                step(ck)
            take_transposed(2 * B - 1, h_turned, hT, hT_ready)

        @block.tensor
        def _(pe):
            def begin(b, half, first):
                ck = 2 * b + half
                pe.wait_ge(o_in[half], 16 * HG * (b + 1))
                if beyond_first_batch(b):
                    pe.wait_ge(hT_ready, CC * (ck - 1))
                for cc in range(CC):
                    for j in range(NT):
                        last = nc.tensor.transpose(ps_t[cc][:, j * P:(j + 1) * P], oc[:, half, j, cc * P:(cc + 1) * P], ident)
                    last.then_inc(turned, 1)
                pe.wait_ge(oT_ready, CC * (ck + 1))
                if not first:
                    pe.wait_ge(y_used, 2 * ck)
                for j in range(NT):
                    for cc in range(CC):
                        last = nc.tensor.matmul(ps_y[j // 2][:, (j % 2) * C:(j % 2 + 1) * C], oT[:, cc, j * P:(j + 1) * P], wo[:, cc, :],
                                                start=(cc == 0), stop=(cc == CC - 1))
                    if j % 2:
                        last.then_inc(y_ready, 1)

            def finish(b, half, first, ahead):
                ck = 2 * b + half
                ahead()
                pe.wait_ge(h_ready, ck + 1)
                for cc in range(CC):
                    for j in range(NT):
                        last = nc.tensor.transpose(ps_t[cc][:, j * P:(j + 1) * P], hc[:, half, j, cc * P:(cc + 1) * P], ident)
                    last.then_inc(h_turned, 1)
                pe.wait_ge(hT_ready, CC * (ck + 1))
                if not first:
                    pe.wait_ge(l_used, ck)
                for j in range(NT):
                    for cc in range(CC):
                        last = nc.tensor.matmul(ps_l[:, j, :], hT[:, cc, j * P:(j + 1) * P], wg[:, cc, :], start=(cc == 0), stop=(cc == CC - 1))
                last.then_inc(l_ready, 1)

            over_chunks_ahead(pe, begin, finish)


def route(nc, t, cst, logits, weight, place, tile_expert):
    ps = t.psum("ro_ps", [P, 2, TT, E])
    top = t.sbuf("ro_top", [P, TT, 8])
    index = t.sbuf("ro_index", [P, TT, 8], U32)
    chosen = t.sbuf("ro_chosen", [P, TT, 2])
    onehot = t.sbuf("ro_onehot", [P, TT, 2, E])
    count = t.sbuf("ro_count", [P, TT, E])
    scan = [t.sbuf(f"ro_scan{n}", [P, TT, E]) for n in range(2)]
    loc = t.sbuf("ro_loc", [P, TT, E])
    rows = t.sbuf("ro_rows", [P, TT, 2, E])
    placef = t.sbuf("ro_placef", [P, TT, 2])
    gap = t.sbuf("ro_gap", [P, TT])
    egap = t.sbuf("ro_egap", [P, TT])
    denom = t.sbuf("ro_denom", [P, TT])
    total = t.sbuf("ro_total", [P, E])
    tiles_i = t.sbuf("ro_tiles_i", [P, E], mybir.dt.int32)
    shifted = t.sbuf("ro_shifted", [P, E], mybir.dt.int32)
    tiles = t.sbuf("ro_tiles", [P, E])
    ends = t.sbuf("ro_ends", [P, E + 1])
    passed = t.sbuf("ro_passed", [P, TILES, E])
    expf = t.sbuf("ro_expf", [P, TILES])
    step, gap_ready, egap_ready, counted, ranked = (
        t.sem("ro_" + n) for n in ("step", "gap_ready", "egap_ready", "counted", "ranked"))

    with nc.Block() as block:
        @block.scalar
        def _(act):
            act.wait_ge(gap_ready, 1)
            nc.scalar.activation(egap[:, :], gap[:, :], ACT.Exp).then_inc(egap_ready, 1)

        @block.tensor
        def _(pe):
            pe.wait_ge(counted, 1)
            flat = count[:, :, :].rearrange("p t e -> p (t e)")
            nc.tensor.matmul(ps[:, 0].rearrange("p t e -> p (t e)"), const(cst, "before"), flat, start=True, stop=True)
            nc.tensor.matmul(ps[:, 1].rearrange("p t e -> p (t e)"), const(cst, "ones"), flat, start=True, stop=True).then_inc(ranked, 1)

        @block.vector
        def _(dve):
            done = 0

            def link(ins):
                nonlocal done
                done += 1
                ins.then_inc(step, 1)
                dve.wait_ge(step, done)

            for k in range(TT):
                last = nc.vector.max(top[:, k], logits[:, k])
            link(last)
            for k in range(TT):
                last = nc.vector.max_index(index[:, k], top[:, k], logits[:, k])
            link(last)
            nc.vector.tensor_tensor(gap[:, :], top[:, :, 1], top[:, :, 0], ALU.subtract).then_inc(gap_ready, 1)
            link(nc.vector.tensor_copy(chosen[:, :, :], index[:, :, 0:2]))
            wide = lambda a: a.unsqueeze(3).to_broadcast([P, TT, 2, E])
            experts = const(cst, "expert").unsqueeze(1).to_broadcast([P, TT, E])
            for s in range(2):
                last = nc.vector.tensor_tensor(onehot[:, :, s], chosen[:, :, s].unsqueeze(2).to_broadcast([P, TT, E]), experts, ALU.is_equal)
            link(last)
            nc.vector.tensor_tensor(count[:, :, :], onehot[:, :, 0], onehot[:, :, 1], ALU.add).then_inc(counted, 1)
            dve.wait_ge(egap_ready, 1)
            link(nc.vector.tensor_scalar(denom[:, :], egap[:, :], 1.0, None, ALU.add))
            link(nc.vector.reciprocal(weight[:, :, 0], denom[:, :]))
            link(nc.vector.tensor_tensor(weight[:, :, 1], weight[:, :, 0], egap[:, :], ALU.mult))
            dve.wait_ge(ranked, 1)
            link(nc.vector.tensor_copy(scan[0][:, :, :], ps[:, 1]))
            at, k = 0, 1
            while k < TT:
                nc.vector.tensor_copy(scan[1 - at][:, 0:k], scan[at][:, 0:k])
                link(nc.vector.tensor_tensor(scan[1 - at][:, k:], scan[at][:, k:], scan[at][:, 0:TT - k], ALU.add))
                at, k = 1 - at, 2 * k
            upto = scan[at]
            link(nc.vector.tensor_scalar(total[:, :], upto[:, TT - 1], float(P - 1), None, ALU.add))
            link(nc.vector.tensor_copy(tiles_i[:, :], total[:, :]))
            link(nc.vector.tensor_single_scalar(shifted[:, :], tiles_i[:, :], 7, ALU.logical_shift_right))
            link(nc.vector.tensor_copy(tiles[:, :], shifted[:, :]))
            link(nc.vector.memset(ends[:, 0:1], 0.0))
            for e in range(E):
                link(nc.vector.tensor_tensor(ends[:, e + 1:e + 2], ends[:, e:e + 1], tiles[:, e:e + 1], ALU.add))
            link(nc.vector.tensor_tensor(loc[:, :, :], upto[:, :, :], ps[:, 1], ALU.subtract))
            link(nc.vector.tensor_tensor(loc[:, :, :], loc[:, :, :], ps[:, 0], ALU.add))
            link(nc.vector.scalar_tensor_tensor(out=loc[:, :, :], in0=ends[:, 0:E].unsqueeze(1).to_broadcast([P, TT, E]), scalar=float(P),
                                                in1=loc[:, :, :], op0=ALU.mult, op1=ALU.add))
            for s in range(2):
                last = nc.vector.tensor_tensor(rows[:, :, s], onehot[:, :, s], loc[:, :, :], ALU.mult)
            link(last)
            link(nc.vector.tensor_reduce(placef[:, :, :], rows[:, :, :, :], AX.X, ALU.add))
            link(nc.vector.tensor_copy(place[:, :, :], placef[:, :, :].rearrange("p t s -> p s t")))
            link(nc.vector.tensor_tensor(passed[:, :, :], ends[:, 1:E + 1].unsqueeze(1).to_broadcast([P, TILES, E]),
                                         const(cst, "tile").unsqueeze(2).to_broadcast([P, TILES, E]), ALU.is_le))
            link(nc.vector.tensor_reduce(expf[:, :], passed[:, :, :], AX.X, ALU.add))
            link(nc.vector.tensor_scalar(expf[:, :], expf[:, :], float(E - 1), None, ALU.min))
            pairs = expf[:, :].rearrange("p (k two) -> p k two", two=2)
            nc.vector.tensor_copy(tile_expert[:, :, 0:2], pairs)
            nc.vector.tensor_copy(tile_expert[:, 0:TILES // 2 - 1, 2:4], pairs[:, 1:, :])
            nc.vector.memset(tile_expert[:, TILES // 2 - 1:, 2:4], 0)


def scatter_and_split(nc, t, h, place, xs, w1, w2, w1s, w2s, bb_dram, bb):
    RINGS = 4
    FC = F // P
    ht = h.rearrange("b (k p) c -> (b k) p c", p=P)
    rows = [t.sbuf(f"sc_rows{n}", [P, C]) for n in range(RINGS)]
    h_in, scattered = ([t.sem(f"sc_{n}{k}") for k in range(RINGS)] for n in ("h_in", "scattered"))
    stage = [[t.sbuf(f"sw_{w}{n}", [P, CC * F]) for n in range(2)] for w in range(2)]
    w_in = [[t.sem(f"sw_in{w}{n}") for n in range(2)] for w in range(2)]
    hi, lo, bb_in = t.sem("sw_hi"), t.sem("sw_lo"), t.sem("sw_bb_in")
    src = [w1.rearrange("e (c p) f -> e p c f", p=P), w2.rearrange("e (c p) n -> e p c n", p=P)]
    views = [lambda a: a.rearrange("p (c f) -> p c f", c=CC), lambda a: a.rearrange("p (c n) -> p c n", c=FC)]
    with nc.Block() as block:
        @block.sync
        def _(sp):
            for k in range(TT):
                if k >= RINGS:
                    sp.wait_ge(scattered[k % RINGS], 32 * (k // RINGS))
                sp.dma_start(rows[k % RINGS][:, :], ht[k]).then_inc(h_in[k % RINGS], 16)
                if k % 2 == 0:
                    e, w = divmod(k // 2, 2)
                    if e >= 2:
                        sp.wait_ge(lo, 2 * (e - 2) + w + 1)
                    sp.dma_start(views[w](stage[w][e % 2][:, :]), src[w][e]).then_inc(w_in[w][e % 2], 16)
            for dst, src_bb in zip(bb, bb_dram):
                sp.dma_start(dst[:, :, :], src_bb).then_inc(bb_in, 16)
            sp.wait_ge(bb_in, 32)

        @block.gpsimd
        def _(pool):
            for k in range(TT):
                pool.wait_ge(h_in[k % RINGS], 16 * (k // RINGS + 1))
                for s in range(2):
                    nc.gpsimd.indirect_dma_start(xs, bass.IndirectOffsetOnAxis(place[:, s, k:k + 1], 0), rows[k % RINGS][:, :], None).then_inc(
                        scattered[k % RINGS], 16)
            for n in range(RINGS):
                pool.wait_ge(scattered[n], 32 * TT // RINGS)

        @block.scalar
        def _(act):
            for e in range(E):
                for w, pair in enumerate((w1s, w2s)):
                    act.wait_ge(w_in[w][e % 2], 16 * (e // 2 + 1))
                    nc.scalar.copy(pair[0][:, e].rearrange("p a b -> p (a b)"), stage[w][e % 2][:, :]).then_inc(hi, 1)

        @block.vector
        def _(dve):
            for e in range(E):
                for w, pair in enumerate((w1s, w2s)):
                    dve.wait_ge(hi, 2 * e + w + 1)
                    nc.vector.tensor_tensor(pair[1][:, e].rearrange("p a b -> p (a b)"), stage[w][e % 2][:, :],
                                            pair[0][:, e].rearrange("p a b -> p (a b)"), ALU.subtract).then_inc(lo, 1)


def experts(nc, t, cst, xs, ys, tile_expert, bb, w1s, w2s):
    FC = F // P
    HALF = FC // 2
    ps_x = t.psum("ex_x", [P, CC, P])
    ps_h = [[t.psum(f"ex_h{n}{k}", [P, HALF, P]) for k in range(2)] for n in range(2)]
    ps_y = [t.psum(f"ex_y{n}", [P, C]) for n in range(2)]
    xc = t.sbuf("ex_xc", [P, 2, C])
    xh = t.sbuf("ex_xh", [P, 2, CC, P], FP16)
    xl = t.sbuf("ex_xl", [P, 2, CC, P], BF16)
    act_f = t.sbuf("ex_gelu", [P, 2, FC, P])
    ah = t.sbuf("ex_ah", [P, 2, FC, P], FP16)
    al = t.sbuf("ex_al", [P, 2, FC, P], BF16)
    yc = t.sbuf("ex_yc", [P, 2, C])
    bb1, bb2 = bb
    ident = const(cst, "ident")
    x_in, y_left = ([t.sem(f"ex_{n}{k}") for k in range(2)] for n in ("x_in", "y_left"))
    turned, xh_ready, xl_ready, h_ready, gelu_ready, ah_ready, al_ready, y_ready, y_used = (
        t.sem("ex_" + n) for n in ("turned", "xh_ready", "xl_ready", "h_ready", "gelu_ready", "ah_ready", "al_ready", "y_ready", "y_used"))
    xst = xs.rearrange("(i p) c -> i p c", p=P)
    yst = ys.rearrange("(i p) c -> i p c", p=P)
    row = lambda a: a.rearrange("a p c -> p (a c)")
    PAIRS = TILES // 2

    def over_pairs(eng, step):
        for par in range(2):
            step(0, par, par == 0)
        with eng.Fori(1, PAIRS) as k:
            for par in range(2):
                step(k, par, False)

    def experts_of(eng, k):
        _, values = nc.values_load_multi_w_load_instructions(
            tile_expert[0:1, k, :] if isinstance(k, int) else tile_expert[0:1, bass.ds(k, 1), :].rearrange("p a e -> p (a e)"),
            engines=[eng.engine], min_val=0, max_val=E - 1, skip_runtime_bounds_check_because="route clamps them")
        return values

    with nc.Block() as block:
        @block.sync
        def _(sp):
            for par in range(2):
                sp.dma_start(xc[:, par], xst[par]).then_inc(x_in[par], 16)

            def load(k, par):
                sp.wait_ge(turned, 2 * k + par + 1)
                sp.dma_start(xc[:, par], row(xst[bass.ds(2 * (k + 1) + par, 1)])).then_inc(x_in[par], 16)

            def store(k, par):
                sp.wait_ge(y_used, 2 * k + par + 1)
                sp.dma_start(row(yst[bass.ds(2 * k + par, 1)]), yc[:, par]).then_inc(y_left[par], 16)

            for par in range(2):
                load(0, par)
            with sp.Fori(1, PAIRS - 1) as k:
                for par in range(2):
                    load(k, par)
                    store(k - 1, par)
            for k in range(PAIRS - 2, PAIRS):
                for par in range(2):
                    store(k, par)
            for par in range(2):
                sp.wait_ge(y_left[par], 16 * PAIRS)

        @block.tensor
        def _(pe):
            def turn(k, par, first):
                i = 2 * k + par
                pe.wait_ge(x_in[par], 16 * (k + 1))
                if not first:
                    pe.wait_ge(xl_ready, i)
                for cc in range(CC):
                    last = nc.tensor.transpose(ps_x[:, cc, :], xc[:, par, cc * P:(cc + 1) * P], ident)
                last.then_inc(turned, 1)

            def first_product(k, par, e, first):
                i = 2 * k + par
                pe.wait_ge(xl_ready, i + 1)
                for half in range(2):
                    if not first:
                        pe.wait_ge(gelu_ready, FC * (i - 2) + HALF * (half + 1))
                    for f in range(HALF):
                        fc = half * HALF + f
                        terms = [(w, a, cc) for cc in range(CC) for w, a in ((0, xh), (0, xl), (1, xh))]
                        for n, (w, a, cc) in enumerate(terms):
                            last = nc.tensor.matmul(ps_h[par][half][:, f, :],
                                                    w1s[w][:, bass.ds(e, 1), cc, fc * P:(fc + 1) * P].rearrange("p a f -> p (a f)"),
                                                    a[:, par, cc, :], start=(n == 0), stop=(n == len(terms) - 1))
                    last.then_inc(h_ready, 1)

            def second_product(k, par, e, first):
                i = 2 * k + par
                if not first:
                    pe.wait_ge(y_used, i - 1)
                for half in range(2):
                    pe.wait_ge(al_ready, 2 * i + half + 1)
                    for f in range(HALF):
                        fc = half * HALF + f
                        for n, (w, a) in enumerate(((0, ah), (0, al), (1, ah))):
                            last = nc.tensor.matmul(ps_y[par][:, :], a[:, par, fc, :],
                                                    w2s[w][:, bass.ds(e, 1), fc, :].rearrange("p a n -> p (a n)"),
                                                    start=(fc == 0 and n == 0), stop=(fc == FC - 1 and n == 2))
                last.then_inc(y_ready, 1)

            e = experts_of(pe, 0)
            turn(0, 0, True)
            turn(0, 1, False)
            first_product(0, 0, e[0], True)
            turn(1, 0, False)
            first_product(0, 1, e[1], True)
            second_product(0, 0, e[0], True)
            turn(1, 1, False)
            first_product(1, 0, e[2], False)
            second_product(0, 1, e[1], True)
            with pe.Fori(1, PAIRS - 1) as k:
                e = experts_of(pe, k)
                turn(k + 1, 0, False)
                first_product(k, 1, e[1], False)
                second_product(k, 0, e[0], False)
                turn(k + 1, 1, False)
                first_product(k + 1, 0, e[2], False)
                second_product(k, 1, e[1], False)
            e = experts_of(pe, PAIRS - 1)
            first_product(PAIRS - 1, 1, e[1], False)
            second_product(PAIRS - 1, 0, e[0], False)
            second_product(PAIRS - 1, 1, e[1], False)

        @block.scalar
        def _(act):
            def step(k, par, first):
                i = 2 * k + par
                act.wait_ge(turned, i + 1)
                if not (isinstance(k, int) and k == 0):
                    act.wait_ge(h_ready, 2 * (i - 1))
                nc.scalar.copy(xh[:, par], ps_x[:, :, :]).then_inc(xh_ready, 1)

            def gelu(k, par, e, first):
                i = 2 * k + par
                for half in range(2):
                    act.wait_ge(h_ready, 2 * i + half + 1)
                    if not first:
                        act.wait_ge(al_ready, 2 * (i - 2) + half + 1)
                    for f in range(HALF):
                        fc = half * HALF + f
                        nc.scalar.activation(act_f[:, par, fc, :], ps_h[par][half][:, f, :], ACT.Gelu_apprx_tanh,
                                             bias=bb1[:, bass.ds(e, 1), fc:fc + 1].rearrange("p a f -> p (a f)")).then_inc(gelu_ready, 1)

            e = experts_of(act, 0)
            step(0, 0, True)
            step(0, 1, True)
            gelu(0, 0, e[0], True)
            step(1, 0, False)
            gelu(0, 1, e[1], True)
            step(1, 1, False)
            with act.Fori(1, PAIRS - 1) as k:
                e = experts_of(act, k)
                gelu(k, 0, e[0], False)
                step(k + 1, 0, False)
                gelu(k, 1, e[1], False)
                step(k + 1, 1, False)
            e = experts_of(act, PAIRS - 1)
            gelu(PAIRS - 1, 0, e[0], False)
            gelu(PAIRS - 1, 1, e[1], False)

        @block.vector
        def _(dve):
            def low_x(k, par):
                i = 2 * k + par
                dve.wait_ge(xh_ready, i + 1)
                nc.vector.tensor_tensor(xl[:, par], ps_x[:, :, :], xh[:, par], ALU.subtract).then_inc(xl_ready, 1)

            def split(k, par, first):
                i = 2 * k + par
                for half in range(2):
                    part = slice(half * HALF, (half + 1) * HALF)
                    dve.wait_ge(gelu_ready, FC * i + HALF * (half + 1))
                    if not first and half == 0:
                        dve.wait_ge(y_ready, i - 1)
                    nc.vector.tensor_copy(ah[:, par, part], act_f[:, par, part]).then_inc(ah_ready, 1)
                    dve.wait_ge(ah_ready, 2 * i + half + 1)
                    nc.vector.tensor_tensor(al[:, par, part], act_f[:, par, part], ah[:, par, part], ALU.subtract).then_inc(al_ready, 1)

            def add_bias(k, par, e, first):
                i = 2 * k + par
                dve.wait_ge(y_ready, i + 1)
                if not first:
                    dve.wait_ge(y_left[par], 16 * k)
                nc.vector.tensor_tensor(yc[:, par], ps_y[par][:, :], bb2[:, bass.ds(e, 1), :].rearrange("p a n -> p (a n)"),
                                        ALU.add).then_inc(y_used, 1)

            e = experts_of(dve, 0)
            low_x(0, 0)
            low_x(0, 1)
            split(0, 0, True)
            low_x(1, 0)
            split(0, 1, True)
            add_bias(0, 0, e[0], True)
            low_x(1, 1)
            split(1, 0, False)
            add_bias(0, 1, e[1], True)
            with dve.Fori(1, PAIRS - 1) as k:
                e = experts_of(dve, k)
                low_x(k + 1, 0)
                split(k, 1, False)
                add_bias(k, 0, e[0], False)
                low_x(k + 1, 1)
                split(k + 1, 0, False)
                add_bias(k, 1, e[1], False)
            e = experts_of(dve, PAIRS - 1)
            split(PAIRS - 1, 1, False)
            add_bias(PAIRS - 1, 0, e[0], False)
            add_bias(PAIRS - 1, 1, e[1], False)


def combine(nc, t, cst, weight, place, ys, h, x1, out):
    y = t.sbuf("co_y", [P, 2, NT, 2, C])
    hc = t.sbuf("co_h", [P, 2, NT, C])
    xc = t.sbuf("co_x", [P, 2, NT, C])
    part = t.sbuf("co_part", [P, NT, C])
    s = t.sbuf("co_sum", [P, NT, C])
    norm1 = t.sbuf("co_norm", [P, NT, C])
    gained = t.sbuf("co_gained", [P, NT, C])
    v = t.sbuf("co_v", [P, NT, C])
    vn = t.sbuf("co_vn", [P, NT, C])
    result = t.sbuf("co_result", [P, 2, NT, C])
    stats = t.sbuf("co_stats", [P, 2, NT, 6])
    mv = t.sbuf("co_mv", [P, 2, NT, 2])
    std = t.sbuf("co_std", [P, 2, NT])
    rstd = t.sbuf("co_rstd", [P, 2, NT])
    y_in, h_in, x_in, left = ([t.sem(f"co_{n}{k}") for k in range(2)] for n in ("y_in", "h_in", "x_in", "left"))
    part_ready, sum_ready, n_ready, gained_ready, v_ready, vn_ready, ready = (
        t.sem("co_" + n) for n in ("part_ready", "sum_ready", "n_ready", "gained_ready", "v_ready", "vn_ready", "ready"))
    stats_done, var_ready, std_ready, rstd_ready = ([t.sem(f"co_{n}{k}") for k in range(2)] for n in ("stats", "var", "std", "rstd"))
    eps = const(cst, "eps")
    tiles = lambda a: a.rearrange("b (s j p) c -> (b s) p j c", s=2, p=P)
    one = lambda a: a.rearrange("a p j c -> p (a j) c")
    over_tiles = lambda a: a.unsqueeze(1).to_broadcast([P, NT, C])
    chunks = 2 * B

    with nc.Block() as block:
        @block.gpsimd
        def _(pool):
            for ck in range(chunks):
                if ck >= 2:
                    pool.wait_ge(sum_ready, NT * (ck - 1))
                for j in range(NT):
                    for e in range(2):
                        nc.gpsimd.indirect_dma_start(y[:, ck % 2, j, e, :], None, ys,
                                                     bass.IndirectOffsetOnAxis(place[:, e, ck * NT + j:ck * NT + j + 1], 0)).then_inc(y_in[ck % 2], 16)

        @block.sync
        def _(sp):
            def load(b, half):
                sp.dma_start(hc[:, half], one(tiles(h)[bass.ds(2 * b + half, 1)])).then_inc(h_in[half], 16)
                sp.dma_start(xc[:, half], one(tiles(x1)[bass.ds(2 * b + half, 1)])).then_inc(x_in[half], 16)

            def chunk(b, half, more):
                ck = 2 * b + half
                sp.wait_ge(ready, ck + 1)
                sp.dma_start(one(tiles(out)[bass.ds(ck, 1)]), result[:, half]).then_inc(left[half], 16)
                if more:
                    load(b + 1, half)

            for half in range(2):
                load(0, half)
            with sp.Fori(0, B - 1) as b:
                for half in range(2):
                    chunk(b, half, True)
            for half in range(2):
                chunk(B - 1, half, False)
            for half in range(2):
                sp.wait_ge(left[half], 16 * B)

        @block.scalar
        def _(act):
            def chunk(b, half, first):
                for k in range(2):
                    act.wait_ge(var_ready[k], NT * (2 * b + half + 1))
                    nc.scalar.activation(std[:, k, :], mv[:, k, :, 1], ACT.Sqrt, bias=eps).then_inc(std_ready[k], 1)

            over_chunks(act, chunk)

        @block.vector
        def _(dve):
            def norm(ck, k, src, dst, ready):
                for j in range(NT):
                    nc.vector.bn_stats(stats[:, k, j], src[:, j, :]).then_inc(stats_done[k], 1)
                dve.wait_ge(stats_done[k], NT * (ck + 1))
                nc.vector.memset(std[:, k, :], 0.0)
                for j in range(NT):
                    nc.vector.bn_aggr(mv[:, k, j], stats[:, k, j]).then_inc(var_ready[k], 1)
                dve.wait_ge(std_ready[k], ck + 1)
                nc.vector.reciprocal(rstd[:, k, :], std[:, k, :]).then_inc(rstd_ready[k], 1)
                dve.wait_ge(rstd_ready[k], ck + 1)
                for j in range(NT):
                    nc.vector.tensor_scalar(dst[:, j], src[:, j], mv[:, k, j, 0:1], rstd[:, k, j:j + 1], ALU.subtract, ALU.mult).then_inc(ready, 1)

            def chunk(b, half, first):
                ck = 2 * b + half
                dve.wait_ge(h_in[half], 16 * (b + 1))
                dve.wait_ge(y_in[half], 16 * 2 * NT * (b + 1))
                share = lambda j, e: weight[:, bass.ds(ck * NT + j, 1), e]
                for j in range(NT):
                    nc.vector.scalar_tensor_tensor(out=part[:, j], in0=y[:, half, j, 0], scalar=share(j, 0), in1=hc[:, half, j],
                                                   op0=ALU.mult, op1=ALU.add).then_inc(part_ready, 1)
                dve.wait_ge(part_ready, NT * (ck + 1))
                for j in range(NT):
                    nc.vector.scalar_tensor_tensor(out=s[:, j], in0=y[:, half, j, 1], scalar=share(j, 1), in1=part[:, j],
                                                   op0=ALU.mult, op1=ALU.add).then_inc(sum_ready, 1)
                dve.wait_ge(sum_ready, NT * (ck + 1))
                norm(ck, 0, s, norm1, n_ready)
                dve.wait_ge(n_ready, NT * (ck + 1))
                nc.vector.tensor_tensor(gained[:, :, :], norm1[:, :, :], over_tiles(const(cst, "g2")), ALU.mult).then_inc(gained_ready, 1)
                dve.wait_ge(gained_ready, ck + 1)
                nc.vector.tensor_tensor(v[:, :, :], gained[:, :, :], over_tiles(const(cst, "b2")), ALU.add).then_inc(v_ready, 1)
                dve.wait_ge(v_ready, ck + 1)
                norm(ck, 1, v, vn, vn_ready)
                dve.wait_ge(vn_ready, NT * (ck + 1))
                dve.wait_ge(x_in[half], 16 * (b + 1))
                if not isinstance(b, int):
                    dve.wait_ge(left[half], 16 * b)
                nc.vector.tensor_tensor(result[:, half], xc[:, half], vn[:, :, :], ALU.add).then_inc(ready, 1)

            over_chunks(dve, chunk)


UNITS = 12
LAG = 2
RING = 4

ROWS = [(qt, 0, P * (qt + 1)) for qt in range(4)] + \
       [x for qt in range(4, KB) for x in ((qt, 0, 512), (qt, 4, P * (qt - 3)))]
COLUMNS = [(qc, j, max(512 * qc, P * j)) for qc in range(2) for j in range(4 * qc + 4)]


def attention(nc, t, name, cst, masks, qk, vs, part_rows, scale, os):
    ps_s = [t.psum(f"{name}_s{n}", [P, 512]) for n in range(3)]
    ps_st = [t.psum(f"{name}_st{n}", [P, 512]) for n in range(2)]
    ps_o = [t.psum(f"{name}_o{n}", [P, 512]) for n in range(2)]
    ps_m = t.psum(f"{name}_m", [P, 512])
    stack = [[t.sbuf(f"{name}_{w}{n}", [98, T], F32R) for n in range(RING)] for w in "qk"]
    vh = t.sbuf(f"{name}_v", [P, RING, KB, 2 * HD])
    prob = t.sbuf(f"{name}_p", [P, 3, 512])
    maxima = t.sbuf(f"{name}_mx", [P, 2, UNITS])
    split = t.sbuf(f"{name}_split", [P, 2, 2, KB], F32R)
    mrow = t.sbuf(f"{name}_mrow", [2 * KB, RING, P], F32R)
    oT = t.sbuf(f"{name}_oT", [P, 2, 512])
    recip = t.sbuf(f"{name}_recip", [P, 2, 4, 4])
    ob = t.sbuf(f"{name}_ob", [P, 2, 4, 4, HD])
    ident = const(cst, "ident")
    ident_b, mask_rows, mask_cols = masks[:, 0], masks[:, 1], masks[:, 2]

    loaded = [t.sem(f"{name}_loaded{n}") for n in range(RING)]
    mrow_in = [t.sem(f"{name}_mrow_in{n}") for n in range(RING)]
    stored = [t.sem(f"{name}_stored{n}") for n in range(2)]
    zeroed, s_ready, s_reduced, st_ready, p_ready, pv_done = (
        t.sem(f"{name}_" + n) for n in ("zeroed", "s_ready", "s_reduced", "st_ready", "p_ready", "pv_done"))
    joined, high, split_ready, mT_ready, mrow_ready = (
        t.sem(f"{name}_" + n) for n in ("joined", "high", "split_ready", "mT_ready", "mrow_ready"))
    oT_ready, o_turned, recip_ready, o_ready = (t.sem(f"{name}_" + n) for n in ("oT_ready", "o_turned", "recip_ready", "o_ready"))
    LOADS = 16 * 7
    groups = NH // 4

    def over_groups(eng, body):
        body(0, True, False)
        with eng.Fori(1, groups - 1) as g:
            body(g, False, False)
        body(groups - 1, False, True)

    with nc.Block() as block:
        @block.sync
        def _(sp):
            def load(head, slot):
                for part, (hq, hk) in enumerate(((0, 0), (0, 1), (1, 0))):
                    for w, hl in ((0, hq), (1, hk)):
                        src = qk[w][hl][bass.ds(head, 1), 0:part_rows, :].rearrange("a r t -> (a r) t")
                        sp.dma_start(stack[w][slot][32 * part:32 * part + part_rows, :].bitcast(F32), src).then_inc(loaded[slot], 16)
                sp.dma_start(vh[:, slot], vs[bass.ds(head, 1), :, :].rearrange("a p (k e) -> p (a k) e", e=2 * HD)).then_inc(loaded[slot], 16)

            def store(g, qc):
                sp.wait_ge(o_ready, 2 * g + qc + 1)
                sp.dma_start(os[bass.ds(g * 2 + qc, 1)].rearrange("a p q d -> p (a q) d"),
                             ob[:, qc].rearrange("p q h d -> p q (h d)")).then_inc(stored[qc], 16)

            sp.wait_ge(zeroed, 3)
            for n in range(3):
                load(n, n)

            def body(g, first, last):
                for h in range(4):
                    n = 4 * g + h
                    if not (last and h > 0):
                        if not (first and h == 0):
                            sp.wait_ge(pv_done, UNITS * n)
                        load(n + 3, (h + 3) % 4)
                    if first and h == 0:
                        for m in range(2):
                            rows(m, m)
                    elif not (last and h == 3):
                        rows(n + 1, (h + 1) % 4)
                    if h == 0 and not first:
                        store(g - 1, 1)
                store(g, 0)

            def rows(m, slot):
                sp.wait_ge(mrow_ready, m + 1)
                for k in range(2):
                    sp.dma_start(stack[0][slot][96 + k:97 + k, :].bitcast(F32), mrow[k * KB:(k + 1) * KB, slot, :].bitcast(F32)).then_inc(mrow_in[slot], 16)

            over_groups(sp, body)
            store(groups - 1, 1)
            for qc in range(2):
                sp.wait_ge(stored[qc], 16 * groups)

        @block.gpsimd
        def _(pool):
            for n in range(RING):
                for w in range(2):
                    last = nc.gpsimd.memset(stack[w][n][0:96, :].bitcast(F32), 0.0)
            last.then_inc(zeroed, 1)
            for n in range(RING):
                last = nc.gpsimd.memset(stack[1][n][96:98, :].bitcast(F32), -1.0)
            last.then_inc(zeroed, 2)

        @block.vector
        def _(dve):
            def reduce(m, u, parity):
                qt, k0, width = ROWS[u]
                dve.wait_ge(s_ready, UNITS * m + u + 1)
                nc.vector.tensor_reduce(maxima[:, parity, u:u + 1], ps_s[u % 3][:, 0:width], AX.X, ALU.max).then_inc(s_reduced, 1)

            def join(m, parity):
                dve.wait_ge(s_reduced, UNITS * (m + 1))
                two = maxima[:, parity, 4:UNITS].rearrange("p (q k) -> p q k", k=2)
                nc.vector.tensor_tensor(maxima[:, parity, 4:8], two[:, :, 0], two[:, :, 1], ALU.max).then_inc(joined, 1)
                dve.wait_ge(joined, m + 1)
                nc.vector.tensor_copy(split[:, parity, 0], maxima[:, parity, 0:KB]).then_inc(high, 1)
                dve.wait_ge(high, m + 1)
                nc.vector.tensor_tensor(split[:, parity, 1], maxima[:, parity, 0:KB], split[:, parity, 0].bitcast(F32),
                                        ALU.subtract).then_inc(split_ready, 1)

            def take_rows(m, slot):
                dve.wait_ge(mT_ready, m + 1)
                nc.vector.tensor_copy(mrow[:, slot, :], ps_m[0:2 * KB, 0:P]).then_inc(mrow_ready, 1)

            def normalise(g, qc, first):
                dve.wait_ge(o_turned, 2 * g + qc + 1)
                o = ps_m[:, :].rearrange("p (q h e) -> p q h e", q=4, h=4)
                nc.vector.reciprocal(recip[:, qc], o[:, :, :, HD]).then_inc(recip_ready, 1)
                dve.wait_ge(recip_ready, 2 * g + qc + 1)
                if not first:
                    dve.wait_ge(stored[qc], 16 * g)
                nc.vector.tensor_tensor(ob[:, qc], o[:, :, :, 0:HD], recip[:, qc].unsqueeze(3).to_broadcast([P, 4, 4, HD]),
                                        ALU.mult).then_inc(o_ready, 1)

            for m in range(2):
                for u in range(UNITS):
                    reduce(m, u, m)
                join(m, m)
            take_rows(0, 0)

            def body(g, first, last):
                for h in range(4):
                    n = 4 * g + h
                    for u in range(UNITS):
                        if not (last and h >= 2):
                            reduce(n + 2, u, h % 2)
                        if u == 5 and not (last and h == 3):
                            take_rows(n + 1, (h + 1) % 4)
                        if u == 9 and h == 0 and not first:
                            normalise(g - 1, 1, first_second)
                    if not (last and h >= 2):
                        join(n + 2, h % 2)
                normalise(g, 0, first)

            first_second = True
            body(0, True, False)
            body(1, False, False)
            first_second = False
            with dve.Fori(2, groups - 1) as g:
                body(g, False, False)
            body(groups - 1, False, True)
            normalise(groups - 1, 1, False)

        @block.scalar
        def _(act):
            def take_output(g, qc, first):
                act.wait_ge(pv_done, UNITS * 4 * g + (UNITS * 3 + 4 if qc == 0 else UNITS * 4))
                if not first:
                    act.wait_ge(o_turned, 2 * g + qc - 1)
                nc.scalar.copy(oT[:, qc, :], ps_o[qc][:, :]).then_inc(oT_ready, 1)

            def body(g, first, last):
                for h in range(4):
                    n = 4 * g + h
                    for u in range(UNITS):
                        qc, j, q0 = COLUMNS[u]
                        width = 512 * (qc + 1) - q0
                        act.wait_ge(st_ready, UNITS * n + u + 1)
                        if not (first and h == 0 and u < 3):
                            act.wait_ge(pv_done, UNITS * n + u - 2)
                        nc.scalar.activation(prob[:, u % 3, 0:width], ps_st[u % 2][:, 0:width], ACT.Exp, scale=scale).then_inc(p_ready, 1)
                        if u == 2 and h == 0 and not first:
                            take_output(g - 1, 1, first_two)
                        if u == 7 and h == 3:
                            take_output(g, 0, first)

            first_two = True
            body(0, True, False)
            body(1, False, False)
            first_two = False
            with act.Fori(2, groups) as g:
                body(g, False, False)
            take_output(groups - 1, 1, False)

        @block.tensor
        def _(pe):
            def row_scores(m, u, slot, first):
                qt, k0, width = ROWS[u]
                if not first:
                    pe.wait_ge(s_reduced, UNITS * m + u - 2)
                on_diagonal = k0 * P + width == (qt + 1) * P
                ins = nc.tensor.matmul(ps_s[u % 3][:, 0:width], stack[0][slot][0:96, qt * P:(qt + 1) * P],
                                       stack[1][slot][0:96, k0 * P:k0 * P + width], start=True, stop=not on_diagonal)
                if on_diagonal:
                    ins = nc.tensor.matmul(ps_s[u % 3][:, width - P:width], ident_b, mask_rows, start=False, stop=True)
                ins.then_inc(s_ready, 1)

            def column_scores(n, u, slot, first):
                qc, j, q0 = COLUMNS[u]
                width = 512 * (qc + 1) - q0
                if not first:
                    pe.wait_ge(p_ready, UNITS * n + u - 1)
                ins = nc.tensor.matmul(ps_st[u % 2][:, 0:width], stack[1][slot][:, j * P:(j + 1) * P], stack[0][slot][:, q0:q0 + width],
                                       start=True, stop=j < 4 * qc)
                if j >= 4 * qc:
                    ins = nc.tensor.matmul(ps_st[u % 2][:, 0:P], ident_b, mask_cols, start=False, stop=True)
                ins.then_inc(st_ready, 1)

            def value_product(n, u, h):
                qc, j, q0 = COLUMNS[u]
                width = 512 * (qc + 1) - q0
                pe.wait_ge(p_ready, UNITS * n + u + 1)
                nc.tensor.matmul(ps_o[qc][32 * h:32 * h + 32, 512 - width:512], vh[:, h, j, :], prob[:, u % 3, 0:width],
                                 start=(j == 0), stop=(j == 4 * qc + 3)).then_inc(pv_done, 1)

            def turn_maxima(m, parity):
                pe.wait_ge(split_ready, m + 1)
                nc.tensor.transpose(ps_m[0:2 * KB, 0:P], split[:, parity].rearrange("p s q -> p (s q)").bitcast(F32), ident).then_inc(mT_ready, 1)

            def turn_output(g, qc):
                pe.wait_ge(oT_ready, 2 * g + qc + 1)
                for q in range(4):
                    last = nc.tensor.transpose(ps_m[:, q * P:(q + 1) * P], oT[:, qc, q * P:(q + 1) * P], ident)
                last.then_inc(o_turned, 1)

            for m in range(2):
                pe.wait_ge(loaded[m], LOADS)
                for u in range(UNITS):
                    row_scores(m, u, m, m == 0 and u < 3)
            turn_maxima(0, 0)

            def body(g, first, last):
                for h in range(4):
                    n = 4 * g + h
                    for u in range(UNITS):
                        if not (last and h >= 2):
                            if u == 0:
                                pe.wait_ge(loaded[(h + 2) % 4], LOADS * (g + 1 + h // 2))
                            row_scores(n + 2, u, (h + 2) % 4, False)
                        if u == 0:
                            pe.wait_ge(mrow_in[h], 32 * (g + 1))
                        column_scores(n, u, h, first and h == 0 and u < 2)
                        if u >= LAG:
                            if h == 0 and not first and u == LAG:
                                pe.wait_ge(oT_ready, 2 * g - 1)
                            if h == 0 and not first and u == LAG + 4:
                                pe.wait_ge(oT_ready, 2 * g)
                            value_product(n, u - LAG, h)
                        elif h > 0:
                            value_product(n - 1, UNITS + u - LAG, h - 1)
                        elif not first:
                            value_product(n - 1, UNITS + u - LAG, 3)
                        if u == 3 and not (last and h == 3):
                            if h == 0 and not first:
                                pe.wait_ge(o_ready, 2 * g - 1)
                            elif h == 1 and not first:
                                pe.wait_ge(o_ready, 2 * g)
                            else:
                                pe.wait_ge(mrow_ready, n + 1)
                            turn_maxima(n + 1, (h + 1) % 2)
                        if u == 8 and h == 0 and not first:
                            pe.wait_ge(mrow_ready, n + 2)
                            turn_output(g - 1, 1)
                    if h == 3:
                        pe.wait_ge(mrow_ready, n + (1 if last else 2))
                        turn_output(g, 0)

            over_groups(pe, body)
            for u in range(UNITS - LAG, UNITS):
                value_product(NH - 1, u, 3)
            pe.wait_ge(o_ready, 2 * groups - 1)
            turn_output(groups - 1, 1)


def build(nc, a, outs):
    internal = lambda name, shape, dt=F32: nc.dram_tensor(name, shape, dt, kind="Internal").ap()
    qk = [[internal(f"{w}_{hl}", [NH, 2 * HD, T]) for hl in ("high", "low")] for w in "qk"]
    vs = internal("v_rows", [NH, P, KB * 2 * HD])
    os = internal("attended", [NH // 4 * 2, P, 4, 4 * HD])
    x1, n1, h = (internal(n, [B, T, C]) for n in ("x1", "n1", "h_rows"))
    xs, ys = (internal(n, [TILES * P, C]) for n in ("sorted_rows", "expert_rows"))
    sems = []
    with ExitStack() as whole:
        t = outer = Tools(nc, whole, sems)
        cst = {"block": t.sbuf("constants", [P, WIDTH["block"]])}
        masks = t.sbuf("masks", [P, 3, P], BF16)
        wout = t.sbuf("w_out1", [P, 2, C])
        cout = t.sbuf("bias_out1", [P, C])
        masked = t.sem("masked")
        with nc.Block() as block:
            @block.gpsimd
            def _(pool):
                nc.gpsimd.memset(masks[:, 0], 0.0).then_inc(masked, 1)
                nc.gpsimd.memset(masks[:, 1:3], 0.0).then_inc(masked, 1)
                pool.wait_ge(masked, 2)
                nc.gpsimd.affine_select(out=masks[:, 0], in_=masks[:, 0], compare_op=ALU.not_equal, fill=1.0, base=0,
                                        pattern=[[-1, P]], channel_multiplier=1)
                nc.gpsimd.affine_select(out=masks[:, 1], in_=masks[:, 1], compare_op=ALU.is_ge, fill=MASKED, base=0,
                                        pattern=[[-1, P]], channel_multiplier=1)
                nc.gpsimd.affine_select(out=masks[:, 2], in_=masks[:, 2], compare_op=ALU.is_ge, fill=MASKED, base=0,
                                        pattern=[[1, P]], channel_multiplier=-1)
        with ExitStack() as ctx:
            t = Tools(nc, ctx, sems)
            cst["latent"] = t.sbuf("latent_constants", [P, WIDTH["latent"]])
            rope = t.sbuf("rope", [P, 2, T])
            wlat = t.sbuf("w_latent", [P, CC, 2, 2, 2, P])
            blat = t.sbuf("b_latent", [P, 2, 2, 2])
            with ExitStack() as inner:
                compose_weights(nc, Tools(nc, inner, sems), {which: a[which] for which in PACKS}, cst, a["rope"], rope, wlat, blat, wout, cout)
            with ExitStack() as inner:
                latent_projections(nc, Tools(nc, inner, sems), a["x"], cst, rope, wlat, blat, qk, vs)
        with ExitStack() as ctx:
            attention(nc, Tools(nc, ctx, sems), "a1", cst, masks, qk, vs, 2 * HD, float(L) ** -0.5, os)
        renew_semaphores(nc, sems)
        with ExitStack() as ctx:
            between_attentions(nc, Tools(nc, ctx, sems), a["x"], os, cst, wout, cout, x1, n1, qk, vs)
        with ExitStack() as ctx:
            attention(nc, Tools(nc, ctx, sems), "a2", cst, masks, qk, vs, HD, float(HD) ** -0.5, os)
        renew_semaphores(nc, sems)
        logits = outer.sbuf("logits", [P, TT, E])
        weight = outer.sbuf("weight", [P, TT, 2])
        place = outer.sbuf("place", [P, 2, TT], U32)
        tile_expert = outer.sbuf("tile_expert", [P, TILES // 2, 4], mybir.dt.int32)
        with ExitStack() as ctx:
            after_attentions(nc, Tools(nc, ctx, sems), n1, os, cst, h, logits, xs)
        with ExitStack() as ctx:
            route(nc, Tools(nc, ctx, sems), cst, logits, weight, place, tile_expert)
        with ExitStack() as ctx:
            e = Tools(nc, ctx, sems)
            w1s = [e.sbuf("w1_high", [P, E, CC, F], FP16), e.sbuf("w1_low", [P, E, CC, F], BF16)]
            w2s = [e.sbuf("w2_high", [P, E, F // P, C], FP16), e.sbuf("w2_low", [P, E, F // P, C], BF16)]
            bb = [e.sbuf("bb1", [P, E, F // P]), e.sbuf("bb2", [P, E, C])]
            with ExitStack() as inner:
                scatter_and_split(nc, Tools(nc, inner, sems), h, place, xs, a["w1"], a["w2"], w1s, w2s, [a["bb1"], a["bb2"]], bb)
            with ExitStack() as inner:
                experts(nc, Tools(nc, inner, sems), cst, xs, ys, tile_expert, bb, w1s, w2s)
        with ExitStack() as ctx:
            combine(nc, Tools(nc, ctx, sems), cst, weight, place, ys, h, x1, outs["out"])


def kernel(**inputs):
    import concourse.bacc as _bacc
    from concourse.bass_utils import run_bass_kernel_spmd as _run

    i = {k: np.asarray(v) for k, v in inputs.items()}
    arrays = {
        "x": np.ascontiguousarray(i["L0_attn_x"]),
        "latent": pack("latent", attention_constants(i)),
        "block": pack("block", block_constants(i)),
        "w1": np.ascontiguousarray(i["L0_ffn_w1"]),
        "w2": np.ascontiguousarray(i["L0_ffn_w2"]),
        "bb1": np.ascontiguousarray(i["L0_ffn_bb1"].reshape(E, F // P, P).transpose(2, 0, 1)),
        "bb2": np.tile(i["L0_ffn_bb2"], (P, 1, 1)),
        "rope": rope_tables(),
    }
    nc = _bacc.Bacc("TRN2", target_bir_lowering=False, num_devices=1)
    a = {n: nc.dram_tensor(n + "_dram", v.shape, mybir.dt.from_np(v.dtype), kind="ExternalInput").ap() for n, v in arrays.items()}
    out = nc.dram_tensor("out_dram", (B, T, C), F32, kind="ExternalOutput").ap()
    build(nc, a, {"out": out})
    r = _run(nc, [{n + "_dram": v for n, v in arrays.items()}], core_ids=[0])
    return r.results[0]["out_dram"]
```

```python
from contextlib import ExitStack

import concourse.bass as bass
from concourse import mybir
import numpy as np

F32 = mybir.dt.float32
F32R = mybir.dt.float32r
BF16 = mybir.dt.bfloat16
FP16 = mybir.dt.float16
U32 = mybir.dt.uint32
ALU = mybir.AluOpType
ACT = mybir.ActivationFunctionType
AX = mybir.AxisListType

P = 128
B, T, C = 4, 1024, 256
H, HD, L = 16, 16, 32
NH = B * H
E, F = 8, 1024
CC = C // P
CH = 512
NT = CH // P
KB = T // P
TT = B * T // P
TILES = 2 * TT + E
EPS = 1e-5
MASKED = -1e30

PACKS = {
    "latent": dict(
        wq_rows=2 * C,
        wk_rows=2 * C,
        bq=2, bk=2,
        q2l_blocks=2 * P,
        kv2l_blocks=2 * P,
        q2l_bias=2, kv2l_bias=2,
        wqk_blocks=4 * P,
        wqk_bias=2,
        wv=CC * C,
        bv=C,
        l2o_blocks=4 * P,
        kvl_blocks=4 * P,
        cproj=2 * C,
        l2o_bias=P,
        kvl_bias=P,
        cproj_bias=C,
    ),
    "block": dict(
        ident=P,
        eps=1,
        wqkv2=CC * 3 * C,
        wo2=CC * C,
        g1=C, b1=C, g2=C, b2=C,
        wg=CC * E,
        before=P,
        ones=P,
        expert=E,
        tile=TILES,
    ),
}
PLACE = {name: (pack, sum(list(widths.values())[:k]), width)
         for pack, widths in PACKS.items() for k, (name, width) in enumerate(widths.items())}
WIDTH = {pack: sum(widths.values()) for pack, widths in PACKS.items()}


def pack(which, named):
    out = np.zeros((P, WIDTH[which]), np.float32)
    for name, a in named.items():
        _, at, width = PLACE[name]
        out[: a.shape[0], at:at + width] = a.reshape(a.shape[0], -1)
    return out


def const(cst, name):
    which, at, width = PLACE[name]
    return cst[which][:, at:at + width]


def attention_constants(i):
    w, bias = i["L0_attn_c_attn_w"], i["L0_attn_c_attn_b"]
    q2l, kv2l, wqk, l2o = (i["L0_attn_" + n] for n in ("q2l_w", "kv2l_w", "wqk_w", "l2o_w"))
    rows = lambda a: a.reshape(2, P, C).transpose(1, 0, 2)
    halves = lambda a: a.reshape(2, P).T

    def blocks(m):
        r, c = m.shape
        out = np.zeros((8, r, 8, c), np.float32)
        for h in range(8):
            out[h, :, h, :] = m
        return out.reshape(8 * r, 8 * c)

    wqk_blocks = np.stack([blocks(wqk[po::2, pi::2].T) for po in range(2) for pi in range(2)], 1)
    l2o_blocks = np.zeros((8, HD, 4, 4, L), np.float32)
    kvl_blocks = np.zeros((4, L, 4, 8, HD), np.float32)
    for hg in range(4):
        for h in range(4):
            l2o_blocks[(hg % 2) * 4 + h, :, hg, h, :] = l2o
            kvl_blocks[h, :, hg, (hg % 2) * 4 + h, :] = kv2l
    tiled = lambda v: np.tile(v, 8)[:, None]
    return {
        "wq_rows": rows(w[:C]), "wk_rows": rows(w[C:2 * C]),
        "bq": halves(bias[:C]), "bk": halves(bias[C:2 * C]),
        "q2l_blocks": np.stack([blocks(q2l[p::2].T) for p in range(2)], 1),
        "kv2l_blocks": np.stack([blocks(kv2l[p::2].T) for p in range(2)], 1),
        "q2l_bias": np.concatenate([tiled(i["L0_attn_q2l_b"][p::2]) for p in range(2)], 1),
        "kv2l_bias": np.concatenate([tiled(i["L0_attn_kv2l_b"][p::2]) for p in range(2)], 1),
        "wqk_blocks": wqk_blocks,
        "wqk_bias": np.concatenate([tiled(i["L0_attn_wqk_b"][p::2]) for p in range(2)], 1),
        "wv": w[2 * C:].T.reshape(CC, P, C).transpose(1, 0, 2),
        "bv": np.tile(bias[2 * C:], (P, 1)),
        "l2o_blocks": l2o_blocks.reshape(P, 4 * P), "kvl_blocks": kvl_blocks.reshape(P, 4 * P),
        "cproj": i["L0_attn_cproj_w"].T.reshape(2, P, C).transpose(1, 0, 2),
        "l2o_bias": np.tile(np.tile(i["L0_attn_l2o_b"], 8)[:, None], (1, P)),
        "kvl_bias": np.tile(np.tile(i["L0_attn_kv2l_b"], 4)[:, None], (1, P)),
        "cproj_bias": np.tile(i["L0_attn_cproj_b"], (P, 1)),
    }


def block_constants(i):
    chunks = lambda a: a.reshape(CC, P, -1).transpose(1, 0, 2)
    f = lambda n: i["L0_ffn_" + n]
    out = {
        "wqkv2": chunks(f("w_qkv")), "wo2": chunks(f("w_o")), "wg": chunks(f("wg")),
        "ident": np.eye(P, dtype=np.float32), "eps": np.full((P, 1), EPS, np.float32),
        "before": np.triu(np.ones((P, P), np.float32), 1), "ones": np.ones((P, P), np.float32),
        "expert": np.tile(np.arange(E, dtype=np.float32), (P, 1)), "tile": np.tile(np.arange(TILES, dtype=np.float32), (P, 1)),
    }
    return out | {n: np.tile(f(n), (P, 1)) for n in ("g1", "b1", "g2", "b2")}


def rope_tables():
    inv = (1.0 / 10000.0 ** (np.arange(0, L, 2, dtype=np.float32) / np.float32(L))).astype(np.float32)
    angle = np.tile(inv, 8)[:, None] * np.arange(T, dtype=np.float32)[None, :]
    return np.stack([np.cos(angle), np.sin(angle)], 1).astype(np.float32)


def over_chunks(eng, chunk):
    for half in range(2):
        chunk(0, half, half == 0)
    with eng.Fori(1, B) as b:
        for half in range(2):
            chunk(b, half, False)


def over_chunks_ahead(eng, begin, finish):
    def ahead(b, half):
        def call(*between):
            begin(b, half, False, *between)
            return True
        return call

    begin(0, 0, True)
    finish(0, 0, True, ahead(0, 1))
    finish(0, 1, False, ahead(1, 0))
    with eng.Fori(1, B - 1) as b:
        finish(b, 0, False, ahead(b, 1))
        finish(b, 1, False, ahead(b + 1, 0))
    finish(B - 1, 0, False, ahead(B - 1, 1))
    finish(B - 1, 1, False, lambda *between: False)


def beyond_first_batch(b):
    return not isinstance(b, int) or b > 0


class Tools:

    def __init__(self, nc, ctx, sems):
        self.nc, self.ctx, self.sems = nc, ctx, sems

    def sbuf(self, name, shape, dt=F32):
        return self.ctx.enter_context(self.nc.sbuf_tensor(name, shape, dt))

    def psum(self, name, shape, dt=F32):
        return self.ctx.enter_context(self.nc.psum_tensor(name, shape, dt))

    def sem(self, name):
        self.sems.append(self.nc.alloc_semaphore(name))
        return self.sems[-1]


def renew_semaphores(nc, sems):
    nc.clear_and_free_semaphores(sems)
    sems.clear()
    nc.all_engine_barrier()


def compose_weights(nc, t, packed, cst, rope_dram, rope, wlat, blat, wout, cout):
    ps = [t.psum(f"cw_ps{n}", [P, 512]) for n in range(2)]
    t1 = t.sbuf("cw_t1", [P, 4, C])
    loaded, made, moved = t.sem("cw_loaded"), t.sem("cw_made"), t.sem("cw_moved")

    c = lambda name: const(cst, name)
    rows = [c("wq_rows").rearrange("p (g c) -> p g c", g=2), c("wk_rows").rearrange("p (g c) -> p g c", g=2)]
    to_latent = [c("q2l_blocks").rearrange("p (e m) -> p e m", e=2), c("kv2l_blocks").rearrange("p (e m) -> p e m", e=2)]
    l2o = c("l2o_blocks").rearrange("p (g m) -> p g m", g=4)
    kvl = c("kvl_blocks").rearrange("p (g m) -> p g m", g=4)
    cproj = c("cproj").rearrange("p (g n) -> p g n", g=2)
    with nc.Block() as block:
        @block.sync
        def _(sp):
            for which in PACKS:
                sp.dma_start(cst[which][:, :], packed[which]).then_inc(loaded, 16)
            sp.dma_start(rope[:, :, :], rope_dram).then_inc(loaded, 16)

        @block.tensor
        def _(pe):
            pe.wait_ge(loaded, 48)
            step = 0
            for w in range(2):
                for g in range(2):
                    if step >= 2:
                        pe.wait_ge(moved, step - 1)
                    for cc in range(CC):
                        last = nc.tensor.matmul(ps[step % 2][:, cc * C:(cc + 1) * C], rows[w][:, g, cc * P:(cc + 1) * P],
                                                to_latent[w].rearrange("p e m -> p (e m)"), start=True, stop=True)
                    last.then_inc(made, 1)
                    step += 1
            pe.wait_ge(moved, step - 1)
            for w, b in enumerate(("bq", "bk")):
                for e in range(2):
                    last = nc.tensor.matmul(ps[0][:, (w * 2 + e) * 2:(w * 2 + e) * 2 + 2], to_latent[w][:, e, :], c(b),
                                            start=True, stop=True)
            last.then_inc(made, 1)
            step += 1
            for hg in range(4):
                pe.wait_ge(moved, step - 1)
                nc.tensor.matmul(ps[step % 2][:, 0:C], l2o[:, hg, :], cproj[:, hg // 2, :], start=True, stop=True).then_inc(made, 1)
                step += 1
            pe.wait_ge(moved, step)
            for g in range(2):
                for k in range(2):
                    last = nc.tensor.matmul(ps[g][:, 0:C], kvl[:, 2 * g + k, :], t1[:, 2 * g + k, :], start=(k == 0), stop=(k == 1))
                last.then_inc(made, 1)
                step += 1
            pe.wait_ge(moved, step - 1)
            for g in range(2):
                nc.tensor.matmul(ps[0][:, 0:C], c("l2o_bias"), cproj[:, g, :], start=(g == 0), stop=False)
            for hg in range(4):
                last = nc.tensor.matmul(ps[0][:, 0:C], c("kvl_bias"), t1[:, hg, :], start=False, stop=(hg == 3))
            last.then_inc(made, 1)

        @block.vector
        def _(dve):
            step = 0
            for w in range(2):
                for g in range(2):
                    dve.wait_ge(made, step + 1)
                    nc.vector.tensor_copy(wlat[:, :, w, :, g, :],
                                          ps[step % 2][:, :].rearrange("p (c e m) -> p c e m", c=CC, e=2)).then_inc(moved, 1)
                    step += 1
            dve.wait_ge(made, step + 1)
            for w, b in enumerate(("q2l_bias", "kv2l_bias")):
                for e in range(2):
                    last = nc.vector.tensor_scalar(blat[:, w, e, :], ps[0][:, (w * 2 + e) * 2:(w * 2 + e) * 2 + 2],
                                                   c(b)[:, e:e + 1], None, ALU.add)
            last.then_inc(moved, 1)
            step += 1
            for hg in range(4):
                dve.wait_ge(made, step + 1)
                nc.vector.tensor_copy(t1[:, hg, :], ps[step % 2][:, 0:C]).then_inc(moved, 1)
                step += 1
            for g in range(2):
                dve.wait_ge(made, step + 1)
                nc.vector.tensor_copy(wout[:, g, :], ps[g][:, 0:C]).then_inc(moved, 1)
                step += 1
            dve.wait_ge(made, step + 1)
            nc.vector.tensor_tensor(cout[:, :], ps[0][:, 0:C], c("cproj_bias"), ALU.add).then_inc(moved, 1)


def latent_projections(nc, t, x, cst, rope, wlat, blat, qk, vs):
    ps_t = [t.psum(f"lp_t{n}", [P, CH]) for n in range(2)]
    ps_pair = [[t.psum(f"lp_pair{n}{e}", [P, CH]) for e in range(2)] for n in range(2)]
    ps_q = [t.psum(f"lp_q{e}", [P, CH]) for e in range(2)]
    xc = t.sbuf("lp_x", [P, 2, NT, C])
    xn = t.sbuf("lp_xn", [P, NT, C])
    xT = t.sbuf("lp_xT", [P, 2, CC, CH])
    stats = t.sbuf("lp_stats", [P, NT, 6])
    mv = t.sbuf("lp_mv", [P, NT, 2])
    std = t.sbuf("lp_std", [P, NT])
    rstd = t.sbuf("lp_rstd", [P, NT])
    prod = t.sbuf("lp_prod", [P, 2, 4, CH])
    rot = t.sbuf("lp_rot", [P, 2, 2, CH])
    out = t.sbuf("lp_out", [P, 4, 2, 2, CH], F32R)
    vt = t.sbuf("lp_v", [P, NT, H, 2 * HD])
    x_in = [t.sem(f"lp_x_in{n}") for n in range(2)]
    stats_done, var_ready, std_ready, rstd_ready = (t.sem("lp_" + n) for n in ("stats_done", "var_ready", "std_ready", "rstd_ready"))
    xn_ready, turned, xT_ready = (t.sem("lp_" + n) for n in ("xn_ready", "turned", "xT_ready"))
    pair_ready, products, rot_ready, q_ready = (t.sem("lp_" + n) for n in ("pair_ready", "products", "rot_ready", "q_ready"))
    hi_ready, lo_ready, v_ready, v_used, zeroed = (t.sem("lp_" + n) for n in ("hi_ready", "lo_ready", "v_ready", "v_used", "zeroed"))
    out_left = [t.sem(f"lp_out_left{r}") for r in range(4)]
    v_left = t.sem("lp_v_left")
    wqk = const(cst, "wqk_blocks").rearrange("p (o i m) -> p o i m", o=2, i=2)
    ident, wqk_bias, eps = const(cst, "ident"), const(cst, "wqk_bias"), const(cst, "eps")
    wv = const(cst, "wv").rearrange("p (c n) -> p c n", c=CC)
    bv = const(cst, "bv").rearrange("p (h d) -> p h d", h=H)
    xt = x.rearrange("b (s j p) c -> (b s) p j c", s=2, p=P)
    chunks = 2 * B

    with nc.Block() as block:
        @block.sync
        def _(sp):
            for half in range(2):
                sp.dma_start(xc[:, half], xt[half]).then_inc(x_in[half], 16)

            def chunk(b, half, more):
                ck = 2 * b + half
                if more:
                    sp.wait_ge(xn_ready, NT * (ck + 1))
                    sp.dma_start(xc[:, half], xt[bass.ds(ck + 2, 1)].rearrange("a p j c -> p (a j) c")).then_inc(x_in[half], 16)
                for r in range(4):
                    w, g = r // 2, r % 2
                    sp.wait_ge(lo_ready, 2 * (4 * ck + r + 1))
                    for hl in range(2):
                        for e in range(2):
                            dst = qk[w][hl][bass.ds(b * H + g * 8, 8), e * HD:(e + 1) * HD, half * CH:(half + 1) * CH]
                            sp.dma_start(dst, out[:, r, hl, e, :].bitcast(F32)).then_inc(out_left[r], 16)
                sp.wait_ge(v_used, NT * (ck + 1))
                for j in range(NT):
                    kb = half * NT + j
                    dst = vs[bass.ds(b * H, H), :, kb * 2 * HD:(kb + 1) * 2 * HD].rearrange("h p e -> p h e")
                    sp.dma_start(dst, vt[:, j]).then_inc(v_left, 16)

            with sp.Fori(0, B - 1) as b:
                for half in range(2):
                    chunk(b, half, True)
            for half in range(2):
                chunk(B - 1, half, False)
            for r in range(4):
                sp.wait_ge(out_left[r], 16 * 4 * chunks)
            sp.wait_ge(v_left, 16 * NT * chunks)

        @block.vector
        def _(dve):
            nc.vector.memset(vt[:, :, :, HD + 1:], 0.0).then_inc(zeroed, 1)
            nc.vector.memset(vt[:, :, :, HD:HD + 1], 1.0).then_inc(zeroed, 1)

            def begin(b, half, first):
                ck = 2 * b + half
                dve.wait_ge(x_in[half], 16 * b + 16)
                for j in range(NT):
                    nc.vector.bn_stats(stats[:, j], xc[:, half, j, :]).then_inc(stats_done, 1)
                dve.wait_ge(stats_done, NT * (ck + 1))
                nc.vector.memset(std[:, :], 0.0)
                for j in range(NT):
                    nc.vector.bn_aggr(mv[:, j], stats[:, j]).then_inc(var_ready, 1)
                dve.wait_ge(std_ready, ck + 1)
                nc.vector.reciprocal(rstd[:, :], std[:, :]).then_inc(rstd_ready, 1)
                dve.wait_ge(rstd_ready, ck + 1)
                if not first:
                    dve.wait_ge(turned, CC * ck)
                for j in range(NT):
                    nc.vector.tensor_scalar(xn[:, j], xc[:, half, j, :], mv[:, j, 0:1], rstd[:, j:j + 1],
                                            ALU.subtract, ALU.mult).then_inc(xn_ready, 1)

            def rotate(ck, half, r):
                w, g, n = r // 2, r % 2, 4 * ck + r
                dve.wait_ge(pair_ready, n + 1)
                cos, sin = (rope[:, k, half * CH:(half + 1) * CH] for k in range(2))
                for k, (e, table) in enumerate(((0, cos), (1, sin), (1, cos), (0, sin))):
                    nc.vector.scalar_tensor_tensor(out=prod[:, r % 2, k], in0=ps_pair[r % 2][e][:, :], scalar=blat[:, w, e, g:g + 1],
                                                   in1=table, op0=ALU.add, op1=ALU.mult).then_inc(products, 1)
                dve.wait_ge(products, 4 * (n + 1))
                nc.vector.tensor_tensor(rot[:, r % 2, 0], prod[:, r % 2, 0], prod[:, r % 2, 1], ALU.subtract).then_inc(rot_ready, 1)
                nc.vector.tensor_tensor(rot[:, r % 2, 1], prod[:, r % 2, 2], prod[:, r % 2, 3], ALU.add).then_inc(rot_ready, 1)

            def low(ck, r):
                w, n = r // 2, 4 * ck + r
                dve.wait_ge(hi_ready, 2 * (n + 1))
                for e in range(2):
                    hi, lo = out[:, r, 0, e, :].bitcast(F32), out[:, r, 1, e, :]
                    if w == 0:
                        nc.vector.scalar_tensor_tensor(out=lo, in0=ps_q[e][:, :], scalar=wqk_bias[:, e:e + 1], in1=hi,
                                                       op0=ALU.add, op1=ALU.subtract).then_inc(lo_ready, 1)
                    else:
                        nc.vector.tensor_tensor(lo, rot[:, r % 2, e], hi, ALU.subtract).then_inc(lo_ready, 1)

            def finish(b, half, first, ahead):
                ck = 2 * b + half
                rotate(ck, half, 0)
                rotate(ck, half, 1)
                low(ck, 0)
                ahead()
                low(ck, 1)
                rotate(ck, half, 2)
                rotate(ck, half, 3)
                low(ck, 2)
                low(ck, 3)
                if first:
                    dve.wait_ge(zeroed, 2)
                else:
                    dve.wait_ge(v_left, 16 * NT * ck)
                for j in range(NT):
                    dve.wait_ge(v_ready, 2 * ck + j // 2 + 1)
                    nc.vector.tensor_tensor(vt[:, j, :, 0:HD], ps_t[j // 2][:, (j % 2) * C:(j % 2 + 1) * C].rearrange("p (h d) -> p h d", h=H),
                                            bv, ALU.add).then_inc(v_used, 1)

            over_chunks_ahead(dve, begin, finish)

        @block.scalar
        def _(act):
            def begin(b, half, first, between=lambda: None):
                ck = 2 * b + half
                act.wait_ge(var_ready, NT * (ck + 1))
                nc.scalar.activation(std[:, :], mv[:, :, 1], ACT.Sqrt, bias=eps).then_inc(std_ready, 1)
                between()
                if beyond_first_batch(b):
                    act.wait_ge(v_ready, 2 * (ck - 1))
                for cc in range(CC):
                    act.wait_ge(turned, CC * ck + cc + 1)
                    nc.scalar.copy(xT[:, half, cc, :], ps_t[cc][:, :]).then_inc(xT_ready, 1)

            def high(ck, r, first):
                w, n = r // 2, 4 * ck + r
                if w == 0:
                    act.wait_ge(q_ready, 2 * ck + r + 1)
                else:
                    act.wait_ge(rot_ready, 2 * (n + 1))
                if not first:
                    act.wait_ge(out_left[r], 64 * ck)
                for e in range(2):
                    if w == 0:
                        ins = nc.scalar.activation(out[:, r, 0, e, :], ps_q[e][:, :], ACT.Identity, bias=wqk_bias[:, e:e + 1])
                    else:
                        ins = nc.scalar.copy(out[:, r, 0, e, :], rot[:, r % 2, e])
                    ins.then_inc(hi_ready, 1)

            def finish(b, half, first, ahead):
                ck = 2 * b + half
                high(ck, 0, first)
                if not ahead(lambda: high(ck, 1, first)):
                    high(ck, 1, first)
                for r in range(2, 4):
                    high(ck, r, first)

            over_chunks_ahead(act, begin, finish)

        @block.tensor
        def _(pe):
            def begin(b, half, first):
                ck = 2 * b + half
                pe.wait_ge(xn_ready, NT * (ck + 1))
                if beyond_first_batch(b):
                    pe.wait_ge(v_used, NT * (ck - 1))
                for cc in range(CC):
                    for j in range(NT):
                        last = nc.tensor.transpose(ps_t[cc][:, j * P:(j + 1) * P], xn[:, j, cc * P:(cc + 1) * P], ident)
                    last.then_inc(turned, 1)

            def finish(b, half, first, ahead):
                ck = 2 * b + half
                pe.wait_ge(xT_ready, CC * (ck + 1))

                def pair(r):
                    w, g, n = r // 2, r % 2, 4 * ck + r
                    if not (first and r < 2):
                        pe.wait_ge(products, 4 * (n - 1))
                    for e in range(2):
                        for cc in range(CC):
                            last = nc.tensor.matmul(ps_pair[r % 2][e][:, :], wlat[:, cc, w, e, g, :], xT[:, half, cc, :],
                                                    start=(cc == 0), stop=(cc == CC - 1))
                    last.then_inc(pair_ready, 1)

                def apply_wqk(r):
                    n = 4 * ck + r
                    pe.wait_ge(rot_ready, 2 * (n + 1))
                    if r == 1:
                        pe.wait_ge(lo_ready, 2 * n)
                    elif not first:
                        pe.wait_ge(lo_ready, 2 * (n - 2))
                    for o in range(2):
                        for e in range(2):
                            last = nc.tensor.matmul(ps_q[o][:, :], wqk[:, o, e, :], rot[:, r % 2, e], start=(e == 0), stop=(e == 1))
                    last.then_inc(q_ready, 1)

                pair(0)
                pair(1)
                apply_wqk(0)
                pair(2)
                apply_wqk(1)
                if ahead():
                    pair(3)
                    pe.wait_ge(xT_ready, CC * (ck + 2))
                else:
                    pair(3)
                    pe.wait_ge(v_used, NT * ck)
                for j in range(NT):
                    for cc in range(CC):
                        last = nc.tensor.matmul(ps_t[j // 2][:, (j % 2) * C:(j % 2 + 1) * C], xT[:, half, cc, j * P:(j + 1) * P], wv[:, cc, :],
                                                start=(cc == 0), stop=(cc == CC - 1))
                    if j % 2:
                        last.then_inc(v_ready, 1)

            over_chunks_ahead(pe, begin, finish)


def between_attentions(nc, t, x, os, cst, wout, cout, x1, n1, qk, vs):
    ps_t = [t.psum(f"mi_t{n}", [P, CH]) for n in range(2)]
    ps_y = [t.psum(f"mi_y{n}", [P, CH]) for n in range(2)]
    ps_p = [t.psum(f"mi_p{n}", [P, CH]) for n in range(4)]
    oc = t.sbuf("mi_o", [P, 2, NT, C])
    xc = t.sbuf("mi_x", [P, 2, NT, C])
    oT = t.sbuf("mi_oT", [P, CC, CH])
    nT = t.sbuf("mi_nT", [P, CC, CH])
    y = t.sbuf("mi_y", [P, NT, C])
    yn = t.sbuf("mi_yn", [P, NT, C])
    x1c = t.sbuf("mi_x1", [P, NT, C])
    n1c = t.sbuf("mi_n1", [P, NT, C])
    stats = t.sbuf("mi_stats", [P, 2, NT, 6])
    mv = t.sbuf("mi_mv", [P, 2, NT, 2])
    std = t.sbuf("mi_std", [P, 2, NT])
    rstd = t.sbuf("mi_rstd", [P, 2, NT])
    out = t.sbuf("mi_out", [P, 4, 2, CH], F32R)
    vt = t.sbuf("mi_v", [P, NT, H, 2 * HD])
    names = ("turned", "oT_ready", "y_ready", "y_used", "nT_ready", "n_turned", "p_ready", "hi_ready", "lo_ready", "v_ready", "v_used",
             "yn_ready", "x1_ready", "n1_ready", "zeroed")
    turned, oT_ready, y_ready, y_used, nT_ready, n_turned, p_ready, hi_ready, lo_ready, v_ready, v_used, yn_ready, x1_ready, \
        n1_ready, zeroed = (t.sem("mi_" + n) for n in names)
    stats_done, var_ready, std_ready, rstd_ready = ([t.sem(f"mi_{n}{k}") for k in range(2)] for n in ("stats", "var", "std", "rstd"))
    o_in, x_in = ([t.sem(f"mi_{n}_in{k}") for k in range(2)] for n in "ox")
    out_left = [t.sem(f"mi_out_left{r}") for r in range(4)]
    v_left, x1_left, n1_left = (t.sem(f"mi_{n}_left") for n in ("v", "x1", "n1"))
    ident, eps = const(cst, "ident"), const(cst, "eps")
    wqkv = const(cst, "wqkv2").rearrange("p (c n) -> p c n", c=CC)
    tiles = lambda a: a.rearrange("b (s j p) c -> (b s) p j c", s=2, p=P)
    xt = tiles(x)
    x1t = tiles(x1)
    n1t = tiles(n1)
    chunks = 2 * B
    HG = H // 4

    with nc.Block() as block:
        @block.sync
        def _(sp):
            def load(b, half):
                for hg in range(HG):
                    sp.dma_start(oc[:, half, :, hg * 4 * HD:(hg + 1) * 4 * HD],
                                 os[bass.ds(2 * (b * HG + hg) + half, 1)].rearrange("a p q d -> p (a q) d")).then_inc(o_in[half], 16)
                sp.dma_start(xc[:, half], xt[bass.ds(2 * b + half, 1)].rearrange("a p j c -> p (a j) c")).then_inc(x_in[half], 16)

            for half in range(2):
                load(0, half)

            def chunk(b, half, more):
                ck = 2 * b + half
                sp.wait_ge(x1_ready, ck + 1)
                if more:
                    load(b + 1, half)
                sp.dma_start(x1t[bass.ds(ck, 1)].rearrange("a p j c -> p (a j) c"), x1c[:, :, :]).then_inc(x1_left, 16)
                sp.wait_ge(n1_ready, NT * (ck + 1))
                sp.dma_start(n1t[bass.ds(ck, 1)].rearrange("a p j c -> p (a j) c"), n1c[:, :, :]).then_inc(n1_left, 16)
                for r in range(4):
                    w, g = r // 2, r % 2
                    sp.wait_ge(lo_ready, 4 * ck + r + 1)
                    for hl in range(2):
                        dst = qk[w][hl][bass.ds(b * H + g * 8, 8), 0:HD, half * CH:(half + 1) * CH]
                        sp.dma_start(dst, out[:, r, hl, :].bitcast(F32)).then_inc(out_left[r], 16)
                sp.wait_ge(v_used, 2 * (ck + 1))
                for j in range(NT):
                    kb = half * NT + j
                    dst = vs[bass.ds(b * H, H), :, kb * 2 * HD:(kb + 1) * 2 * HD].rearrange("h p e -> p h e")
                    sp.dma_start(dst, vt[:, j]).then_inc(v_left, 16)

            with sp.Fori(0, B - 1) as b:
                for half in range(2):
                    chunk(b, half, True)
            for half in range(2):
                chunk(B - 1, half, False)
            for r in range(4):
                sp.wait_ge(out_left[r], 16 * 2 * chunks)
            sp.wait_ge(v_left, 16 * NT * chunks)
            sp.wait_ge(x1_left, 16 * chunks)
            sp.wait_ge(n1_left, 16 * chunks)

        @block.vector
        def _(dve):
            nc.vector.memset(vt[:, :, :, HD + 1:], 0.0).then_inc(zeroed, 1)
            nc.vector.memset(vt[:, :, :, HD:HD + 1], 1.0).then_inc(zeroed, 1)

            def norm(ck, k, src, dst, ready):
                for j in range(NT):
                    nc.vector.bn_stats(stats[:, k, j], src[:, j, :]).then_inc(stats_done[k], 1)
                dve.wait_ge(stats_done[k], NT * (ck + 1))
                nc.vector.memset(std[:, k, :], 0.0)
                for j in range(NT):
                    nc.vector.bn_aggr(mv[:, k, j], stats[:, k, j]).then_inc(var_ready[k], 1)
                dve.wait_ge(std_ready[k], ck + 1)
                nc.vector.reciprocal(rstd[:, k, :], std[:, k, :]).then_inc(rstd_ready[k], 1)
                dve.wait_ge(rstd_ready[k], ck + 1)
                for j in range(NT):
                    nc.vector.tensor_scalar(dst[:, j], src[:, j], mv[:, k, j, 0:1], rstd[:, k, j:j + 1], ALU.subtract, ALU.mult).then_inc(ready, 1)

            def begin(b, half, first):
                ck = 2 * b + half
                for k in range(2):
                    dve.wait_ge(y_ready, 2 * ck + k + 1)
                    nc.vector.tensor_tensor(y[:, 2 * k:2 * k + 2], ps_y[k][:, :].rearrange("p (j n) -> p j n", j=2),
                                            cout[:, :].unsqueeze(1).to_broadcast([P, 2, C]), ALU.add).then_inc(y_used, 1)
                dve.wait_ge(y_used, 2 * (ck + 1))
                norm(ck, 0, y, yn, yn_ready)
                dve.wait_ge(yn_ready, NT * (ck + 1))
                dve.wait_ge(x_in[half], 16 * (b + 1))
                if not first:
                    dve.wait_ge(x1_left, 16 * ck)
                nc.vector.tensor_tensor(x1c[:, :, :], xc[:, half], yn[:, :, :], ALU.add).then_inc(x1_ready, 1)
                dve.wait_ge(x1_ready, ck + 1)
                if not first:
                    dve.wait_ge(n1_left, 16 * ck)
                norm(ck, 1, x1c, n1c, n1_ready)

            def finish(b, half, first, ahead):
                ck = 2 * b + half
                ahead()
                for r in range(4):
                    n = 4 * ck + r
                    dve.wait_ge(hi_ready, n + 1)
                    nc.vector.tensor_tensor(out[:, r, 1, :], ps_p[r][:, :], out[:, r, 0, :].bitcast(F32), ALU.subtract).then_inc(lo_ready, 1)
                if first:
                    dve.wait_ge(zeroed, 2)
                else:
                    dve.wait_ge(v_left, 16 * NT * ck)
                for k in range(2):
                    dve.wait_ge(v_ready, 2 * ck + k + 1)
                    nc.vector.tensor_copy(vt[:, 2 * k:2 * k + 2, :, 0:HD],
                                          ps_y[k][:, :].rearrange("p (j h d) -> p j h d", j=2, h=H)).then_inc(v_used, 1)

            over_chunks_ahead(dve, begin, finish)

        @block.scalar
        def _(act):
            def deviation(ck, k):
                act.wait_ge(var_ready[k], NT * (ck + 1))
                nc.scalar.activation(std[:, k, :], mv[:, k, :, 1], ACT.Sqrt, bias=eps).then_inc(std_ready[k], 1)

            def take_transposed(ck, src_turned, dst, done):
                for cc in range(CC):
                    act.wait_ge(src_turned, CC * ck + cc + 1)
                    nc.scalar.copy(dst[:, cc, :], ps_t[cc][:, :]).then_inc(done, 1)

            def high(ck, r, first):
                act.wait_ge(p_ready, 4 * ck + r + 1)
                if not first:
                    act.wait_ge(out_left[r], 32 * ck)
                nc.scalar.copy(out[:, r, 0, :], ps_p[r][:, :]).then_inc(hi_ready, 1)

            def begin(ck, before):
                take_transposed(ck, turned, oT, oT_ready)
                deviation(ck, 0)
                for r in range(2):
                    before(r)
                deviation(ck, 1)
                for r in range(2, 4):
                    before(r)
                take_transposed(ck, n_turned, nT, nT_ready)

            begin(0, lambda r: None)
            begin(1, lambda r: high(0, r, True))
            begin(2, lambda r: high(1, r, False))
            with act.Fori(1, B - 1) as b:
                for half in range(2):
                    begin(2 * b + half + 1, lambda r: high(2 * b + half, r, False))
            begin(2 * B - 1, lambda r: high(2 * B - 2, r, False))
            for r in range(4):
                high(2 * B - 1, r, False)

        @block.tensor
        def _(pe):
            def turn(src, done):
                for cc in range(CC):
                    for j in range(NT):
                        last = nc.tensor.transpose(ps_t[cc][:, j * P:(j + 1) * P], src[:, j, cc * P:(cc + 1) * P], ident)
                    last.then_inc(done, 1)

            def begin(b, half, first):
                ck = 2 * b + half
                pe.wait_ge(o_in[half], 16 * HG * (b + 1))
                if not first:
                    pe.wait_ge(nT_ready, CC * ck)
                turn(oc[:, half], turned)
                pe.wait_ge(oT_ready, CC * (ck + 1))
                if beyond_first_batch(b):
                    pe.wait_ge(v_used, 2 * (ck - 1))
                for j in range(NT):
                    for cc in range(CC):
                        last = nc.tensor.matmul(ps_y[j // 2][:, (j % 2) * C:(j % 2 + 1) * C], oT[:, cc, j * P:(j + 1) * P], wout[:, cc, :],
                                                start=(cc == 0), stop=(cc == CC - 1))
                    if j % 2:
                        last.then_inc(y_ready, 1)

            def turn_n1(ck):
                pe.wait_ge(n1_ready, NT * (ck + 1))
                turn(n1c, n_turned)

            def finish(b, half, first, ahead):
                ck = 2 * b + half
                if first:
                    turn_n1(0)
                pe.wait_ge(nT_ready, CC * (ck + 1))
                more = ahead()
                for r in range(4):
                    if not first:
                        pe.wait_ge(lo_ready, 4 * (ck - 1) + r + 1)
                    for cc in range(CC):
                        last = nc.tensor.matmul(ps_p[r][:, :], wqkv[:, cc, r * P:(r + 1) * P], nT[:, cc, :], start=(cc == 0), stop=(cc == CC - 1))
                    last.then_inc(p_ready, 1)
                if more:
                    pe.wait_ge(y_used, 2 * (ck + 2))
                else:
                    pe.wait_ge(v_used, 2 * ck)
                for j in range(NT):
                    for cc in range(CC):
                        last = nc.tensor.matmul(ps_y[j // 2][:, (j % 2) * C:(j % 2 + 1) * C], nT[:, cc, j * P:(j + 1) * P], wqkv[:, cc, 2 * C:],
                                                start=(cc == 0), stop=(cc == CC - 1))
                    if j % 2:
                        last.then_inc(v_ready, 1)
                if more:
                    turn_n1(ck + 1)

            over_chunks_ahead(pe, begin, finish)


def after_attentions(nc, t, n1, os, cst, h, logits):
    ps_t = [t.psum(f"af_t{n}", [P, CH]) for n in range(2)]
    ps_y = [t.psum(f"af_y{n}", [P, CH]) for n in range(2)]
    ps_l = t.psum("af_l", [P, NT, E])
    oc = t.sbuf("af_o", [P, 2, NT, C])
    nc1 = t.sbuf("af_n", [P, 2, NT, C])
    oT = t.sbuf("af_oT", [P, CC, CH])
    hT = t.sbuf("af_hT", [P, CC, CH])
    y = t.sbuf("af_y", [P, NT, C])
    yn = t.sbuf("af_yn", [P, NT, C])
    yg = t.sbuf("af_yg", [P, NT, C])
    hc = t.sbuf("af_h", [P, 2, NT, C])
    stats = t.sbuf("af_stats", [P, NT, 6])
    mv = t.sbuf("af_mv", [P, NT, 2])
    std = t.sbuf("af_std", [P, NT])
    rstd = t.sbuf("af_rstd", [P, NT])
    names = ("turned", "oT_ready", "y_ready", "y_used", "stats_done", "var_ready", "std_ready", "rstd_ready", "yn_ready", "yg_ready",
             "h_ready", "h_turned", "hT_ready", "l_ready", "l_used")
    turned, oT_ready, y_ready, y_used, stats_done, var_ready, std_ready, rstd_ready, yn_ready, yg_ready, h_ready, h_turned, hT_ready, \
        l_ready, l_used = (t.sem("af_" + n) for n in names)
    o_in, n_in, h_left = ([t.sem(f"af_{n}{k}") for k in range(2)] for n in ("o_in", "n_in", "h_left"))
    ident, eps = const(cst, "ident"), const(cst, "eps")
    wo = const(cst, "wo2").rearrange("p (c n) -> p c n", c=CC)
    wg = const(cst, "wg").rearrange("p (c n) -> p c n", c=CC)
    n1t = n1.rearrange("b (s j p) c -> (b s) p j c", s=2, p=P)
    ht = h.rearrange("b (s j p) c -> (b s) p j c", s=2, p=P)
    HG = H // 4
    over_tiles = lambda a: a.unsqueeze(1).to_broadcast([P, NT, C])

    with nc.Block() as block:
        @block.sync
        def _(sp):
            def load(b, half):
                for hg in range(HG):
                    sp.dma_start(oc[:, half, :, hg * 4 * HD:(hg + 1) * 4 * HD],
                                 os[bass.ds(2 * (b * HG + hg) + half, 1)].rearrange("a p q d -> p (a q) d")).then_inc(o_in[half], 16)
                sp.dma_start(nc1[:, half], n1t[bass.ds(2 * b + half, 1)].rearrange("a p j c -> p (a j) c")).then_inc(n_in[half], 16)

            for half in range(2):
                load(0, half)

            def chunk(b, half, more):
                ck = 2 * b + half
                sp.wait_ge(h_ready, ck + 1)
                if more:
                    load(b + 1, half)
                sp.dma_start(ht[bass.ds(ck, 1)].rearrange("a p j c -> p (a j) c"), hc[:, half]).then_inc(h_left[half], 16)

            with sp.Fori(0, B - 1) as b:
                for half in range(2):
                    chunk(b, half, True)
            for half in range(2):
                chunk(B - 1, half, False)
                sp.wait_ge(h_left[half], 16 * B)

        @block.vector
        def _(dve):
            def begin(b, half, first):
                ck = 2 * b + half
                dve.wait_ge(n_in[half], 16 * (b + 1))
                for k in range(2):
                    dve.wait_ge(y_ready, 2 * ck + k + 1)
                    nc.vector.tensor_tensor(y[:, 2 * k:2 * k + 2], ps_y[k][:, :].rearrange("p (j n) -> p j n", j=2),
                                            nc1[:, half, 2 * k:2 * k + 2], ALU.add).then_inc(y_used, 1)
                dve.wait_ge(y_used, 2 * (ck + 1))
                for j in range(NT):
                    nc.vector.bn_stats(stats[:, j], y[:, j, :]).then_inc(stats_done, 1)
                dve.wait_ge(stats_done, NT * (ck + 1))
                nc.vector.memset(std[:, :], 0.0)
                for j in range(NT):
                    nc.vector.bn_aggr(mv[:, j], stats[:, j]).then_inc(var_ready, 1)
                dve.wait_ge(std_ready, ck + 1)
                nc.vector.reciprocal(rstd[:, :], std[:, :]).then_inc(rstd_ready, 1)
                dve.wait_ge(rstd_ready, ck + 1)
                for j in range(NT):
                    nc.vector.tensor_scalar(yn[:, j], y[:, j], mv[:, j, 0:1], rstd[:, j:j + 1], ALU.subtract, ALU.mult).then_inc(yn_ready, 1)
                dve.wait_ge(yn_ready, NT * (ck + 1))
                nc.vector.tensor_tensor(yg[:, :, :], yn[:, :, :], over_tiles(const(cst, "g1")), ALU.mult).then_inc(yg_ready, 1)
                dve.wait_ge(yg_ready, ck + 1)
                if beyond_first_batch(b):
                    dve.wait_ge(h_left[half], 16 * b)
                nc.vector.tensor_tensor(hc[:, half], yg[:, :, :], over_tiles(const(cst, "b1")), ALU.add).then_inc(h_ready, 1)

            def finish(b, half, first, ahead):
                ck = 2 * b + half
                ahead()
                dve.wait_ge(l_ready, ck + 1)
                nc.vector.tensor_copy(logits[:, bass.ds(ck * NT, NT), :], ps_l[:, :, :]).then_inc(l_used, 1)

            over_chunks_ahead(dve, begin, finish)

        @block.scalar
        def _(act):
            def take_transposed(ck, src_turned, dst, done):
                for cc in range(CC):
                    act.wait_ge(src_turned, CC * ck + cc + 1)
                    nc.scalar.copy(dst[:, cc, :], ps_t[cc][:, :]).then_inc(done, 1)

            def deviation(ck):
                act.wait_ge(var_ready, NT * (ck + 1))
                nc.scalar.activation(std[:, :], mv[:, :, 1], ACT.Sqrt, bias=eps).then_inc(std_ready, 1)

            def step(ck):
                take_transposed(ck + 1, turned, oT, oT_ready)
                take_transposed(ck, h_turned, hT, hT_ready)
                deviation(ck + 1)

            take_transposed(0, turned, oT, oT_ready)
            deviation(0)
            step(0)
            with act.Fori(1, 2 * B - 1) as ck:
                step(ck)
            take_transposed(2 * B - 1, h_turned, hT, hT_ready)

        @block.tensor
        def _(pe):
            def begin(b, half, first):
                ck = 2 * b + half
                pe.wait_ge(o_in[half], 16 * HG * (b + 1))
                if beyond_first_batch(b):
                    pe.wait_ge(hT_ready, CC * (ck - 1))
                for cc in range(CC):
                    for j in range(NT):
                        last = nc.tensor.transpose(ps_t[cc][:, j * P:(j + 1) * P], oc[:, half, j, cc * P:(cc + 1) * P], ident)
                    last.then_inc(turned, 1)
                pe.wait_ge(oT_ready, CC * (ck + 1))
                if not first:
                    pe.wait_ge(y_used, 2 * ck)
                for j in range(NT):
                    for cc in range(CC):
                        last = nc.tensor.matmul(ps_y[j // 2][:, (j % 2) * C:(j % 2 + 1) * C], oT[:, cc, j * P:(j + 1) * P], wo[:, cc, :],
                                                start=(cc == 0), stop=(cc == CC - 1))
                    if j % 2:
                        last.then_inc(y_ready, 1)

            def finish(b, half, first, ahead):
                ck = 2 * b + half
                ahead()
                pe.wait_ge(h_ready, ck + 1)
                for cc in range(CC):
                    for j in range(NT):
                        last = nc.tensor.transpose(ps_t[cc][:, j * P:(j + 1) * P], hc[:, half, j, cc * P:(cc + 1) * P], ident)
                    last.then_inc(h_turned, 1)
                pe.wait_ge(hT_ready, CC * (ck + 1))
                if not first:
                    pe.wait_ge(l_used, ck)
                for j in range(NT):
                    for cc in range(CC):
                        last = nc.tensor.matmul(ps_l[:, j, :], hT[:, cc, j * P:(j + 1) * P], wg[:, cc, :], start=(cc == 0), stop=(cc == CC - 1))
                last.then_inc(l_ready, 1)

            over_chunks_ahead(pe, begin, finish)


def route(nc, t, cst, logits, weight, place, tile_expert):
    ps = t.psum("ro_ps", [P, 2, TT, E])
    top = t.sbuf("ro_top", [P, TT, 8])
    index = t.sbuf("ro_index", [P, TT, 8], U32)
    chosen = t.sbuf("ro_chosen", [P, TT, 2])
    onehot = t.sbuf("ro_onehot", [P, TT, 2, E])
    count = t.sbuf("ro_count", [P, TT, E])
    scan = [t.sbuf(f"ro_scan{n}", [P, TT, E]) for n in range(2)]
    loc = t.sbuf("ro_loc", [P, TT, E])
    rows = t.sbuf("ro_rows", [P, TT, 2, E])
    placef = t.sbuf("ro_placef", [P, TT, 2])
    gap = t.sbuf("ro_gap", [P, TT])
    egap = t.sbuf("ro_egap", [P, TT])
    denom = t.sbuf("ro_denom", [P, TT])
    total = t.sbuf("ro_total", [P, E])
    tiles_i = t.sbuf("ro_tiles_i", [P, E], mybir.dt.int32)
    shifted = t.sbuf("ro_shifted", [P, E], mybir.dt.int32)
    tiles = t.sbuf("ro_tiles", [P, E])
    ends = t.sbuf("ro_ends", [P, E + 1])
    passed = t.sbuf("ro_passed", [P, TILES, E])
    expf = t.sbuf("ro_expf", [P, TILES])
    step, gap_ready, egap_ready, counted, ranked = (
        t.sem("ro_" + n) for n in ("step", "gap_ready", "egap_ready", "counted", "ranked"))

    with nc.Block() as block:
        @block.scalar
        def _(act):
            act.wait_ge(gap_ready, 1)
            nc.scalar.activation(egap[:, :], gap[:, :], ACT.Exp).then_inc(egap_ready, 1)

        @block.tensor
        def _(pe):
            pe.wait_ge(counted, 1)
            flat = count[:, :, :].rearrange("p t e -> p (t e)")
            nc.tensor.matmul(ps[:, 0].rearrange("p t e -> p (t e)"), const(cst, "before"), flat, start=True, stop=True)
            nc.tensor.matmul(ps[:, 1].rearrange("p t e -> p (t e)"), const(cst, "ones"), flat, start=True, stop=True).then_inc(ranked, 1)

        @block.vector
        def _(dve):
            done = 0

            def link(ins):
                nonlocal done
                done += 1
                ins.then_inc(step, 1)
                dve.wait_ge(step, done)

            for k in range(TT):
                last = nc.vector.max(top[:, k], logits[:, k])
            link(last)
            for k in range(TT):
                last = nc.vector.max_index(index[:, k], top[:, k], logits[:, k])
            link(last)
            nc.vector.tensor_tensor(gap[:, :], top[:, :, 1], top[:, :, 0], ALU.subtract).then_inc(gap_ready, 1)
            link(nc.vector.tensor_copy(chosen[:, :, :], index[:, :, 0:2]))
            wide = lambda a: a.unsqueeze(3).to_broadcast([P, TT, 2, E])
            experts = const(cst, "expert").unsqueeze(1).to_broadcast([P, TT, E])
            for s in range(2):
                last = nc.vector.tensor_tensor(onehot[:, :, s], chosen[:, :, s].unsqueeze(2).to_broadcast([P, TT, E]), experts, ALU.is_equal)
            link(last)
            nc.vector.tensor_tensor(count[:, :, :], onehot[:, :, 0], onehot[:, :, 1], ALU.add).then_inc(counted, 1)
            dve.wait_ge(egap_ready, 1)
            link(nc.vector.tensor_scalar(denom[:, :], egap[:, :], 1.0, None, ALU.add))
            link(nc.vector.reciprocal(weight[:, :, 0], denom[:, :]))
            link(nc.vector.tensor_tensor(weight[:, :, 1], weight[:, :, 0], egap[:, :], ALU.mult))
            dve.wait_ge(ranked, 1)
            link(nc.vector.tensor_copy(scan[0][:, :, :], ps[:, 1]))
            at, k = 0, 1
            while k < TT:
                nc.vector.tensor_copy(scan[1 - at][:, 0:k], scan[at][:, 0:k])
                link(nc.vector.tensor_tensor(scan[1 - at][:, k:], scan[at][:, k:], scan[at][:, 0:TT - k], ALU.add))
                at, k = 1 - at, 2 * k
            upto = scan[at]
            link(nc.vector.tensor_scalar(total[:, :], upto[:, TT - 1], float(P - 1), None, ALU.add))
            link(nc.vector.tensor_copy(tiles_i[:, :], total[:, :]))
            link(nc.vector.tensor_single_scalar(shifted[:, :], tiles_i[:, :], 7, ALU.logical_shift_right))
            link(nc.vector.tensor_copy(tiles[:, :], shifted[:, :]))
            link(nc.vector.memset(ends[:, 0:1], 0.0))
            for e in range(E):
                link(nc.vector.tensor_tensor(ends[:, e + 1:e + 2], ends[:, e:e + 1], tiles[:, e:e + 1], ALU.add))
            link(nc.vector.tensor_tensor(loc[:, :, :], upto[:, :, :], ps[:, 1], ALU.subtract))
            link(nc.vector.tensor_tensor(loc[:, :, :], loc[:, :, :], ps[:, 0], ALU.add))
            link(nc.vector.scalar_tensor_tensor(out=loc[:, :, :], in0=ends[:, 0:E].unsqueeze(1).to_broadcast([P, TT, E]), scalar=float(P),
                                                in1=loc[:, :, :], op0=ALU.mult, op1=ALU.add))
            for s in range(2):
                last = nc.vector.tensor_tensor(rows[:, :, s], onehot[:, :, s], loc[:, :, :], ALU.mult)
            link(last)
            link(nc.vector.tensor_reduce(placef[:, :, :], rows[:, :, :, :], AX.X, ALU.add))
            link(nc.vector.tensor_copy(place[:, :, :], placef[:, :, :].rearrange("p t s -> p s t")))
            link(nc.vector.tensor_tensor(passed[:, :, :], ends[:, 1:E + 1].unsqueeze(1).to_broadcast([P, TILES, E]),
                                         const(cst, "tile").unsqueeze(2).to_broadcast([P, TILES, E]), ALU.is_le))
            link(nc.vector.tensor_reduce(expf[:, :], passed[:, :, :], AX.X, ALU.add))
            link(nc.vector.tensor_scalar(expf[:, :], expf[:, :], float(E - 1), None, ALU.min))
            pairs = expf[:, :].rearrange("p (k two) -> p k two", two=2)
            nc.vector.tensor_copy(tile_expert[:, :, 0:2], pairs)
            nc.vector.tensor_copy(tile_expert[:, 0:TILES // 2 - 1, 2:4], pairs[:, 1:, :])
            nc.vector.memset(tile_expert[:, TILES // 2 - 1:, 2:4], 0)


def scatter_and_split(nc, t, h, place, xs, w1, w2, w1s, w2s, bb_dram, bb):
    RINGS = 4
    FC = F // P
    ht = h.rearrange("b (k p) c -> (b k) p c", p=P)
    rows = [t.sbuf(f"sc_rows{n}", [P, C]) for n in range(RINGS)]
    h_in, scattered = ([t.sem(f"sc_{n}{k}") for k in range(RINGS)] for n in ("h_in", "scattered"))
    stage = [[t.sbuf(f"sw_{w}{n}", [P, CC * F]) for n in range(2)] for w in range(2)]
    w_in = [[t.sem(f"sw_in{w}{n}") for n in range(2)] for w in range(2)]
    hi, lo, bb_in = t.sem("sw_hi"), t.sem("sw_lo"), t.sem("sw_bb_in")
    src = [w1.rearrange("e (c p) f -> e p c f", p=P), w2.rearrange("e (c p) n -> e p c n", p=P)]
    views = [lambda a: a.rearrange("p (c f) -> p c f", c=CC), lambda a: a.rearrange("p (c n) -> p c n", c=FC)]
    with nc.Block() as block:
        @block.sync
        def _(sp):
            for k in range(TT):
                if k >= RINGS:
                    sp.wait_ge(scattered[k % RINGS], 32 * (k // RINGS))
                sp.dma_start(rows[k % RINGS][:, :], ht[k]).then_inc(h_in[k % RINGS], 16)
                if k % 2 == 0:
                    e, w = divmod(k // 2, 2)
                    if e >= 2:
                        sp.wait_ge(lo, 2 * (e - 2) + w + 1)
                    sp.dma_start(views[w](stage[w][e % 2][:, :]), src[w][e]).then_inc(w_in[w][e % 2], 16)
            for dst, src_bb in zip(bb, bb_dram):
                sp.dma_start(dst[:, :, :], src_bb).then_inc(bb_in, 16)
            sp.wait_ge(bb_in, 32)

        @block.gpsimd
        def _(pool):
            for k in range(TT):
                pool.wait_ge(h_in[k % RINGS], 16 * (k // RINGS + 1))
                for s in range(2):
                    nc.gpsimd.indirect_dma_start(xs, bass.IndirectOffsetOnAxis(place[:, s, k:k + 1], 0), rows[k % RINGS][:, :], None).then_inc(
                        scattered[k % RINGS], 16)
            for n in range(RINGS):
                pool.wait_ge(scattered[n], 32 * TT // RINGS)

        @block.scalar
        def _(act):
            for e in range(E):
                for w, pair in enumerate((w1s, w2s)):
                    act.wait_ge(w_in[w][e % 2], 16 * (e // 2 + 1))
                    nc.scalar.copy(pair[0][:, e].rearrange("p a b -> p (a b)"), stage[w][e % 2][:, :]).then_inc(hi, 1)

        @block.vector
        def _(dve):
            for e in range(E):
                for w, pair in enumerate((w1s, w2s)):
                    dve.wait_ge(hi, 2 * e + w + 1)
                    nc.vector.tensor_tensor(pair[1][:, e].rearrange("p a b -> p (a b)"), stage[w][e % 2][:, :],
                                            pair[0][:, e].rearrange("p a b -> p (a b)"), ALU.subtract).then_inc(lo, 1)


def experts(nc, t, cst, xs, ys, tile_expert, bb, w1s, w2s):
    FC = F // P
    HALF = FC // 2
    ps_x = t.psum("ex_x", [P, CC, P])
    ps_h = [[t.psum(f"ex_h{n}{k}", [P, HALF, P]) for k in range(2)] for n in range(2)]
    ps_y = [t.psum(f"ex_y{n}", [P, C]) for n in range(2)]
    xc = t.sbuf("ex_xc", [P, 2, C])
    xh = t.sbuf("ex_xh", [P, 2, CC, P], FP16)
    xl = t.sbuf("ex_xl", [P, 2, CC, P], BF16)
    act_f = t.sbuf("ex_gelu", [P, 2, FC, P])
    ah = t.sbuf("ex_ah", [P, 2, FC, P], FP16)
    al = t.sbuf("ex_al", [P, 2, FC, P], BF16)
    yc = t.sbuf("ex_yc", [P, 2, C])
    bb1, bb2 = bb
    ident = const(cst, "ident")
    x_in, y_left = ([t.sem(f"ex_{n}{k}") for k in range(2)] for n in ("x_in", "y_left"))
    turned, xh_ready, xl_ready, h_ready, gelu_ready, ah_ready, al_ready, y_ready, y_used = (
        t.sem("ex_" + n) for n in ("turned", "xh_ready", "xl_ready", "h_ready", "gelu_ready", "ah_ready", "al_ready", "y_ready", "y_used"))
    xst = xs.rearrange("(i p) c -> i p c", p=P)
    yst = ys.rearrange("(i p) c -> i p c", p=P)
    row = lambda a: a.rearrange("a p c -> p (a c)")
    PAIRS = TILES // 2

    def over_pairs(eng, step):
        for par in range(2):
            step(0, par, par == 0)
        with eng.Fori(1, PAIRS) as k:
            for par in range(2):
                step(k, par, False)

    def experts_of(eng, k):
        _, values = nc.values_load_multi_w_load_instructions(
            tile_expert[0:1, k, :] if isinstance(k, int) else tile_expert[0:1, bass.ds(k, 1), :].rearrange("p a e -> p (a e)"),
            engines=[eng.engine], min_val=0, max_val=E - 1, skip_runtime_bounds_check_because="route clamps them")
        return values

    with nc.Block() as block:
        @block.sync
        def _(sp):
            for par in range(2):
                sp.dma_start(xc[:, par], xst[par]).then_inc(x_in[par], 16)

            def load(k, par):
                sp.wait_ge(turned, 2 * k + par + 1)
                sp.dma_start(xc[:, par], row(xst[bass.ds(2 * (k + 1) + par, 1)])).then_inc(x_in[par], 16)

            def store(k, par):
                sp.wait_ge(y_used, 2 * k + par + 1)
                sp.dma_start(row(yst[bass.ds(2 * k + par, 1)]), yc[:, par]).then_inc(y_left[par], 16)

            for par in range(2):
                load(0, par)
            with sp.Fori(1, PAIRS - 1) as k:
                for par in range(2):
                    load(k, par)
                    store(k - 1, par)
            for k in range(PAIRS - 2, PAIRS):
                for par in range(2):
                    store(k, par)
            for par in range(2):
                sp.wait_ge(y_left[par], 16 * PAIRS)

        @block.tensor
        def _(pe):
            def turn(k, par, first):
                i = 2 * k + par
                pe.wait_ge(x_in[par], 16 * (k + 1))
                if not first:
                    pe.wait_ge(xl_ready, i)
                for cc in range(CC):
                    last = nc.tensor.transpose(ps_x[:, cc, :], xc[:, par, cc * P:(cc + 1) * P], ident)
                last.then_inc(turned, 1)

            def first_product(k, par, e, first):
                i = 2 * k + par
                pe.wait_ge(xl_ready, i + 1)
                for half in range(2):
                    if not first:
                        pe.wait_ge(gelu_ready, FC * (i - 2) + HALF * (half + 1))
                    for f in range(HALF):
                        fc = half * HALF + f
                        terms = [(w, a, cc) for cc in range(CC) for w, a in ((0, xh), (0, xl), (1, xh))]
                        for n, (w, a, cc) in enumerate(terms):
                            last = nc.tensor.matmul(ps_h[par][half][:, f, :],
                                                    w1s[w][:, bass.ds(e, 1), cc, fc * P:(fc + 1) * P].rearrange("p a f -> p (a f)"),
                                                    a[:, par, cc, :], start=(n == 0), stop=(n == len(terms) - 1))
                    last.then_inc(h_ready, 1)

            def second_product(k, par, e, first):
                i = 2 * k + par
                if not first:
                    pe.wait_ge(y_used, i - 1)
                for half in range(2):
                    pe.wait_ge(al_ready, 2 * i + half + 1)
                    for f in range(HALF):
                        fc = half * HALF + f
                        for n, (w, a) in enumerate(((0, ah), (0, al), (1, ah))):
                            last = nc.tensor.matmul(ps_y[par][:, :], a[:, par, fc, :],
                                                    w2s[w][:, bass.ds(e, 1), fc, :].rearrange("p a n -> p (a n)"),
                                                    start=(fc == 0 and n == 0), stop=(fc == FC - 1 and n == 2))
                last.then_inc(y_ready, 1)

            e = experts_of(pe, 0)
            turn(0, 0, True)
            turn(0, 1, False)
            first_product(0, 0, e[0], True)
            turn(1, 0, False)
            first_product(0, 1, e[1], True)
            second_product(0, 0, e[0], True)
            turn(1, 1, False)
            first_product(1, 0, e[2], False)
            second_product(0, 1, e[1], True)
            with pe.Fori(1, PAIRS - 1) as k:
                e = experts_of(pe, k)
                turn(k + 1, 0, False)
                first_product(k, 1, e[1], False)
                second_product(k, 0, e[0], False)
                turn(k + 1, 1, False)
                first_product(k + 1, 0, e[2], False)
                second_product(k, 1, e[1], False)
            e = experts_of(pe, PAIRS - 1)
            first_product(PAIRS - 1, 1, e[1], False)
            second_product(PAIRS - 1, 0, e[0], False)
            second_product(PAIRS - 1, 1, e[1], False)

        @block.scalar
        def _(act):
            def step(k, par, first):
                i = 2 * k + par
                act.wait_ge(turned, i + 1)
                if not (isinstance(k, int) and k == 0):
                    act.wait_ge(h_ready, 2 * (i - 1))
                nc.scalar.copy(xh[:, par], ps_x[:, :, :]).then_inc(xh_ready, 1)

            def gelu(k, par, e, first):
                i = 2 * k + par
                for half in range(2):
                    act.wait_ge(h_ready, 2 * i + half + 1)
                    if not first:
                        act.wait_ge(al_ready, 2 * (i - 2) + half + 1)
                    for f in range(HALF):
                        fc = half * HALF + f
                        nc.scalar.activation(act_f[:, par, fc, :], ps_h[par][half][:, f, :], ACT.Gelu_apprx_tanh,
                                             bias=bb1[:, bass.ds(e, 1), fc:fc + 1].rearrange("p a f -> p (a f)")).then_inc(gelu_ready, 1)

            e = experts_of(act, 0)
            step(0, 0, True)
            step(0, 1, True)
            gelu(0, 0, e[0], True)
            step(1, 0, False)
            gelu(0, 1, e[1], True)
            step(1, 1, False)
            with act.Fori(1, PAIRS - 1) as k:
                e = experts_of(act, k)
                gelu(k, 0, e[0], False)
                step(k + 1, 0, False)
                gelu(k, 1, e[1], False)
                step(k + 1, 1, False)
            e = experts_of(act, PAIRS - 1)
            gelu(PAIRS - 1, 0, e[0], False)
            gelu(PAIRS - 1, 1, e[1], False)

        @block.vector
        def _(dve):
            def low_x(k, par):
                i = 2 * k + par
                dve.wait_ge(xh_ready, i + 1)
                nc.vector.tensor_tensor(xl[:, par], ps_x[:, :, :], xh[:, par], ALU.subtract).then_inc(xl_ready, 1)

            def split(k, par, first):
                i = 2 * k + par
                for half in range(2):
                    part = slice(half * HALF, (half + 1) * HALF)
                    dve.wait_ge(gelu_ready, FC * i + HALF * (half + 1))
                    if not first and half == 0:
                        dve.wait_ge(y_ready, i - 1)
                    nc.vector.tensor_copy(ah[:, par, part], act_f[:, par, part]).then_inc(ah_ready, 1)
                    dve.wait_ge(ah_ready, 2 * i + half + 1)
                    nc.vector.tensor_tensor(al[:, par, part], act_f[:, par, part], ah[:, par, part], ALU.subtract).then_inc(al_ready, 1)

            def add_bias(k, par, e, first):
                i = 2 * k + par
                dve.wait_ge(y_ready, i + 1)
                if not first:
                    dve.wait_ge(y_left[par], 16 * k)
                nc.vector.tensor_tensor(yc[:, par], ps_y[par][:, :], bb2[:, bass.ds(e, 1), :].rearrange("p a n -> p (a n)"),
                                        ALU.add).then_inc(y_used, 1)

            e = experts_of(dve, 0)
            low_x(0, 0)
            low_x(0, 1)
            split(0, 0, True)
            low_x(1, 0)
            split(0, 1, True)
            add_bias(0, 0, e[0], True)
            low_x(1, 1)
            split(1, 0, False)
            add_bias(0, 1, e[1], True)
            with dve.Fori(1, PAIRS - 1) as k:
                e = experts_of(dve, k)
                low_x(k + 1, 0)
                split(k, 1, False)
                add_bias(k, 0, e[0], False)
                low_x(k + 1, 1)
                split(k + 1, 0, False)
                add_bias(k, 1, e[1], False)
            e = experts_of(dve, PAIRS - 1)
            split(PAIRS - 1, 1, False)
            add_bias(PAIRS - 1, 0, e[0], False)
            add_bias(PAIRS - 1, 1, e[1], False)


def combine(nc, t, cst, weight, place, ys, h, x1, out):
    y = t.sbuf("co_y", [P, TT, 2, C])
    hc = t.sbuf("co_h", [P, TT, C])
    xc = t.sbuf("co_x", [P, TT, C])
    part = t.sbuf("co_part", [P, NT, C])
    s = t.sbuf("co_sum", [P, NT, C])
    norm1 = t.sbuf("co_norm", [P, NT, C])
    gained = t.sbuf("co_gained", [P, NT, C])
    v = t.sbuf("co_v", [P, NT, C])
    vn = t.sbuf("co_vn", [P, NT, C])
    result = t.sbuf("co_result", [P, 2, NT, C])
    stats = t.sbuf("co_stats", [P, 2, NT, 6])
    mv = t.sbuf("co_mv", [P, 2, NT, 2])
    std = t.sbuf("co_std", [P, 2, NT])
    rstd = t.sbuf("co_rstd", [P, 2, NT])
    y_in, h_in, x_in, left = ([t.sem(f"co_{n}{k}") for k in range(2)] for n in ("y_in", "h_in", "x_in", "left"))
    part_ready, sum_ready, n_ready, gained_ready, v_ready, vn_ready, ready = (
        t.sem("co_" + n) for n in ("part_ready", "sum_ready", "n_ready", "gained_ready", "v_ready", "vn_ready", "ready"))
    stats_done, var_ready, std_ready, rstd_ready = ([t.sem(f"co_{n}{k}") for k in range(2)] for n in ("stats", "var", "std", "rstd"))
    eps = const(cst, "eps")
    tiles = lambda a: a.rearrange("b (s j p) c -> (b s) p j c", s=2, p=P)
    one = lambda a: a.rearrange("a p j c -> p (a j) c")
    over_tiles = lambda a: a.unsqueeze(1).to_broadcast([P, NT, C])
    chunks = 2 * B

    with nc.Block() as block:
        @block.gpsimd
        def _(pool):
            for ck in range(chunks):
                if ck >= 2:
                    pool.wait_ge(y_in[ck % 2], 16 * 2 * NT * (ck // 2))
                for j in range(NT):
                    for e in range(2):
                        nc.gpsimd.indirect_dma_start(y[:, ck * NT + j, e, :], None, ys,
                                                     bass.IndirectOffsetOnAxis(place[:, e, ck * NT + j:ck * NT + j + 1], 0)).then_inc(y_in[ck % 2], 16)

        @block.sync
        def _(sp):
            for ck in range(chunks):
                for src, dst, arrived in ((h, hc, h_in[ck % 2]), (x1, xc, x_in[ck % 2])):
                    if ck >= 2:
                        sp.wait_ge(arrived, 16 * (ck // 2))
                    sp.dma_start(dst[:, ck * NT:(ck + 1) * NT, :], tiles(src)[ck]).then_inc(arrived, 16)
            with sp.Fori(0, B) as b:
                for half in range(2):
                    sp.wait_ge(ready, 2 * b + half + 1)
                    sp.dma_start(one(tiles(out)[bass.ds(2 * b + half, 1)]), result[:, half]).then_inc(left[half], 16)
            for half in range(2):
                sp.wait_ge(left[half], 16 * B)

        def over_steps(eng, step):
            step(None, (0, 0))
            step((0, 0), (0, 1))
            step((0, 1), (1, 0))
            with eng.Fori(1, B - 1) as b:
                step((b, 0), (b, 1))
                step((b, 1), (b + 1, 0))
            step((B - 1, 0), (B - 1, 1))
            step((B - 1, 1), None)

        @block.scalar
        def _(act):
            def step(old, new):
                for k, chunk in ((0, new), (1, old)):
                    if chunk:
                        b, half = chunk
                        act.wait_ge(var_ready[k], NT * (2 * b + half + 1))
                        nc.scalar.activation(std[:, k, :], mv[:, k, :, 1], ACT.Sqrt, bias=eps).then_inc(std_ready[k], 1)

            over_steps(act, step)

        @block.vector
        def _(dve):
            def sum_up(b, half):
                ck = 2 * b + half
                dve.wait_ge(h_in[half], 16 * (b + 1))
                dve.wait_ge(y_in[half], 16 * 2 * NT * (b + 1))
                share = lambda j, e: weight[:, bass.ds(ck * NT + j, 1), e]
                h_row = lambda j: hc[:, bass.ds(ck * NT + j, 1), :].rearrange("p a c -> p (a c)")
                row = lambda j, e: y[:, bass.ds(ck * NT + j, 1), e, :].rearrange("p a c -> p (a c)")
                for j in range(NT):
                    nc.vector.scalar_tensor_tensor(out=part[:, j], in0=row(j, 0), scalar=share(j, 0), in1=h_row(j),
                                                   op0=ALU.mult, op1=ALU.add).then_inc(part_ready, 1)
                dve.wait_ge(part_ready, NT * (ck + 1))
                for j in range(NT):
                    nc.vector.scalar_tensor_tensor(out=s[:, j], in0=row(j, 1), scalar=share(j, 1), in1=part[:, j],
                                                   op0=ALU.mult, op1=ALU.add).then_inc(sum_ready, 1)

            def apply_gain(b, half):
                ck = 2 * b + half
                nc.vector.tensor_tensor(gained[:, :, :], norm1[:, :, :], over_tiles(const(cst, "g2")), ALU.mult).then_inc(gained_ready, 1)
                dve.wait_ge(gained_ready, ck + 1)
                nc.vector.tensor_tensor(v[:, :, :], gained[:, :, :], over_tiles(const(cst, "b2")), ALU.add).then_inc(v_ready, 1)

            def step(old, new):
                norms = []
                if new:
                    norms.append((2 * new[0] + new[1], 0, s, norm1, sum_ready, NT, n_ready))
                if old:
                    norms.append((2 * old[0] + old[1], 1, v, vn, v_ready, 1, vn_ready))
                if old:
                    dve.wait_ge(n_ready, NT * (2 * old[0] + old[1] + 1))
                if new:
                    sum_up(*new)
                if old:
                    apply_gain(*old)
                for ck, k, src, dst, src_ready, per_chunk, dst_ready in norms:
                    dve.wait_ge(src_ready, per_chunk * (ck + 1))
                    for j in range(NT):
                        nc.vector.bn_stats(stats[:, k, j], src[:, j, :]).then_inc(stats_done[k], 1)
                for ck, k, src, dst, src_ready, per_chunk, dst_ready in norms:
                    dve.wait_ge(stats_done[k], NT * (ck + 1))
                    nc.vector.memset(std[:, k, :], 0.0)
                    for j in range(NT):
                        nc.vector.bn_aggr(mv[:, k, j], stats[:, k, j]).then_inc(var_ready[k], 1)
                for ck, k, src, dst, src_ready, per_chunk, dst_ready in norms:
                    dve.wait_ge(std_ready[k], ck + 1)
                    nc.vector.reciprocal(rstd[:, k, :], std[:, k, :]).then_inc(rstd_ready[k], 1)
                for ck, k, src, dst, src_ready, per_chunk, dst_ready in norms:
                    dve.wait_ge(rstd_ready[k], ck + 1)
                    for j in range(NT):
                        nc.vector.tensor_scalar(dst[:, j], src[:, j], mv[:, k, j, 0:1], rstd[:, k, j:j + 1], ALU.subtract, ALU.mult).then_inc(dst_ready, 1)
                if old:
                    b, half = old
                    dve.wait_ge(vn_ready, NT * (2 * b + half + 1))
                    dve.wait_ge(x_in[half], 16 * (b + 1))
                    if beyond_first_batch(b):
                        dve.wait_ge(left[half], 16 * b)
                    nc.vector.tensor_tensor(result[:, half], xc[:, bass.ds((2 * b + half) * NT, NT), :], vn[:, :, :], ALU.add).then_inc(ready, 1)

            over_steps(dve, step)


GROUP = 4
UNITS = 12
STEPS = GROUP * UNITS
SETS = 3
SLOTS = SETS * GROUP
LAG = 3

ROWS = [(qt, 0, P * (qt + 1)) for qt in range(4)] + \
       [x for qt in range(4, KB) for x in ((qt, 0, 512), (qt, 4, P * (qt - 3)))]
COLUMNS = [(qc, j, max(512 * qc, P * j)) for qc in range(2) for j in range(4 * qc + 4)]

START, END = 0, 44
STEP_COST = [300 + 512 * (COLUMNS[s // GROUP][0] + 1) - COLUMNS[s // GROUP][2] for s in range(STEPS)]
PIECE_COST = [60 + ROWS[k % UNITS][2] for k in range(STEPS)]


def step_of(k):
    share = sum(PIECE_COST[:k]) / sum(PIECE_COST)
    return max(s for s in range(START, END) if sum(STEP_COST[START:s]) <= share * sum(STEP_COST[START:END]))


MAXIMA_AT = [[k for k in range(STEPS) if step_of(k) == s] for s in range(STEPS)]
TURN_AT = [step_of(UNITS * h + UNITS - 1) + (5, 5, 5, 2)[h] for h in range(GROUP)]
TAKE_LAST, TURN_LAST, NORM_LAST = 4, 6, 8
TAKE_FIRST, TURN_FIRST, NORM_FIRST = 20, 22, 24


def attention(nc, t, name, cst, masks, qk, vs, part_rows, scale, os, xs=None):
    FILLS = 8
    if xs is not None:
        zeros = t.sbuf(f"{name}_zeros", [P, TILES * C // FILLS])
        blank, filled = t.sem(f"{name}_blank"), t.sem(f"{name}_filled")
    ps_s = [t.psum(f"{name}_s{n}", [P, 512]) for n in range(3)]
    ps_st = [t.psum(f"{name}_st{n}", [P, 512]) for n in range(2)]
    ps_o = [t.psum(f"{name}_o{n}", [P, 512]) for n in range(2)]
    ps_m = t.psum(f"{name}_m", [P, 512])
    stack = [[t.sbuf(f"{name}_{w}{n}", [98, T], F32R) for n in range(SLOTS)] for w in "qk"]
    vh = t.sbuf(f"{name}_v", [P, SLOTS, KB, 2 * HD])
    prob = t.sbuf(f"{name}_p", [P, GROUP, 2, 512])
    maxima = t.sbuf(f"{name}_mx", [P, 2, UNITS])
    split = t.sbuf(f"{name}_split", [P, 2, 2, KB], F32R)
    mrow = t.sbuf(f"{name}_mrow", [2 * KB, SLOTS, P], F32R)
    oT = t.sbuf(f"{name}_oT", [P, 2, 512])
    recip = t.sbuf(f"{name}_recip", [P, 2, 4, 4])
    ob = t.sbuf(f"{name}_ob", [P, 2, 4, 4, HD])
    ident = const(cst, "ident")
    ident_b, mask_rows, mask_cols = masks[:, 0], masks[:, 1], masks[:, 2]

    loaded = [t.sem(f"{name}_loaded{n}") for n in range(SLOTS)]
    v_in = [t.sem(f"{name}_v_in{n}") for n in range(SETS)]
    mrow_in = [t.sem(f"{name}_mrow_in{n}") for n in range(SLOTS)]
    stored = t.sem(f"{name}_stored")
    q_zeroed, k_zeroed, s_ready, s_reduced, st_ready, p_ready, pv_done = (
        t.sem(f"{name}_" + n) for n in ("q_zeroed", "k_zeroed", "s_ready", "s_reduced", "st_ready", "p_ready", "pv_done"))
    joined, high, split_ready, mT_ready, mrow_ready = (
        t.sem(f"{name}_" + n) for n in ("joined", "high", "split_ready", "mT_ready", "mrow_ready"))
    oT_ready, o_turned, recip_ready, o_ready = (t.sem(f"{name}_" + n) for n in ("oT_ready", "o_turned", "recip_ready", "o_ready"))
    LOADS = 16 * 6
    groups = NH // GROUP

    nc.disable_value_cache = True

    def over_groups(eng, body):
        body(0, 0, 0, 1, 0, True, False)
        with eng.Fori(0, groups // SETS - 1) as k:
            body(3 * k + 1, 1, k, 2, k, False, False)
            body(3 * k + 2, 2, k, 0, k + 1, False, False)
            body(3 * k + 3, 0, k + 1, 1, k + 1, False, False)
        for g in range(groups - SETS, groups):
            body(g, g % SETS, g // SETS, (g + 1) % SETS, (g + 1) // SETS, False, g == groups - 1)

    def held(eng, value):
        return value if isinstance(value, int) else eng.compute_val(value)

    with nc.Block() as block:
        @block.sync
        def _(sp):
            def wait_zeroed(slot):
                sp.wait_ge(q_zeroed, slot + 1)
                if part_rows < 32:
                    sp.wait_ge(k_zeroed, slot + 1)

            def load(g, par, h):
                slot = GROUP * par + h
                for part, parts in enumerate(((0, 0), (0, 1), (1, 0))):
                    for w, hl in enumerate(parts):
                        src = qk[w][hl][bass.ds(GROUP * g + h, 1), 0:part_rows, :].rearrange("a r t -> (a r) t")
                        sp.dma_start(stack[w][slot][32 * part:32 * part + part_rows, :].bitcast(F32), src).then_inc(loaded[slot], 16)

            def load_v(g, par):
                for h in range(GROUP):
                    sp.dma_start(vh[:, GROUP * par + h], vs[bass.ds(GROUP * g + h, 1), :, :].rearrange("a p (k e) -> p (a k) e", e=2 * HD)).then_inc(
                        v_in[par], 16)

            def rows(m, slot):
                sp.wait_ge(mrow_ready, m + 1)
                for k in range(2):
                    sp.dma_start(stack[0][slot][96 + k:97 + k, :].bitcast(F32), mrow[k * KB:(k + 1) * KB, slot, :].bitcast(F32)).then_inc(mrow_in[slot], 16)

            def store(g, qc):
                sp.wait_ge(o_ready, 2 * g + qc + 1)
                sp.dma_start(os[bass.ds(g * 2 + qc, 1)].rearrange("a p q d -> p (a q) d"),
                             ob[:, qc].rearrange("p q h d -> p q (h d)")).then_inc(stored, 16)

            def body(g, par, own, nxt, nxt_own, first, last):
                free = (par + 2) % SETS
                loads = not (isinstance(g, int) and g + 2 >= groups)
                if first:
                    for h in range(GROUP):
                        rows(h, h)
                if loads:
                    for h in range(GROUP):
                        if first:
                            wait_zeroed(GROUP * free + h)
                        elif h == 0:
                            sp.wait_ge(st_ready, STEPS * g)
                        load(g + 2, free, h)
                        if h == 1 and not first:
                            store(g - 1, 1)
                    if not first:
                        sp.wait_ge(pv_done, UNITS * g)
                    load_v(g + 2, free)
                else:
                    store(g - 1, 1)
                for h in range(GROUP):
                    if h == 1:
                        store(g, 0)
                    if not last:
                        rows(GROUP * (g + 1) + h, GROUP * nxt + h)

            for g in range(2):
                for h in range(GROUP):
                    wait_zeroed(GROUP * g + h)
                    load(g, g, h)
                load_v(g, g)
            over_groups(sp, body)
            store(groups - 1, 1)
            sp.wait_ge(stored, 16 * 2 * groups)

        @block.gpsimd
        def _(pool):
            for n in range(SLOTS):
                if part_rows < 32:
                    nc.gpsimd.memset(stack[0][n][0:96, :].bitcast(F32), 0.0)
                nc.gpsimd.memset(stack[1][n][96:98, :].bitcast(F32), -1.0).then_inc(q_zeroed, 1)
            if xs is not None:
                pool.wait_ge(q_zeroed, SLOTS)
                nc.gpsimd.memset(zeros[:, :], 0.0).then_inc(blank, 1)
                pool.wait_ge(blank, 1)
                for n in range(FILLS):
                    pool.dma_start(xs.rearrange("(n p r) c -> n p (r c)", n=FILLS, p=P)[n], zeros[:, :]).then_inc(filled, 16)
                pool.wait_ge(filled, 16 * FILLS)

        @block.vector
        def _(dve):
            def reduce(G, before, k):
                u = k % UNITS
                qt, k0, width = ROWS[u]
                dve.wait_ge(s_ready, before + k + 1)
                nc.vector.tensor_reduce(maxima[:, k // UNITS % 2, u:u + 1], ps_s[k % 3][:, 0:width], AX.X, ALU.max).then_inc(s_reduced, 1)
                if u == UNITS - 1:
                    join(GROUP * G + k // UNITS, k // UNITS % 2)

            def join(m, parity):
                dve.wait_ge(s_reduced, UNITS * (m + 1))
                two = maxima[:, parity, 4:UNITS].rearrange("p (q k) -> p q k", k=2)
                nc.vector.tensor_tensor(maxima[:, parity, 4:8], two[:, :, 0], two[:, :, 1], ALU.max).then_inc(joined, 1)
                dve.wait_ge(joined, m + 1)
                nc.vector.tensor_copy(split[:, parity, 0], maxima[:, parity, 0:KB]).then_inc(high, 1)
                dve.wait_ge(high, m + 1)
                nc.vector.tensor_tensor(split[:, parity, 1], maxima[:, parity, 0:KB], split[:, parity, 0].bitcast(F32),
                                        ALU.subtract).then_inc(split_ready, 1)

            def take_rows(m, slot):
                dve.wait_ge(mT_ready, m + 1)
                nc.vector.tensor_copy(mrow[:, slot, :], ps_m[0:2 * KB, 0:P]).then_inc(mrow_ready, 1)

            def normalise(g, qc, first):
                dve.wait_ge(o_turned, 2 * g + qc + 1)
                o = ps_m[:, :].rearrange("p (q h e) -> p q h e", q=4, h=4)
                nc.vector.reciprocal(recip[:, qc], o[:, :, :, HD]).then_inc(recip_ready, 1)
                dve.wait_ge(recip_ready, 2 * g + qc + 1)
                if not (first and qc == 0):
                    dve.wait_ge(stored, 16 * (2 * g + qc))
                nc.vector.tensor_tensor(ob[:, qc], o[:, :, :, 0:HD], recip[:, qc].unsqueeze(3).to_broadcast([P, 4, 4, HD]),
                                        ALU.mult).then_inc(o_ready, 1)

            def body(g, par, own, nxt, nxt_own, first, last):
                ahead = held(dve, STEPS * (g + 1))
                for s in range(STEPS):
                    if not last:
                        for k in MAXIMA_AT[s]:
                            reduce(g + 1, ahead, k)
                        if s - 1 in TURN_AT:
                            h = TURN_AT.index(s - 1)
                            take_rows(GROUP * (g + 1) + h, GROUP * nxt + h)
                    if s == NORM_LAST and not first:
                        normalise(g - 1, 1, False)
                    if s == NORM_FIRST:
                        normalise(g, 0, first)

            for n in range(SLOTS):
                if part_rows < 32:
                    nc.vector.memset(stack[1][n][0:96, :].bitcast(F32), 0.0).then_inc(k_zeroed, 1)
            for k in range(STEPS):
                reduce(0, 0, k)
                if k % UNITS == 4 and k > UNITS:
                    take_rows(k // UNITS - 1, k // UNITS - 1)
            take_rows(GROUP - 1, GROUP - 1)
            over_groups(dve, body)
            normalise(groups - 1, 1, False)

        @block.scalar
        def _(act):
            def take_output(g, qc, first):
                act.wait_ge(pv_done, UNITS * g + (4 if qc == 0 else UNITS))
                if not first:
                    act.wait_ge(o_turned, 2 * g + qc)
                nc.scalar.copy(oT[:, qc, :], ps_o[qc][:, :]).then_inc(oT_ready, 1)

            def body(g, par, own, nxt, nxt_own, first, last):
                here = held(act, STEPS * g)
                for s in range(STEPS):
                    h, u = s % GROUP, s // GROUP
                    qc, j, q0 = COLUMNS[u]
                    width = 512 * (qc + 1) - q0
                    act.wait_ge(st_ready, here + s + 1)
                    if h == 0 and not (first and u < 2):
                        act.wait_ge(pv_done, UNITS * g + u - 1)
                    nc.scalar.activation(prob[:, h, u % 2, 0:width], ps_st[s % 2][:, 0:width], ACT.Exp, scale=scale).then_inc(p_ready, 1)
                    if s == TAKE_LAST and not first:
                        take_output(g - 1, 1, False)
                    if s == TAKE_FIRST:
                        take_output(g, 0, first)

            over_groups(act, body)
            take_output(groups - 1, 1, False)

        @block.tensor
        def _(pe):
            def row_scores(before, k, slot, loads, first):
                u = k % UNITS
                qt, k0, width = ROWS[u]
                if u == 0:
                    pe.wait_ge(loaded[slot], LOADS * loads)
                if not (first and k < 3):
                    pe.wait_ge(s_reduced, before + k - 2)
                on_diagonal = k0 * P + width == (qt + 1) * P
                ins = nc.tensor.matmul(ps_s[k % 3][:, 0:width], stack[0][slot][0:96, qt * P:(qt + 1) * P],
                                       stack[1][slot][0:96, k0 * P:k0 * P + width], start=True, stop=not on_diagonal)
                if on_diagonal:
                    ins = nc.tensor.matmul(ps_s[k % 3][:, width - P:width], ident_b, mask_rows, start=False, stop=True)
                ins.then_inc(s_ready, 1)

            def column_scores(before, s, par, own, first):
                h, u = s % GROUP, s // GROUP
                slot = GROUP * par + h
                qc, j, q0 = COLUMNS[u]
                width = 512 * (qc + 1) - q0
                if u == 0:
                    pe.wait_ge(mrow_in[slot], 32 * (own + 1))
                if not (first and s < 2):
                    pe.wait_ge(p_ready, before + s - 1)
                ins = nc.tensor.matmul(ps_st[s % 2][:, 0:width], stack[1][slot][:, j * P:(j + 1) * P], stack[0][slot][:, q0:q0 + width],
                                       start=True, stop=j < 4 * qc)
                if j >= 4 * qc:
                    ins = nc.tensor.matmul(ps_st[s % 2][:, 0:P], ident_b, mask_cols, start=False, stop=True)
                ins.then_inc(st_ready, 1)

            def value_products(g, u, par):
                qc, j, q0 = COLUMNS[u]
                width = 512 * (qc + 1) - q0
                pe.wait_ge(p_ready, STEPS * g + GROUP * (u + 1))
                for h in range(GROUP):
                    last = nc.tensor.matmul(ps_o[qc][32 * h:32 * h + 32, 512 - width:512], vh[:, GROUP * par + h, j, :], prob[:, h, u % 2, 0:width],
                                            start=(j == 0), stop=(j == 4 * qc + 3))
                last.then_inc(pv_done, 1)

            def turn_maxima(m, parity):
                pe.wait_ge(split_ready, m + 1)
                nc.tensor.transpose(ps_m[0:2 * KB, 0:P], split[:, parity].rearrange("p s q -> p (s q)").bitcast(F32), ident).then_inc(mT_ready, 1)

            def turn_output(g, qc):
                pe.wait_ge(oT_ready, 2 * g + qc + 1)
                for q in range(4):
                    last = nc.tensor.transpose(ps_m[:, q * P:(q + 1) * P], oT[:, qc, q * P:(q + 1) * P], ident)
                last.then_inc(o_turned, 1)

            def body(g, par, own, nxt, nxt_own, first, last):
                ahead, here = held(pe, STEPS * (g + 1)), held(pe, STEPS * g)
                for s in range(STEPS):
                    if not last:
                        for k in MAXIMA_AT[s]:
                            row_scores(ahead, k, GROUP * nxt + k // UNITS, nxt_own + 1, False)
                    column_scores(here, s, par, own, first)
                    if s == LAG - 1 and not first:
                        value_products(g - 1, UNITS - 1, (par + 2) % SETS)
                    u, r = divmod(s - LAG - (GROUP - 1), GROUP)
                    if u >= 0 and r == 0:
                        if u == 0:
                            pe.wait_ge(v_in[par], 16 * GROUP * (own + 1))
                        if u % 4 == 0 and u < 8 and not first:
                            pe.wait_ge(oT_ready, 2 * g - 1 + u // 4)
                        value_products(g, u, par)
                    if s == TURN_LAST and not first:
                        pe.wait_ge(mrow_ready, GROUP * (g + 1))
                        turn_output(g - 1, 1)
                    if s == TURN_FIRST:
                        if last:
                            pe.wait_ge(o_ready, 2 * g)
                        else:
                            pe.wait_ge(mrow_ready, GROUP * (g + 1) + 1)
                        turn_output(g, 0)
                    if s in TURN_AT and not last:
                        h = TURN_AT.index(s)
                        if h == 0 and first:
                            pe.wait_ge(mrow_ready, GROUP)
                        elif h < 2:
                            pe.wait_ge(o_ready, 2 * g + h)
                        else:
                            pe.wait_ge(mrow_ready, GROUP * (g + 1) + h)
                        turn_maxima(GROUP * (g + 1) + h, h % 2)

            for k in range(STEPS):
                row_scores(0, k, k // UNITS, 1, True)
                if k % UNITS == 2 and k > UNITS:
                    if k // UNITS > 1:
                        pe.wait_ge(mrow_ready, k // UNITS - 1)
                    turn_maxima(k // UNITS - 1, (k // UNITS - 1) % 2)
            pe.wait_ge(mrow_ready, GROUP - 1)
            turn_maxima(GROUP - 1, 1)
            over_groups(pe, body)
            value_products(groups - 1, UNITS - 1, (groups - 1) % SETS)
            pe.wait_ge(o_ready, 2 * groups - 1)
            turn_output(groups - 1, 1)
    nc.disable_value_cache = False


def build(nc, a, outs):
    internal = lambda name, shape, dt=F32: nc.dram_tensor(name, shape, dt, kind="Internal").ap()
    qk = [[internal(f"{w}_{hl}", [NH, 2 * HD, T]) for hl in ("high", "low")] for w in "qk"]
    vs = internal("v_rows", [NH, P, KB * 2 * HD])
    os = internal("attended", [NH // 4 * 2, P, 4, 4 * HD])
    x1, n1, h = (internal(n, [B, T, C]) for n in ("x1", "n1", "h_rows"))
    xs, ys = (internal(n, [TILES * P, C]) for n in ("sorted_rows", "expert_rows"))
    sems = []
    with ExitStack() as whole:
        t = outer = Tools(nc, whole, sems)
        cst = {"block": t.sbuf("constants", [P, WIDTH["block"]])}
        masks = t.sbuf("masks", [P, 3, P], BF16)
        wout = t.sbuf("w_out1", [P, 2, C])
        cout = t.sbuf("bias_out1", [P, C])
        masked = t.sem("masked")
        with nc.Block() as block:
            @block.gpsimd
            def _(pool):
                nc.gpsimd.memset(masks[:, 0], 0.0).then_inc(masked, 1)
                nc.gpsimd.memset(masks[:, 1:3], 0.0).then_inc(masked, 1)
                pool.wait_ge(masked, 2)
                nc.gpsimd.affine_select(out=masks[:, 0], in_=masks[:, 0], compare_op=ALU.not_equal, fill=1.0, base=0,
                                        pattern=[[-1, P]], channel_multiplier=1)
                nc.gpsimd.affine_select(out=masks[:, 1], in_=masks[:, 1], compare_op=ALU.is_ge, fill=MASKED, base=0,
                                        pattern=[[-1, P]], channel_multiplier=1)
                nc.gpsimd.affine_select(out=masks[:, 2], in_=masks[:, 2], compare_op=ALU.is_ge, fill=MASKED, base=0,
                                        pattern=[[1, P]], channel_multiplier=-1)
        with ExitStack() as ctx:
            t = Tools(nc, ctx, sems)
            cst["latent"] = t.sbuf("latent_constants", [P, WIDTH["latent"]])
            rope = t.sbuf("rope", [P, 2, T])
            wlat = t.sbuf("w_latent", [P, CC, 2, 2, 2, P])
            blat = t.sbuf("b_latent", [P, 2, 2, 2])
            with ExitStack() as inner:
                compose_weights(nc, Tools(nc, inner, sems), {which: a[which] for which in PACKS}, cst, a["rope"], rope, wlat, blat, wout, cout)
            with ExitStack() as inner:
                latent_projections(nc, Tools(nc, inner, sems), a["x"], cst, rope, wlat, blat, qk, vs)
        with ExitStack() as ctx:
            attention(nc, Tools(nc, ctx, sems), "a1", cst, masks, qk, vs, 2 * HD, float(L) ** -0.5, os)
        renew_semaphores(nc, sems)
        with ExitStack() as ctx:
            between_attentions(nc, Tools(nc, ctx, sems), a["x"], os, cst, wout, cout, x1, n1, qk, vs)
        with ExitStack() as ctx:
            attention(nc, Tools(nc, ctx, sems), "a2", cst, masks, qk, vs, HD, float(HD) ** -0.5, os, xs)
        renew_semaphores(nc, sems)
        logits = outer.sbuf("logits", [P, TT, E])
        weight = outer.sbuf("weight", [P, TT, 2])
        place = outer.sbuf("place", [P, 2, TT], U32)
        tile_expert = outer.sbuf("tile_expert", [P, TILES // 2, 4], mybir.dt.int32)
        with ExitStack() as ctx:
            after_attentions(nc, Tools(nc, ctx, sems), n1, os, cst, h, logits)
        with ExitStack() as ctx:
            route(nc, Tools(nc, ctx, sems), cst, logits, weight, place, tile_expert)
        with ExitStack() as ctx:
            e = Tools(nc, ctx, sems)
            w1s = [e.sbuf("w1_high", [P, E, CC, F], FP16), e.sbuf("w1_low", [P, E, CC, F], BF16)]
            w2s = [e.sbuf("w2_high", [P, E, F // P, C], FP16), e.sbuf("w2_low", [P, E, F // P, C], BF16)]
            bb = [e.sbuf("bb1", [P, E, F // P]), e.sbuf("bb2", [P, E, C])]
            with ExitStack() as inner:
                scatter_and_split(nc, Tools(nc, inner, sems), h, place, xs, a["w1"], a["w2"], w1s, w2s, [a["bb1"], a["bb2"]], bb)
            with ExitStack() as inner:
                experts(nc, Tools(nc, inner, sems), cst, xs, ys, tile_expert, bb, w1s, w2s)
        with ExitStack() as ctx:
            combine(nc, Tools(nc, ctx, sems), cst, weight, place, ys, h, x1, outs["out"])


def kernel(**inputs):
    import concourse.bacc as _bacc
    from concourse.bass_utils import run_bass_kernel_spmd as _run

    i = {k: np.asarray(v) for k, v in inputs.items()}
    arrays = {
        "x": np.ascontiguousarray(i["L0_attn_x"]),
        "latent": pack("latent", attention_constants(i)),
        "block": pack("block", block_constants(i)),
        "w1": np.ascontiguousarray(i["L0_ffn_w1"]),
        "w2": np.ascontiguousarray(i["L0_ffn_w2"]),
        "bb1": np.ascontiguousarray(i["L0_ffn_bb1"].reshape(E, F // P, P).transpose(2, 0, 1)),
        "bb2": np.tile(i["L0_ffn_bb2"], (P, 1, 1)),
        "rope": rope_tables(),
    }
    nc = _bacc.Bacc("TRN2", target_bir_lowering=False, num_devices=1)
    a = {n: nc.dram_tensor(n + "_dram", v.shape, mybir.dt.from_np(v.dtype), kind="ExternalInput").ap() for n, v in arrays.items()}
    out = nc.dram_tensor("out_dram", (B, T, C), F32, kind="ExternalOutput").ap()
    build(nc, a, {"out": out})
    r = _run(nc, [{n + "_dram": v for n, v in arrays.items()}], core_ids=[0])
    return r.results[0]["out_dram"]
```
